# Optimizing a Trainium2 kernel written in Bass

```python
import numpy as np
import jax
import jax.numpy as jnp

def _softmax(x, axis=-1):
    return jax.nn.softmax(x, axis=axis)

def _gelu(x):
    return jax.nn.gelu(x, approximate=True)

def _silu(x):
    return jax.nn.silu(x)

def _sigmoid(x):
    return jax.nn.sigmoid(x)

def _layernorm(x, axis=-1, eps=1e-05):
    m = jnp.mean(x, axis=axis, keepdims=True)
    v = jnp.var(x, axis=axis, keepdims=True)
    return (x - m) / jnp.sqrt(v + eps)

def _scatter_add(tgt, idx, src, axis=0):
    return tgt.at[idx].add(src)

def _segment_sum(src, seg, n):
    return jax.ops.segment_sum(src, seg, n)
kernel_name = 'mk_seq_postln_d2_jaxref_r8_84cb76'

def setup_inputs(seed: int=0):
    np.random.seed(seed)
    _w = jnp.asarray

    def _L0_attn_setup():
        import jax, jax.numpy as jnp
        import numpy as np
        import math
        DIM = 128
        HEADS = 16
        HEAD_DIM = DIM // HEADS
        key = jax.random.key(seed)
        ks = jax.random.split(key, 7)
        b, n = (2, 256)
        scale = 1.0 / math.sqrt(DIM)
        x = jax.random.normal(ks[0], (b, n, DIM), dtype=jnp.float32)
        Wq = jax.random.normal(ks[1], (DIM, DIM), dtype=jnp.float32) * scale
        Wk = jax.random.normal(ks[2], (DIM, DIM), dtype=jnp.float32) * scale
        Wv = jax.random.normal(ks[3], (DIM, DIM), dtype=jnp.float32) * scale
        Wo = jax.random.normal(ks[4], (DIM, DIM), dtype=jnp.float32) * scale
        bo = jnp.zeros((DIM,), dtype=jnp.float32)
        denom_bias = jnp.zeros((1, HEADS, 1, 1), dtype=jnp.float32)
        return {'x': x, 'Wq': Wq, 'Wk': Wk, 'Wv': Wv, 'Wo': Wo, 'bo': bo, 'denom_bias': denom_bias}
    _L0_attn_in = _L0_attn_setup()

    def _L0_ffn_setup():
        import jax, jax.numpy as jnp
        import numpy as np
        DIM = 128
        DEPTH = 6
        HEADS = 16
        DIM_HEAD = 64
        WINDOW = 32
        INNER = HEADS * DIM_HEAD
        DIM_INNER = int(DIM * 4 * 2 / 3)
        QK_SCALE = 8.0

        def shift_tokens(t):
            a, s = jnp.split(t, 2, -1)
            s = jnp.pad(s, ((0, 0), (1, 0), (0, 0)))[:, :-1]
            return jnp.concatenate([a, s], -1)

        def l2norm(t):
            return t / jnp.maximum(jnp.linalg.norm(t, axis=-1, keepdims=True), 1e-12)

        def rotate_half(x):
            x1, x2 = jnp.split(x, 2, -1)
            return jnp.concatenate([-x2, x1], -1)

        def rotary_tables(n):
            half = jnp.arange(0, DIM_HEAD, 2, dtype=jnp.float32)
            inv_freq = 1.0 / 10000.0 ** (half / DIM_HEAD)
            t = jnp.arange(n, dtype=jnp.float32)
            freqs = t[:, None] * inv_freq[None, :]
            freqs = jnp.concatenate([freqs, freqs], -1)
            base_scale = (half + 0.4 * DIM_HEAD) / (1.4 * DIM_HEAD)
            power = (t - n // 2) / (WINDOW // 2)
            scale = base_scale[None, :] ** power[:, None]
            scale = jnp.concatenate([scale, scale], -1)
            return (freqs, scale)

        def local_attention(q, k, v):
            b, h, n, d = q.shape
            w = WINDOW
            nw = n // w
            bq = q.reshape(b, h, nw, w, d)
            bk = k.reshape(b, h, nw, w, d)
            bv = v.reshape(b, h, nw, w, d)

            def look(t):
                p = jnp.pad(t, ((0, 0), (0, 0), (1, 0), (0, 0), (0, 0)))
                return jnp.concatenate([p[:, :, :nw], p[:, :, 1:]], axis=3)
            bk2, bv2 = (look(bk), look(bv))
            seq = jnp.arange(n).reshape(nw, w)
            seq_p = jnp.pad(seq, ((1, 0), (0, 0)), constant_values=-1)
            jt = jnp.concatenate([seq_p[:nw], seq_p[1:]], axis=1)
            it = seq[:, :, None]
            jb = jt[:, None, :]
            mask = (it < jb) | (it > jb + w) | (jb == -1)
            sim = jnp.einsum('bhwie,bhwje->bhwij', bq, bk2) * QK_SCALE
            sim = jnp.where(mask, -jnp.finfo(sim.dtype).max, sim)
            attn = jax.nn.softmax(sim, -1)
            out = jnp.einsum('bhwij,bhwje->bhwie', attn, bv2)
            return out.reshape(b, h, n, d)

        def attn_layer(x, Wqkv, qs, ksc, Wo):
            b, n, _ = x.shape
            qkv = x @ Wqkv
            q, k, v = jnp.split(qkv, 3, -1)
            sh = lambda t: t.reshape(b, n, HEADS, DIM_HEAD).transpose(0, 2, 1, 3)
            q, k, v = (sh(q), sh(k), sh(v))
            q = l2norm(q) * qs
            k = l2norm(k) * ksc
            freqs, scale = rotary_tables(n)
            cos, sin = (jnp.cos(freqs), jnp.sin(freqs))
            q = q * cos * scale + rotate_half(q) * sin * scale
            inv = 1.0 / scale
            k = k * cos * inv + rotate_half(k) * sin * inv
            out = local_attention(q, k, v)
            out = out.transpose(0, 2, 1, 3).reshape(b, n, INNER)
            return out @ Wo

        def ffn_layer(x, g, bln, W1, b1, W2, b2):
            mu = x.mean(-1, keepdims=True)
            var = ((x - mu) ** 2).mean(-1, keepdims=True)
            xn = (x - mu) / jnp.sqrt(var + 1e-05) * g + bln
            hg = xn @ W1 + b1
            a, gate = jnp.split(hg, 2, -1)
            return a * jax.nn.gelu(gate, approximate=False) @ W2 + b2
        key = jax.random.key(seed)
        ks = jax.random.split(key, 8)
        B, N = (2, 256)
        init = lambda k, shape: jax.random.normal(k, shape, jnp.float32) * 0.02
        return {'x': jax.random.normal(ks[0], (B, N, DIM), jnp.float32), 'Wqkv': init(ks[1], (DEPTH, DIM, 3 * INNER)), 'q_scale': jnp.ones((DEPTH, DIM_HEAD), jnp.float32), 'k_scale': jnp.ones((DEPTH, DIM_HEAD), jnp.float32), 'Wo': init(ks[2], (DEPTH, INNER, DIM)), 'ln_g': jnp.ones((DEPTH, DIM), jnp.float32), 'ln_b': jnp.zeros((DEPTH, DIM), jnp.float32), 'W1': init(ks[3], (DEPTH, DIM, 2 * DIM_INNER)), 'b1': jnp.zeros((DEPTH, 2 * DIM_INNER), jnp.float32), 'W2': init(ks[4], (DEPTH, DIM_INNER, DIM)), 'b2': jnp.zeros((DEPTH, DIM), jnp.float32)}
    _L0_ffn_in = _L0_ffn_setup()

    def _L1_attn_setup():
        import jax, jax.numpy as jnp
        import numpy as np
        from jax import lax
        B, L, D, N, DT_RANK = (2, 256, 128, 16, 64)

        def _assoc_op(left, right):
            a_l, b_l = left
            a_r, b_r = right
            return (a_r * a_l, a_r * b_l + b_r)
        key = jax.random.key(seed)
        ks = jax.random.split(key, 6)
        x = jax.random.normal(ks[0], (B, L, D), dtype=jnp.float32)
        A_log = jnp.log(jnp.broadcast_to(jnp.arange(1, N + 1, dtype=jnp.float32), (D, N)))
        D_param = jnp.ones((D,), dtype=jnp.float32)
        W_bc = jax.random.normal(ks[1], (D, 2 * N), dtype=jnp.float32) / np.sqrt(D)
        W_dt = jax.random.normal(ks[2], (D, DT_RANK), dtype=jnp.float32) / np.sqrt(D)
        W_dtproj = jax.random.normal(ks[3], (DT_RANK, D), dtype=jnp.float32) / np.sqrt(DT_RANK)
        dt = jax.random.uniform(ks[4], (D,), minval=0.001, maxval=0.1, dtype=jnp.float32)
        b_dtproj = dt + jnp.log(-jnp.expm1(-dt))
        return {'x': x, 'A_log': A_log, 'D_param': D_param, 'W_bc': W_bc, 'W_dt': W_dt, 'W_dtproj': W_dtproj, 'b_dtproj': b_dtproj}
    _L1_attn_in = _L1_attn_setup()

    def _L1_ffn_setup():
        import jax, jax.numpy as jnp
        import numpy as np
        B, L, D = (1, 256, 128)
        E, H, G, K = (64, 32, 64, 16)

        def _grouped_routing_scores(router_scores):
            T, En = router_scores.shape
            Tq = T // G
            budget = Tq * K
            order = jnp.argsort(-router_scores, axis=0)
            sorted_vals = jnp.take_along_axis(router_scores, order, axis=0)
            group_score = sorted_vals.reshape(Tq, G, En).sum(axis=1)
            _, top_flat = jax.lax.top_k(group_score.reshape(-1), budget)
            gmask = jnp.zeros((Tq * En,), bool).at[top_flat].set(True).reshape(Tq, En)
            mask_sorted = jnp.broadcast_to(gmask[:, None, :], (Tq, G, En)).reshape(T, En)
            mask = jnp.zeros((T, En), bool).at[order, jnp.arange(En)[None, :]].set(mask_sorted)
            fs = jnp.where(mask, router_scores, 0.0)
            return fs / (fs.sum(axis=-1, keepdims=True) + 1e-06)
        key = jax.random.key(seed)
        ks = jax.random.split(key, 6)
        s = lambda k, shape, scale: jax.random.normal(k, shape, jnp.float32) * scale
        return {'x': jax.random.normal(ks[0], (B, L, D), jnp.float32), 'Wr': s(ks[1], (D, E), D ** (-0.5)), 'br': jnp.zeros((E,), jnp.float32), 'Wup': s(ks[2], (E, D, H), D ** (-0.5)), 'bup': jnp.zeros((E, H), jnp.float32), 'Wgate': s(ks[3], (E, D, H), D ** (-0.5)), 'bgate': jnp.zeros((E, H), jnp.float32), 'Wdown': s(ks[4], (E, H, D), H ** (-0.5)), 'bdown': jnp.zeros((E, D), jnp.float32)}
    _L1_ffn_in = _L1_ffn_setup()
    _d = {'L0_attn_x': _L0_attn_in['x'], 'L0_attn_Wq': _L0_attn_in['Wq'], 'L0_attn_Wk': _L0_attn_in['Wk'], 'L0_attn_Wv': _L0_attn_in['Wv'], 'L0_attn_Wo': _L0_attn_in['Wo'], 'L0_attn_bo': _L0_attn_in['bo'], 'L0_attn_denom_bias': _L0_attn_in['denom_bias'], 'L0_ffn_Wqkv': _L0_ffn_in['Wqkv'], 'L0_ffn_q_scale': _L0_ffn_in['q_scale'], 'L0_ffn_k_scale': _L0_ffn_in['k_scale'], 'L0_ffn_Wo': _L0_ffn_in['Wo'], 'L0_ffn_ln_g': _L0_ffn_in['ln_g'], 'L0_ffn_ln_b': _L0_ffn_in['ln_b'], 'L0_ffn_W1': _L0_ffn_in['W1'], 'L0_ffn_b1': _L0_ffn_in['b1'], 'L0_ffn_W2': _L0_ffn_in['W2'], 'L0_ffn_b2': _L0_ffn_in['b2'], 'L1_attn_A_log': _L1_attn_in['A_log'], 'L1_attn_D_param': _L1_attn_in['D_param'], 'L1_attn_W_bc': _L1_attn_in['W_bc'], 'L1_attn_W_dt': _L1_attn_in['W_dt'], 'L1_attn_W_dtproj': _L1_attn_in['W_dtproj'], 'L1_attn_b_dtproj': _L1_attn_in['b_dtproj'], 'L1_ffn_Wr': _L1_ffn_in['Wr'], 'L1_ffn_br': _L1_ffn_in['br'], 'L1_ffn_Wup': _L1_ffn_in['Wup'], 'L1_ffn_bup': _L1_ffn_in['bup'], 'L1_ffn_Wgate': _L1_ffn_in['Wgate'], 'L1_ffn_bgate': _L1_ffn_in['bgate'], 'L1_ffn_Wdown': _L1_ffn_in['Wdown'], 'L1_ffn_bdown': _L1_ffn_in['bdown']}
    _x0 = _d['L0_attn_x']
    _d['L0_attn_x'] = jax.random.normal(jax.random.fold_in(jax.random.key(seed), 1), (1, 2048, 128), dtype=_x0.dtype)
    del _x0
    return _d

def reference(L0_attn_x, L0_attn_Wq, L0_attn_Wk, L0_attn_Wv, L0_attn_Wo, L0_attn_bo, L0_attn_denom_bias, L0_ffn_Wqkv, L0_ffn_q_scale, L0_ffn_k_scale, L0_ffn_Wo, L0_ffn_ln_g, L0_ffn_ln_b, L0_ffn_W1, L0_ffn_b1, L0_ffn_W2, L0_ffn_b2, L1_attn_A_log, L1_attn_D_param, L1_attn_W_bc, L1_attn_W_dt, L1_attn_W_dtproj, L1_attn_b_dtproj, L1_ffn_Wr, L1_ffn_br, L1_ffn_Wup, L1_ffn_bup, L1_ffn_Wgate, L1_ffn_bgate, L1_ffn_Wdown, L1_ffn_bdown):

    def _L0_attn_ref(x, Wq, Wk, Wv, Wo, bo, denom_bias):
        import jax, jax.numpy as jnp
        import numpy as np
        import math
        DIM = 128
        HEADS = 16
        HEAD_DIM = DIM // HEADS
        b, n, d = x.shape
        h, hd = (HEADS, HEAD_DIM)

        def split_heads(t):
            return t.reshape(b, n, h, hd).transpose(0, 2, 1, 3)
        q = split_heads(x @ Wq.T)
        k = split_heads(x @ Wk.T)
        v = split_heads(x @ Wv.T)
        sim = jnp.einsum('bhid,bhjd->bhij', q, k) / math.sqrt(hd)
        causal_mask = jnp.triu(jnp.ones((n, n), dtype=bool), k=1)
        neg = -jnp.finfo(sim.dtype).max
        sim = jnp.where(causal_mask, neg, sim)
        sim_max = jnp.max(sim, axis=-1, keepdims=True)
        exp_sim = jnp.exp(sim - sim_max)
        denom = jnp.sum(exp_sim, axis=-1, keepdims=True) + jnp.exp(denom_bias)
        attn = exp_sim / denom
        out = jnp.einsum('bhij,bhjd->bhid', attn, v)
        out = out.transpose(0, 2, 1, 3).reshape(b, n, d)
        return out @ Wo.T + bo

    def _L0_ffn_ref(x, Wqkv, q_scale, k_scale, Wo, ln_g, ln_b, W1, b1, W2, b2):
        import jax, jax.numpy as jnp
        import numpy as np
        DIM = 128
        DEPTH = 6
        HEADS = 16
        DIM_HEAD = 64
        WINDOW = 32
        INNER = HEADS * DIM_HEAD
        DIM_INNER = int(DIM * 4 * 2 / 3)
        QK_SCALE = 8.0

        def shift_tokens(t):
            a, s = jnp.split(t, 2, -1)
            s = jnp.pad(s, ((0, 0), (1, 0), (0, 0)))[:, :-1]
            return jnp.concatenate([a, s], -1)

        def l2norm(t):
            return t / jnp.maximum(jnp.linalg.norm(t, axis=-1, keepdims=True), 1e-12)

        def rotate_half(x):
            x1, x2 = jnp.split(x, 2, -1)
            return jnp.concatenate([-x2, x1], -1)

        def rotary_tables(n):
            half = jnp.arange(0, DIM_HEAD, 2, dtype=jnp.float32)
            inv_freq = 1.0 / 10000.0 ** (half / DIM_HEAD)
            t = jnp.arange(n, dtype=jnp.float32)
            freqs = t[:, None] * inv_freq[None, :]
            freqs = jnp.concatenate([freqs, freqs], -1)
            base_scale = (half + 0.4 * DIM_HEAD) / (1.4 * DIM_HEAD)
            power = (t - n // 2) / (WINDOW // 2)
            scale = base_scale[None, :] ** power[:, None]
            scale = jnp.concatenate([scale, scale], -1)
            return (freqs, scale)

        def local_attention(q, k, v):
            b, h, n, d = q.shape
            w = WINDOW
            nw = n // w
            bq = q.reshape(b, h, nw, w, d)
            bk = k.reshape(b, h, nw, w, d)
            bv = v.reshape(b, h, nw, w, d)

            def look(t):
                p = jnp.pad(t, ((0, 0), (0, 0), (1, 0), (0, 0), (0, 0)))
                return jnp.concatenate([p[:, :, :nw], p[:, :, 1:]], axis=3)
            bk2, bv2 = (look(bk), look(bv))
            seq = jnp.arange(n).reshape(nw, w)
            seq_p = jnp.pad(seq, ((1, 0), (0, 0)), constant_values=-1)
            jt = jnp.concatenate([seq_p[:nw], seq_p[1:]], axis=1)
            it = seq[:, :, None]
            jb = jt[:, None, :]
            mask = (it < jb) | (it > jb + w) | (jb == -1)
            sim = jnp.einsum('bhwie,bhwje->bhwij', bq, bk2) * QK_SCALE
            sim = jnp.where(mask, -jnp.finfo(sim.dtype).max, sim)
            attn = jax.nn.softmax(sim, -1)
            out = jnp.einsum('bhwij,bhwje->bhwie', attn, bv2)
            return out.reshape(b, h, n, d)

        def attn_layer(x, Wqkv, qs, ksc, Wo):
            b, n, _ = x.shape
            qkv = x @ Wqkv
            q, k, v = jnp.split(qkv, 3, -1)
            sh = lambda t: t.reshape(b, n, HEADS, DIM_HEAD).transpose(0, 2, 1, 3)
            q, k, v = (sh(q), sh(k), sh(v))
            q = l2norm(q) * qs
            k = l2norm(k) * ksc
            freqs, scale = rotary_tables(n)
            cos, sin = (jnp.cos(freqs), jnp.sin(freqs))
            q = q * cos * scale + rotate_half(q) * sin * scale
            inv = 1.0 / scale
            k = k * cos * inv + rotate_half(k) * sin * inv
            out = local_attention(q, k, v)
            out = out.transpose(0, 2, 1, 3).reshape(b, n, INNER)
            return out @ Wo

        def ffn_layer(x, g, bln, W1, b1, W2, b2):
            mu = x.mean(-1, keepdims=True)
            var = ((x - mu) ** 2).mean(-1, keepdims=True)
            xn = (x - mu) / jnp.sqrt(var + 1e-05) * g + bln
            hg = xn @ W1 + b1
            a, gate = jnp.split(hg, 2, -1)
            return a * jax.nn.gelu(gate, approximate=False) @ W2 + b2
        for i in range(DEPTH):
            x = attn_layer(shift_tokens(x), Wqkv[i], q_scale[i], k_scale[i], Wo[i]) + x
            x = ffn_layer(shift_tokens(x), ln_g[i], ln_b[i], W1[i], b1[i], W2[i], b2[i]) + x
        return x

    def _L1_attn_ref(x, A_log, D_param, W_bc, W_dt, W_dtproj, b_dtproj):
        import jax, jax.numpy as jnp
        import numpy as np
        from jax import lax
        B, L, D, N, DT_RANK = (2, 256, 128, 16, 64)

        def _assoc_op(left, right):
            a_l, b_l = left
            a_r, b_r = right
            return (a_r * a_l, a_r * b_l + b_r)
        x_bc = jnp.einsum('bld,dn->bln', x, W_bc)
        n = A_log.shape[1]
        B_sel = x_bc[..., :n]
        C_sel = x_bc[..., n:]
        dt_low = jnp.einsum('bld,dr->blr', x, W_dt)
        delta = jax.nn.softplus(jnp.einsum('blr,rd->bld', dt_low, W_dtproj) + b_dtproj)
        A = -jnp.exp(A_log)
        A_bar = jnp.exp(delta[..., None] * A)
        Bx = (delta * x)[..., None] * B_sel[:, :, None, :]
        _, all_h = lax.associative_scan(_assoc_op, (A_bar, Bx), axis=1)
        y = jnp.sum(C_sel[:, :, None, :] * all_h, axis=-1)
        return y + D_param * x

    def _L1_ffn_ref(x, Wr, br, Wup, bup, Wgate, bgate, Wdown, bdown):
        import jax, jax.numpy as jnp
        import numpy as np
        B, L, D = (1, 256, 128)
        E, H, G, K = (64, 32, 64, 16)

        def _grouped_routing_scores(router_scores):
            T, En = router_scores.shape
            Tq = T // G
            budget = Tq * K
            order = jnp.argsort(-router_scores, axis=0)
            sorted_vals = jnp.take_along_axis(router_scores, order, axis=0)
            group_score = sorted_vals.reshape(Tq, G, En).sum(axis=1)
            _, top_flat = jax.lax.top_k(group_score.reshape(-1), budget)
            gmask = jnp.zeros((Tq * En,), bool).at[top_flat].set(True).reshape(Tq, En)
            mask_sorted = jnp.broadcast_to(gmask[:, None, :], (Tq, G, En)).reshape(T, En)
            mask = jnp.zeros((T, En), bool).at[order, jnp.arange(En)[None, :]].set(mask_sorted)
            fs = jnp.where(mask, router_scores, 0.0)
            return fs / (fs.sum(axis=-1, keepdims=True) + 1e-06)
        Bx, Lx, Dx = x.shape
        xt = x.reshape(-1, Dx)
        router_scores = jax.nn.softmax(xt @ Wr + br, axis=-1)
        fs = _grouped_routing_scores(router_scores)
        up = jnp.einsum('td,edh->teh', xt, Wup) + bup
        gate = jnp.einsum('td,edh->teh', xt, Wgate) + bgate
        h = jax.nn.silu(up) * gate * fs[:, :, None]
        out = jnp.einsum('teh,ehd->td', h, Wdown) + fs @ bdown
        return out.reshape(Bx, Lx, Dx)
    x = L0_attn_x
    x = _layernorm(x + _L0_attn_ref(x, L0_attn_Wq, L0_attn_Wk, L0_attn_Wv, L0_attn_Wo, L0_attn_bo, L0_attn_denom_bias), axis=-1)
    x = _layernorm(x + _L0_ffn_ref(x, L0_ffn_Wqkv, L0_ffn_q_scale, L0_ffn_k_scale, L0_ffn_Wo, L0_ffn_ln_g, L0_ffn_ln_b, L0_ffn_W1, L0_ffn_b1, L0_ffn_W2, L0_ffn_b2), axis=-1)
    x = _layernorm(x + _L1_attn_ref(x, L1_attn_A_log, L1_attn_D_param, L1_attn_W_bc, L1_attn_W_dt, L1_attn_W_dtproj, L1_attn_b_dtproj), axis=-1)
    x = _layernorm(x + _L1_ffn_ref(x, L1_ffn_Wr, L1_ffn_br, L1_ffn_Wup, L1_ffn_bup, L1_ffn_Wgate, L1_ffn_bgate, L1_ffn_Wdown, L1_ffn_bdown), axis=-1)
    return x

_drawn_inputs = setup_inputs


def setup_inputs(seed=0):
    import zlib

    import numpy as np

    out = dict(_drawn_inputs(seed))
    spreads = {'L0_attn_bo': (0.0, 0.1),
     'L0_attn_denom_bias': (0.0, 2.0),
     'L0_ffn_q_scale': (1.0, 0.6),
     'L0_ffn_k_scale': (1.0, 0.6),
     'L0_ffn_ln_g': (1.0, 0.6),
     'L0_ffn_ln_b': (0.0, 0.8),
     'L0_ffn_b1': (0.0, 0.613),
     'L0_ffn_b2': (0.0, 0.1),
     'L1_attn_D_param': (1.0, 0.2),
     'L1_ffn_br': (0.0, 0.286),
     'L1_ffn_bup': (0.0, 0.451),
     'L1_ffn_bgate': (0.0, 0.448),
     'L1_ffn_bdown': (0.0, 0.274)}
    factors = {'L0_ffn_W1': 2.81, 'L0_ffn_W2': 2.76}
    for name, (base, spread) in spreads.items():
        noise = np.random.default_rng([zlib.crc32(name.encode()), seed]).standard_normal(out[name].shape)
        drawn = base * np.exp(spread * noise) if base else spread * noise
        out[name] = jnp.asarray(drawn.astype(out[name].dtype))
    for name, factor in factors.items():
        out[name] = (out[name] * factor).astype(out[name].dtype)
    return out
```

```python
import numpy as np
from contextlib import ExitStack
import concourse.bass as bass
from concourse import mybir

F32 = mybir.dt.float32
BF16 = mybir.dt.bfloat16
ALU = mybir.AluOpType
ACT = mybir.ActivationFunctionType
AX_X = mybir.AxisListType.X
ds = bass.ds

P = 128
SEQ = 2048
DIM = 128
TILES = SEQ // P
CH = 512
CHUNKS = SEQ // CH
EPS = 1e-5
BIG = 1e30


def semaphores(nc, ctx):
    given = []

    def give(name):
        given.append(nc.alloc_semaphore(name=name))
        return given[-1]

    def clear():
        nc.clear_and_free_semaphores(given)
        nc.all_engine_barrier()

    ctx.callback(clear)
    return give


def causal_attention(nc, xT, att, w, const):
    HEADS, HD = 16, 8
    GROUPS = 4
    GH = HEADS // GROUPS
    SLOT = 32
    Q_PARTS = (0, 0, 1, 0, 1, 2)
    K_PARTS = (0, 1, 0, 2, 1, 0)
    SPLIT_ROWS = HD * len(Q_PARTS)
    outer = ExitStack()
    with outer:
        def sbo(name, shape, dt=F32):
            return outer.enter_context(nc.sbuf_tensor("a_" + name, shape, dt))
        qa = sbo("qa", [P, HEADS, SEQ], BF16)
        ka = sbo("ka", [P, HEADS, SEQ], BF16)
        v_all = sbo("v_all", [P, TILES, DIM])
        wo_pad = sbo("wo_pad", [P, GROUPS, DIM])
        ident = sbo("ident", [P, P])
        identb = sbo("identb", [P, P], BF16)
        tri = sbo("tri", [P, 2, P], BF16)
        denb = sbo("denb", [P, P])
        eb = sbo("eb", [P, GROUPS])
        loaded = [outer.enter_context(nc.semaphore(f"a_group_loaded{g}")) for g in range(GROUPS)]

        ctx = ExitStack()
        with ctx:
            def sb(name, shape, dt=F32):
                return ctx.enter_context(nc.sbuf_tensor("a0_" + name, shape, dt))
            xtok = sb("xtok", [P, 4, DIM])
            wraw = sb("wraw", [P, 4, DIM])
            wT = sb("wT", [P, 4, DIM])
            sel = sb("sel", [P, GROUPS, P])
            tri_in = sb("tri_in", [P, 2, P])
            bo = sb("bo", [P, 1])
            part = sb("part", [P, 2, 3, SEQ // 2], BF16)
            rest = sb("rest", [P, 2, CH])
            ps = [ctx.enter_context(nc.psum_tensor(f"a0_ps{i}", [P, 4, P], F32)) for i in range(4)]
            scratch = nc.dram_tensor("a0_parts", [2, 3, DIM, SEQ], BF16).ap()
            sem = lambda n: ctx.enter_context(nc.semaphore("a0_" + n))
            s_in, s_x, s_zero, s_pe, s_act, s_dve, s_part, s_store, s_xfree = (
                sem(n) for n in ("in", "x", "zero", "pe", "act", "dve", "part", "store", "xfree"))
            block = ctx.enter_context(nc.Block())

            @block.sync
            def _(sp):
                for j, n in enumerate(("Wq", "Wk", "Wv", "Wo")):
                    sp.dma_start(wraw[:, j, :], w[n]).then_inc(s_in, 16)
                sp.dma_start(ident[:, :], const["ident"]).then_inc(s_in, 16)
                sp.dma_start(sel[:, :, :], const["sel"]).then_inc(s_in, 16)
                sp.dma_start(tri_in[:, :, :], const["tri"]).then_inc(s_in, 16)
                sp.dma_start(denb[:, :], const["denb"]).then_inc(s_in, 16)
                sp.dma_start(bo[:, :], w["bo"].rearrange("(p o) -> p o", o=1)).then_inc(s_in, 16)
                for j in range(GH):
                    sp.dma_start(eb[SLOT * j:SLOT * (j + 1), :],
                                 w["denom_bias"].rearrange("o (g j) a b -> (o a b) j g", j=GH)[:, j, :].broadcast_to([SLOT, GROUPS]),
                                 allow_slow_non_contiguous=True).then_inc(s_in, 16)
                for c in range(4):
                    if c:
                        sp.wait_ge(s_xfree, c)
                    sp.dma_start(xtok[:, :, :], w["x"][0, c * CH:(c + 1) * CH, :].rearrange("(t p) d -> p t d", p=P)
                                 ).then_inc(s_x, 16)
                for half in range(2):
                    for s in range(2):
                        sp.wait_ge(s_part, 4 * half + 2 * s + 2)
                        sp.dma_start(scratch[s, :, :, half * 1024:(half + 1) * 1024].rearrange("k p n -> p k n"),
                                     part[:, s, :, :]).then_inc(s_store, 16)
                sp.wait_ge(s_store, 64)
                for g in range(GROUPS):
                    for s, (dst, parts) in enumerate(((qa, Q_PARTS), (ka, K_PARTS))):
                        for r, k in enumerate(parts):
                            sp.dma_start(dst[HD * r:HD * (r + 1), GH * g:GH * (g + 1), :],
                                         scratch[s, k, GH * HD * g:GH * HD * (g + 1), :].rearrange("(h r) n -> r h n", r=HD)
                                         ).then_inc(loaded[g], 16)

            @block.gpsimd
            def _(pool):
                nc.gpsimd.memset(qa[:, :, :], 0.0).then_inc(s_zero, 1)
                nc.gpsimd.memset(xT[:, 0:1], 0.0).then_inc(s_zero, 1)

            @block.scalar
            def _(act):
                act.wait_ge(s_in, 13 * 16)
                nc.scalar.activation(eb[:, :], eb[:, :], ACT.Exp).then_inc(s_act, 1)
                for c in range(4):
                    act.wait_ge(s_pe, c + 1)
                    nc.scalar.copy(xT[:, 1 + c * CH:1 + (c + 1) * CH], ps[c][:, :, :].rearrange("p t d -> p (t d)")).then_inc(s_act, 1)
                act.wait_ge(s_pe, 5)
                nc.scalar.copy(wT[:, :, :], ps[0][:, :, :]).then_inc(s_act, 1)
                act.wait_ge(s_pe, 6)
                nc.scalar.copy(wo_pad[:, :, :], ps[1][:, :, :]).then_inc(s_act, 1)
                for c in range(4):
                    act.wait_ge(s_pe, 7 + c)
                    nc.scalar.copy(v_all[:, 4 * c:4 * c + 4, :], ps[c][:, :, :]).then_inc(s_act, 1)
                for n in range(8):
                    half, s, k = n // 4, (n // 2) % 2, n % 2
                    act.wait_ge(s_pe, 11 + n)
                    if half:
                        act.wait_ge(s_store, 32)
                    dst = part[:, s, :, k * CH:(k + 1) * CH]
                    nc.scalar.copy(dst[:, 0, :], ps[n % 4][:, :, :].rearrange("p t d -> p (t d)")).then_inc(s_act, 1)
                    act.wait_ge(s_dve, 2 * n + 2)
                    nc.scalar.copy(dst[:, 1, :], rest[:, n % 2, :]).then_inc(s_act, 1)

            @block.vector
            def _(dve):
                dve.wait_ge(s_zero, 2)
                nc.vector.memset(ka[:, :, :], -1.0).then_inc(s_zero, 1)
                dve.wait_ge(s_in, 13 * 16)
                nc.vector.tensor_copy(tri[:, :, :], tri_in[:, :, :])
                nc.vector.tensor_copy(identb[:, :], ident[:, :]).then_inc(s_dve, 1)
                for n in range(8):
                    half, s, k = n // 4, (n // 2) % 2, n % 2
                    dst = part[:, s, :, k * CH:(k + 1) * CH]
                    dve.wait_ge(s_act, 11 + 2 * n + 1)
                    nc.vector.tensor_tensor(rest[:, n % 2, :], ps[n % 4][:, :, :].rearrange("p t d -> p (t d)"), dst[:, 0, :],
                                            ALU.subtract).then_inc(s_dve, 1)
                    dve.wait_ge(s_act, 11 + 2 * n + 2)
                    nc.vector.tensor_tensor(dst[:, 2, :], rest[:, n % 2, :], dst[:, 1, :], ALU.subtract).then_inc(s_dve, 1)
                    dve.wait_ge(s_dve, 2 * n + 3)
                    dve.sem_inc(s_part, 1)

            @block.tensor
            def _(pe):
                pe.wait_ge(s_in, 13 * 16)
                for c in range(4):
                    pe.wait_ge(s_x, 16 * (c + 1))
                    for k in range(4):
                        last = nc.tensor.transpose(ps[c][:, k, :], xtok[:, k, :], ident[:, :])
                    last.then_inc(s_pe, 1)
                    pe.wait_ge(s_pe, c + 1)
                    pe.sem_inc(s_xfree, 1)
                pe.wait_ge(s_act, 2)
                for k in range(4):
                    last = nc.tensor.transpose(ps[0][:, k, :], wraw[:, k, :], ident[:, :])
                last.then_inc(s_pe, 1)
                pe.wait_ge(s_act, 6)
                for g in range(GROUPS):
                    last = nc.tensor.matmul(ps[1][:, g, :], sel[:, g, :], wT[:, 3, :], start=True, stop=True)
                last.then_inc(s_pe, 1)
                pe.wait_ge(s_act, 7)
                for c in range(4):
                    for k in range(4):
                        t = 4 * c + k
                        last = nc.tensor.matmul(ps[c][:, k, :], xT[:, 1 + t * P:1 + (t + 1) * P], wT[:, 2, :], start=True, stop=True)
                    last.then_inc(s_pe, 1)
                for n in range(8):
                    half, s, k = n // 4, (n // 2) % 2, n % 2
                    if n < 4:
                        pe.wait_ge(s_act, 8 + n)
                    else:
                        pe.wait_ge(s_dve, 1 + 2 * (n - 4) + 1)
                    c0 = 1 + half * 1024 + k * CH
                    nc.tensor.matmul(ps[n % 4][:, :, :].rearrange("p t d -> p (t d)"), wT[:, s, :], xT[:, c0:c0 + CH],
                                     start=True, stop=True).then_inc(s_pe, 1)

        ctx = ExitStack()
        with ctx:
            def sb(name, shape, dt=F32):
                return ctx.enter_context(nc.sbuf_tensor("a1_" + name, shape, dt))
            bo = sb("bo", [P, 1])
            v_grp = sb("v_grp", [P, TILES, GH, SLOT])
            wo_grp = sb("wo_grp", [P, DIM])
            mpart = sb("mpart", [P, 2, TILES, CHUNKS])
            mrow = sb("mrow", [P, TILES])
            msp = sb("msp", [P, 3, TILES])
            mspb = sb("mspb", [P, 3, TILES], BF16)
            mr = sb("mr", [P, 2, TILES])
            mT = sb("mT", [3 * TILES, P], BF16)
            prob = sb("prob", [P, 2, GH, CH])
            acc = sb("acc", [P, CH])
            den = sb("den", [P, CH])
            rec = sb("rec", [P, CH])
            onrm = sb("onrm", [P, CH])
            st_ps = [ctx.enter_context(nc.psum_tensor(f"a1_st{i}", [P, 2, CH], F32)) for i in range(2)]
            mx_ps = [ctx.enter_context(nc.psum_tensor(f"a1_mx{i}", [P, CH], F32)) for i in range(2)]
            acc_ps = ctx.enter_context(nc.psum_tensor("a1_accps", [P, CH], F32))
            x_ps = ctx.enter_context(nc.psum_tensor("a1_xps", [P, CH], F32))

            STEPS = [(c, kt) for c in range(CHUNKS) for kt in range(4 * c + 4)]
            UNITS = [(j, qt, kc) for j in range(GH) for qt in range(TILES) for kc in range(qt // 4 + 1)]
            NS, NU = len(STEPS), len(UNITS)
            PER = NU // NS
            HEAD_UNITS = NU // GH
            LAST = [4, 12, 24, 40]

            class Count:
                def __init__(self, name, per):
                    self.sem, self.per = ctx.enter_context(nc.semaphore("a1_" + name)), per

            C = {n: Count(n, per) for n, per in dict(st=2 * NS, ex=2 * NS, pv=NS, un=NU, red=NU, mrow=2 * GH, msp=6 * GH,
                                                     mt=GH, mtc=GH, mdma=48 * GH, vg=1, wg=1, ev=4, dn=4, rc=8, on=4, wo=4,
                                                     ac=4).items()}
            s_set = ctx.enter_context(nc.semaphore("a1_values_set"))
            s_att = ctx.enter_context(nc.semaphore("a1_att"))
            s_gate = ctx.enter_context(nc.semaphore("a1_gate"))
            s_bo = ctx.enter_context(nc.semaphore("a1_bo"))

            def wait(eng, name, g, k):
                eng.wait_ge(C[name].sem, g * C[name].per + (C[name].per + k))

            def schedule(do1, do2):
                for s in range(NS + 6):
                    if s < NS:
                        for jp in range(2):
                            if do2:
                                yield "scores", (s, jp)
                            if do1:
                                for u in range(PER * s + PER // 2 * jp, PER * s + PER // 2 * (jp + 1)):
                                    yield "unit", u
                    if do1 and s % 10 == 9 and s < NS:
                        yield "rowmax", s // 10
                    if do2 and 1 <= s <= NS:
                        yield "values", s - 1
                    if do2 and s in [x + 0 for x in LAST]:
                        yield "evacuate", LAST.index(s)
                    if do2 and s - 2 in LAST:
                        yield "denominator", LAST.index(s - 2)
                    if do2 and s - 4 in LAST:
                        yield "project", LAST.index(s - 4)
                    if do1 and s in (11, 21, 31, 41):
                        yield "maxima", s // 10 - 1

            def run(eng, do):
                def g_body(g, do1, do2):
                    for what, arg in schedule(do1, do2):
                        if what in do:
                            do[what](g + 1 if what in ("unit", "maxima", "rowmax") else g, arg, do1 and do2)
                if "start1" in do:
                    do["start1"](0)
                for what, arg in schedule(True, False):
                    if what in do:
                        do[what](0, arg, False)
                with eng.Fori(0, GROUPS - 1) as g:
                    if "start2" in do:
                        do["start2"](g)
                    g_body(g, True, True)
                if "start2" in do:
                    do["start2"](GROUPS - 1)
                g_body(GROUPS - 1, False, True)

            block = ctx.enter_context(nc.Block())

            @block.sync
            def _(sp):
                sp.sem_inc(C["mdma"].sem, C["mdma"].per)
                sp.dma_start(bo[:, :], w["bo"].rearrange("(p o) -> p o", o=1)).then_inc(s_bo, 16)

                def maxima(g, j, both):
                    wait(sp, "mtc", g, j + 1)
                    for s in range(3):
                        sp.dma_start(qa[SPLIT_ROWS + s:SPLIT_ROWS + s + 1, ds(g * GH + j, 1), :].rearrange("o h (t p) -> o (h t) p", p=P),
                                     mT[TILES * s:TILES * (s + 1), :]).then_inc(C["mdma"].sem, 16)

                run(sp, {"maxima": maxima})
                wait(sp, "mdma", GROUPS, 0)

            @block.gpsimd
            def _(pool):
                for n in ("vg", "wg"):
                    pool.sem_inc(C[n].sem, C[n].per)
                nc.gpsimd.memset(v_grp[:, :, :, :], 0.0).then_inc(s_set, 1)
                pool.wait_ge(s_set, 1)
                nc.gpsimd.memset(v_grp[:, :, :, HD:HD + 1], 1.0).then_inc(s_set, 1)
                pool.wait_ge(s_set, 2)

                def start2(g):
                    wait(pool, "pv", g, 0)
                    nc.gpsimd.tensor_copy(v_grp[:, :, :, 0:HD],
                                          v_all[:, :, ds(g * GH * HD, GH * HD)].rearrange("p t (h d) -> p t h d", d=HD)
                                          ).then_inc(C["vg"].sem, 1)
                    wait(pool, "wo", g, 0)
                    nc.gpsimd.tensor_copy(wo_grp[:, :], wo_pad[:, ds(g, 1), :].rearrange("p o d -> p (o d)")
                                          ).then_inc(C["wg"].sem, 1)

                run(pool, {"start2": start2})

            @block.scalar
            def _(act):
                act.sem_inc(C["ex"].sem, C["ex"].per)

                def scores(g, arg, both):
                    s, jp = arg
                    c, kt = STEPS[s]
                    off = max(0, kt * P - c * CH)
                    wait(act, "st", g, 2 * s + jp + 1)
                    wait(act, "pv", g, s - 1)
                    nc.scalar.activation(prob[:, s % 2, 2 * jp:2 * jp + 2, off:CH], st_ps[jp][:, :, off:CH], ACT.Exp,
                                         scale=HD ** -0.5).then_inc(C["ex"].sem, 1)

                run(act, {"scores": scores})

            @block.vector
            def _(dve):
                for n in ("red", "mrow", "msp", "mtc", "ev", "rc", "on", "ac"):
                    dve.sem_inc(C[n].sem, C[n].per)
                dve.wait_ge(s_bo, 16)
                nc.vector.memset(att[:, :], 0.0).then_inc(s_att, 1)
                dve.wait_ge(s_att, 1)

                def unit(g, u, both):
                    j, qt, kc = UNITS[u]
                    n = min(CH, (qt + 1) * P - kc * CH)
                    wait(dve, "un", g, u + 1)
                    nc.vector.tensor_reduce(mpart[:, j % 2, qt, kc:kc + 1], mx_ps[u % 2][:, 0:n], AX_X, ALU.max).then_inc(C["red"].sem, 1)

                def rowmax(g, j, both):
                    wait(dve, "red", g, HEAD_UNITS * (j + 1))
                    for c in range(CHUNKS):
                        last = nc.vector.tensor_reduce(mrow[:, 4 * c:4 * c + 4], mpart[:, j % 2, 4 * c:4 * c + 4, 0:c + 1], AX_X, ALU.max)
                    last.then_inc(C["mrow"].sem, 2)

                def maxima(g, j, both):
                    wait(dve, "mrow", g, 2 * j + 2)
                    k = [6 * j]

                    def step(ins):
                        k[0] += 1
                        ins.then_inc(C["msp"].sem, 1)
                        wait(dve, "msp", g, k[0])
                    wait(dve, "mt", g, j)
                    step(nc.vector.tensor_copy(mspb[:, 0, :], mrow[:, :]))
                    step(nc.vector.tensor_tensor(mr[:, 0, :], mrow[:, :], mspb[:, 0, :], ALU.subtract))
                    step(nc.vector.tensor_copy(mspb[:, 1, :], mr[:, 0, :]))
                    step(nc.vector.tensor_tensor(mr[:, 1, :], mr[:, 0, :], mspb[:, 1, :], ALU.subtract))
                    step(nc.vector.tensor_copy(mspb[:, 2, :], mr[:, 1, :]))
                    step(nc.vector.tensor_copy(msp[:, :, :], mspb[:, :, :]))
                    wait(dve, "mt", g, j + 1)
                    wait(dve, "mdma", g, 48 * j)
                    nc.vector.tensor_copy(mT[:, :], x_ps[0:3 * TILES, 0:P]).then_inc(C["mtc"].sem, 1)

                def evacuate(g, c, both):
                    wait(dve, "pv", g, LAST[c])
                    wait(dve, "wo", g, c)
                    nc.vector.tensor_copy(acc[:, :], acc_ps[:, :]).then_inc(C["ev"].sem, 1)

                def denominator(g, c, both):
                    wait(dve, "dn", g, c + 1)
                    nc.vector.tensor_scalar(den[:, :], x_ps[:, :], eb[:, ds(g, 1)] if g is not GROUPS - 1 else eb[:, g:g + 1],
                                            None, ALU.add).then_inc(C["rc"].sem, 1)
                    wait(dve, "rc", g, 2 * c + 1)
                    nc.vector.reciprocal(rec[:, :], den[:, :]).then_inc(C["rc"].sem, 1)
                    wait(dve, "rc", g, 2 * c + 2)
                    nc.vector.tensor_tensor(onrm[:, :], acc[:, :], rec[:, :], ALU.mult).then_inc(C["on"].sem, 1)

                def project(g, c, both):
                    wait(dve, "wo", g, c + 1)
                    nc.vector.tensor_tensor(att[:, c * CH:(c + 1) * CH], x_ps[:, :], att[:, c * CH:(c + 1) * CH],
                                            ALU.add).then_inc(C["ac"].sem, 1)

                run(dve, {"unit": unit, "rowmax": rowmax, "maxima": maxima, "evacuate": evacuate, "denominator": denominator,
                          "project": project})
                wait(dve, "ac", GROUPS, 0)
                nc.vector.tensor_scalar(att[:, :], att[:, :], bo[:, 0:1], None, ALU.add).then_inc(s_att, 1)

            @block.tensor
            def _(pe):
                for n in ("st", "pv", "un", "mt", "dn", "wo"):
                    pe.sem_inc(C[n].sem, C[n].per)
                pe.wait_ge(s_set, 2)
                for g in range(GROUPS):
                    pe.wait_ge(loaded[g], 12 * 16)

                def head(g, j):
                    return g * GH + j

                def unit(g, u, both):
                    j, qt, kc = UNITS[u]
                    n = min(CH, (qt + 1) * P - kc * CH)
                    diag = kc == qt // 4
                    wait(pe, "red", g, u - 1)
                    last = nc.tensor.matmul(mx_ps[u % 2][:, 0:n],
                                            qa[:, ds(head(g, j), 1), qt * P:(qt + 1) * P].rearrange("p o n -> p (o n)"),
                                            ka[:, ds(head(g, j), 1), kc * CH:kc * CH + n].rearrange("p o n -> p (o n)"),
                                            start=True, stop=not diag)
                    if diag:
                        last = nc.tensor.matmul(mx_ps[u % 2][:, n - P:n], identb[:, :], tri[:, 0, :], start=False, stop=True)
                    last.then_inc(C["un"].sem, 1)

                def scores(g, arg, both):
                    s, jp = arg
                    c, kt = STEPS[s]
                    off = max(0, kt * P - c * CH)
                    diag = kt >= 4 * c
                    if s == 0:
                        wait(pe, "mdma", g, 48 * GH)
                    wait(pe, "ex", g, 2 * s + jp - 1)
                    for k in range(2):
                        h = head(g, 2 * jp + k)
                        last = nc.tensor.matmul(st_ps[jp][:, k, off:CH],
                                                ka[:, ds(h, 1), kt * P:(kt + 1) * P].rearrange("p o n -> p (o n)"),
                                                qa[:, ds(h, 1), c * CH + off:(c + 1) * CH].rearrange("p o n -> p (o n)"),
                                                start=True, stop=not diag)
                        if diag:
                            last = nc.tensor.matmul(st_ps[jp][:, k, off:off + P], identb[:, :], tri[:, 1, :], start=False, stop=True)
                    last.then_inc(C["st"].sem, 1)

                def values(g, s, both):
                    c, kt = STEPS[s]
                    off = max(0, kt * P - c * CH)
                    if s == 0:
                        wait(pe, "vg", g, 1)
                    if kt == 0:
                        wait(pe, "ev", g, c)
                    wait(pe, "ex", g, 2 * s + 2)
                    pe.sem_inc(s_gate, 1)
                    for j in range(GH):
                        last = nc.tensor.matmul(acc_ps[SLOT * j:SLOT * (j + 1), off:CH], v_grp[:, kt, j, :],
                                                prob[:, s % 2, j, off:CH], start=kt == 0, stop=kt == 4 * c + 3)
                    last.then_inc(C["pv"].sem, 1)

                def denominator(g, c, both):
                    wait(pe, "ev", g, c + 1)
                    wait(pe, "ac", g, c)
                    if both:
                        wait(pe, "mtc", g + 1, (0, 1, 2, 4)[c])
                    else:
                        wait(pe, "mtc", g, GH)
                    nc.tensor.matmul(x_ps[:, :], denb[:, :], acc[:, :], start=True, stop=True).then_inc(C["dn"].sem, 1)

                def project(g, c, both):
                    wait(pe, "wg", g, 1)
                    wait(pe, "on", g, c + 1)
                    nc.tensor.matmul(x_ps[:, :], wo_grp[:, :], onrm[:, :], start=True, stop=True).then_inc(C["wo"].sem, 1)

                def maxima(g, j, both):
                    wait(pe, "msp", g, 6 * j + 6)
                    wait(pe, "mtc", g, j)
                    if both:
                        wait(pe, "ac", g - 1, min(j + 1, 3))
                    pe.sem_inc(s_gate, 1)
                    nc.tensor.transpose(x_ps[0:3 * TILES, 0:P], msp[:, :, :].rearrange("p s t -> p (s t)"), ident[:, :]
                                        ).then_inc(C["mt"].sem, 1)

                run(pe, {"unit": unit, "scores": scores, "values": values, "denominator": denominator,
                         "project": project, "maxima": maxima})


def local_layers(nc, xT, x_in, w, const):
    x_out = x_in
    DEPTH, _, QKV = w["Wqkv"].shape
    HEADS, HD, WIN = 16, 64, 32
    INNER = HEADS * HD
    PAIRS = HEADS // 2
    WPT = P // WIN
    FF = w["W2"].shape[1]
    FCH = [(0, 128), (128, 128), (256, FF - 256)]
    CH = 512
    HPC = CH // HD
    ctx = ExitStack()
    with ctx:
        new_semaphore = semaphores(nc, ctx)

        def sb(name, shape, dt=F32):
            return ctx.enter_context(nc.sbuf_tensor("b_" + name, shape, dt))

        def pb(name, shape):
            return ctx.enter_context(nc.psum_tensor("b_" + name, shape, F32))

        class Count:
            def __init__(self, name, per):
                self.sem, self.per = new_semaphore("b_" + name), per

            def at(self, i, k):
                return i * self.per + (self.per + k)

        x_mid = sb("x_mid", [DIM, 1 + SEQ])
        wqkv = sb("wqkv", [DIM, QKV])
        wo = sb("wo", [P, PAIRS, DIM])
        w1 = sb("w1", [DIM, 2 * FF])
        w2 = sb("w2", [P, 3, DIM])
        rot_raw = sb("rot_raw", [P, 4, TILES, HD])
        rot_tab = sb("rot_tab", [P, 4, TILES, HD])
        qk_scale = sb("qk_scale", [P, 2, DEPTH, HD])
        b1c = sb("b1c", [P, DEPTH, 2, 3])
        b2c = sb("b2c", [DIM, DEPTH])
        gc = sb("gc", [DIM, DEPTH])
        bc = sb("bc", [DIM, DEPTH])
        ident = sb("ident", [P, P])
        identb = sb("identb", [P, P], BF16)
        meanw = sb("meanw", [P, P])
        masks_in = sb("masks_in", [P, TILES, 2 * WIN])
        masks = sb("masks", [P, TILES, 2 * WIN], BF16)
        xs = sb("xs", [DIM, P])
        sq = sb("sq", [P, 4, HPC, HD])
        pa = sb("pa", [P, 4, HPC, HD])
        pbm = sb("pbm", [P, 4, HPC, HD])
        rot = sb("rot", [P, 4, HPC, HD])
        qkn = sb("qkn", [P, 4, HPC, HD])
        ln_shift = sb("ln_shift", [P, 1])
        ss = sb("ss", [P, 4, HPC])
        lnss = sb("lnss", [P, 4, HPC])
        r0 = sb("r0", [P, 4, HPC])
        nt = sb("nt", [P, 3, 4, HPC])
        rn = sb("rn", [P, 4, HPC])
        v_tok = sb("v_tok", [P, INNER])
        v_halo = sb("v_halo", [P, INNER])
        v_win = sb("v_win", [P, WPT, INNER // 2])
        qT = sb("qT", [P, PAIRS, P])
        kT = sb("kT", [P, PAIRS, WIN + P])
        smax = sb("smax", [P, HEADS])
        ssub = sb("ssub", [P, HEADS, 2 * WIN])
        pexp = sb("pexp", [P, HEADS, 2 * WIN])
        psum_ = sb("psum_", [P, HEADS])
        prec = sb("prec", [P, HEADS])
        pn = sb("pn", [P, HEADS, 2 * WIN])
        pT = sb("pT", [P, PAIRS, P])
        oT = sb("oT", [P, PAIRS, P])
        zc = sb("zc", [DIM, P])
        zq = sb("zq", [DIM, P])
        var = sb("var", [DIM, P])
        lnv = sb("lnv", [DIM, P])
        rs0 = sb("rs0", [DIM, P])
        rt = sb("rt", [DIM, 3, P])
        zs = sb("zs", [DIM, P])
        xn = sb("xn", [DIM, P])
        xng = sb("xng", [DIM, P])
        gl = sb("gl", [P, 3, P])
        hh = sb("hh", [P, 3, P])

        q_ps = [pb(f"qkv{i}", [P, CH]) for i in range(3)]
        t_ps = [pb(f"tr{i}", [P, 4, P]) for i in range(2)]
        s_ps = pb("s", [P, 2 * CH])
        m_ps = pb("m", [P, 4, P])
        s_v = s_ps[:, :].rearrange("p (h k) -> p h k", h=HEADS)
        o_v = s_ps[:, :].rearrange("p (h k) -> p h k", h=PAIRS)

        sem = lambda n: new_semaphore("b_" + n)
        s_const = sem("const")
        s_zero = sem("zero")
        s_pool = sem("pool_set")
        s_ready = sem("constants_ready")
        s_sp_gate = sem("load_gate")
        s_gate = sem("gate")
        s_wqkv = sem("wqkv_loaded")
        s_wrest = sem("wrest_loaded")
        s_tab = sem("tables_ready")
        C = {}
        for name, per in dict(xs=2, qkv=6, sq=4, ab=4, ssq=2, lns=1, rexp=1, newt=4, rot=4, qn=4, tr=4, qkT=4,
                              halo=1, v=2, vdma=32 * 8, vhalo=16, s=1, mx=1, sub=1, exp=1, sum=1, rec=1, pn=1, ptr=2,
                              ptc=2, pv=2, oc=2, wo=1, xmid=1, zs=2, mean=1, zc=1, zq=1, varm=1, var=1, lnv=1, rs=1,
                              n2=4, xn=1, xng=1, up=2, gl=3, hh=3, dn=1, xo=1).items():
            C[name] = Count(name, per)

        block = ctx.enter_context(nc.Block())

        def wait(eng, name, i, k):
            eng.wait_ge(C[name].sem, C[name].at(i, k))

        ND = 8

        @block.sync
        def _(sp):
            for n in ("vdma", "vhalo"):
                sp.sem_inc(C[n].sem, C[n].per)
            sp.dma_start(rot_raw[:, :, :, :], const["rot"]).then_inc(s_const, 16)
            sp.dma_start(ident[:, :], const["ident"]).then_inc(s_const, 16)
            sp.dma_start(masks_in[:, :, :], const["masks"]).then_inc(s_const, 16)
            for j, n in enumerate(("q_scale", "k_scale")):
                sp.dma_start(qk_scale[:, j, :, :],
                             w[n].rearrange("(o l) d -> o l d", o=1).broadcast_to([P, DEPTH, HD])).then_inc(s_const, 16)
            for c, (c0, n) in enumerate(FCH):
                for g in range(2):
                    sp.dma_start(b1c[0:n, :, g, c:c + 1],
                                 w["b1"][:, g * FF + c0:g * FF + c0 + n].rearrange("l (p o) -> p l o", o=1),
                                 allow_slow_non_contiguous=True).then_inc(s_const, 16)
            for n, t in (("b2", b2c), ("ln_g", gc), ("ln_b", bc)):
                sp.dma_start(t[:, :], w[n].rearrange("l d -> d l"), allow_slow_non_contiguous=True).then_inc(s_const, 16)
            with sp.Fori(0, DEPTH) as l:
                wait(sp, "qkv", l * TILES, 0)
                sp.sem_inc(s_sp_gate, 1)
                wl = w["Wqkv"][ds(l, 1), :, :].rearrange("o d n -> (o d) n")
                sp.dma_start(wqkv[:, 0:2 * INNER], wl[:, 0:2 * INNER]).then_inc(s_wqkv, 16)
                for a in range(2):
                    sp.dma_start(wqkv[:, 2 * INNER + a * CH:2 * INNER + (a + 1) * CH].rearrange("p (h d) -> p h d", d=HD),
                                 wl[:, 2 * INNER:].rearrange("p (h a d) -> p h a d", a=2, d=HD)[:, :, a, :]).then_inc(s_wqkv, 16)
                wait(sp, "dn", l * TILES, 0)
                sp.sem_inc(s_sp_gate, 1)
                sp.dma_start(wo[:, :, :], w["Wo"][ds(l, 1), :, :].rearrange("o (h p) d -> p (o h) d", p=P)).then_inc(s_wrest, 16)
                sp.dma_start(w1[:, :], w["W1"][ds(l, 1), :, :].rearrange("o d n -> (o d) n")).then_inc(s_wrest, 16)
                for c, (c0, n) in enumerate(FCH):
                    sp.dma_start(w2[0:n, c, :], w["W2"][ds(l, 1), c0:c0 + n, :].rearrange("o d n -> (o d) n")).then_inc(s_wrest, 16)
                with sp.Fori(0, TILES) as t:
                    i = l * TILES + t
                    wait(sp, "pv", i, 0)
                    sp.sem_inc(s_sp_gate, 1)
                    wait(sp, "v", i, 2)
                    sp.sem_inc(s_sp_gate, 1)
                    wait(sp, "vhalo", i, 0)
                    sp.sem_inc(s_sp_gate, 1)
                    for a in range(2):
                        for j in range(WPT):
                            r = 64 * a
                            sp.dma_start(v_win[r + WIN:r + 2 * WIN, j, :],
                                         v_tok[WIN * j:WIN * (j + 1), a * CH:(a + 1) * CH]).then_inc(C["vdma"].sem, 16)
                            src = v_halo[P - WIN:P, :] if j == 0 else v_tok[WIN * (j - 1):WIN * j, :]
                            sp.dma_start(v_win[r:r + WIN, j, :], src[:, a * CH:(a + 1) * CH]).then_inc(C["vdma"].sem, 16)
                    wait(sp, "vdma", i, 2 * ND * 16)
                    sp.sem_inc(s_sp_gate, 1)
                    sp.dma_start(v_halo[P - WIN:P, :], v_tok[P - WIN:P, :]).then_inc(C["vhalo"].sem, 16)
            wait(sp, "vhalo", DEPTH * TILES, 0)

        @block.gpsimd
        def _(pool):
            pool.sem_inc(C["rot"].sem, C["rot"].per)
            for n, (part, value) in enumerate(((v_halo[P - WIN:P, :], 0.0), (x_mid[:, 0:1], 0.0),
                                               (x_out[:, 0:1], 0.0), (meanw[:, :], 1.0 / DIM))):
                if n:
                    pool.wait_ge(s_pool, n)
                nc.gpsimd.memset(part, value).then_inc(s_pool, 1)
            pool.wait_ge(s_pool, 4)
            pool.sem_inc(s_zero, 4)
            with pool.Fori(0, DEPTH * TILES) as i:
                for c in range(4):
                    wait(pool, "ab", i, c + 1)
                    wait(pool, "qn", i, c - 3)
                    nc.gpsimd.tensor_tensor(rot[:, c, :, :], pa[:, c, :, :], pbm[:, c, :, :],
                                            ALU.add).then_inc(C["rot"].sem, 1)

        def layers(eng, first, body):
            with eng.Fori(0, DEPTH) as l:
                first(l)
                with eng.Fori(0, TILES - 1) as t:
                    body(l, t, l * TILES + t, True)
                body(l, TILES - 1, l * TILES + (TILES - 1), False)

        @block.scalar
        def _(act):
            for n in ("xs", "sq", "lns", "rexp", "qkT", "v", "exp", "ptc", "oc", "zs", "lnv", "rs", "gl", "halo"):
                act.sem_inc(C[n].sem, C[n].per)
            act.wait_ge(s_zero, 4)
            act.wait_ge(s_ready, 3)

            def squares(i):
                for c in range(4):
                    wait(act, "qkv", i, c + 1)
                    wait(act, "ssq", i, 0)
                    nc.scalar.activation(sq[:, c, :, :], q_ps[c % 3][:, :].rearrange("p (h d) -> p h d", d=HD),
                                         ACT.Square).then_inc(C["sq"].sem, 1)

            def values(i):
                wait(act, "vdma", i, 0)
                wait(act, "vhalo", i, 0)
                for c in range(2):
                    wait(act, "qkv", i, 5 + c)
                    nc.scalar.copy(v_tok[:, c * CH:(c + 1) * CH], q_ps[(4 + c) % 3][:, :]).then_inc(C["v"].sem, 1)

            def norms(i):
                wait(act, "ssq", i, 2)
                wait(act, "newt", i, 0)
                nc.scalar.activation(lnss[:, :, :], ss[:, :, :], ACT.Ln, scale=2.0 ** 20).then_inc(C["lns"].sem, 1)
                wait(act, "lns", i, 1)
                nc.scalar.activation(r0[:, :, :], lnss[:, :, :], ACT.Exp, scale=-0.5, bias=ln_shift[:, 0:1]
                                     ).then_inc(C["rexp"].sem, 1)

            def halo(i, first=False):
                wait(act, "s", i, 0)
                wait(act, "qkT", i, 0)
                before = (x_mid[:, 0:1].rearrange("p (o k) -> p o k", o=1).broadcast_to([P, PAIRS, WIN]) if first
                          else kT[:, :, P:WIN + P])
                nc.scalar.copy(kT[:, :, 0:WIN], before).then_inc(C["halo"].sem, 1)
                wait(act, "halo", i, 1)

            def transposed(i, fs):
                for f in fs:
                    wait(act, "tr", i, f + 1)
                    dst = qT[:, 4 * f:4 * f + 4, :] if f < 2 else kT[:, 4 * f - 8:4 * f - 4, WIN:WIN + P]
                    nc.scalar.copy(dst, t_ps[f % 2][:, :, :]).then_inc(C["qkT"].sem, 1)

            def first(l):
                nc.scalar.preload_act_table_set("natural_log_exp_and_others")
                i = l * TILES
                shifted_first(l)
                squares(i)
                values(i)
                norms(i)
                halo(i, True)
                transposed(i, range(4))

            def shifted_first(l):
                wait(act, "xo", l * TILES, 0)
                nc.scalar.copy(xs[0:64, :], x_in[0:64, 1:P + 1]).then_inc(C["xs"].sem, 1)
                nc.scalar.copy(xs[64:P, :], x_in[64:P, 0:P]).then_inc(C["xs"].sem, 1)

            def body(l, t, i, more):
                if more:
                    wait(act, "qkv", i, 6)
                    nc.scalar.copy(xs[0:64, :], x_in[0:64, ds(t * P + (P + 1), P)]).then_inc(C["xs"].sem, 1)
                    nc.scalar.copy(xs[64:P, :], x_in[64:P, ds(t * P + P, P)]).then_inc(C["xs"].sem, 1)
                    nc.scalar.preload_act_table_set("natural_log_exp_and_others")
                    squares(i + 1)
                else:
                    nc.scalar.preload_act_table_set("natural_log_exp_and_others")
                wait(act, "sub", i, 1)
                nc.scalar.activation(pexp[:, :, :], ssub[:, :, :], ACT.Exp, scale=8.0).then_inc(C["exp"].sem, 1)
                if more:
                    values(i + 1)
                    norms(i + 1)
                for f in range(2):
                    wait(act, "ptr", i, f + 1)
                    wait(act, "pv", i, 0)
                    nc.scalar.copy(pT[:, 4 * f:4 * f + 4, :], t_ps[f][:, :, :]).then_inc(C["ptc"].sem, 1)
                wait(act, "pv", i, 2)
                wait(act, "wo", i, 0)
                for f in range(2):
                    nc.scalar.copy(oT[:, 4 * f:4 * f + 4, :], o_v[:, 4 * f:4 * f + 4, :]).then_inc(C["oc"].sem, 1)
                if more:
                    halo(i + 1)
                    transposed(i + 1, (0, 1))
                wait(act, "xmid", i, 1)
                wait(act, "zc", i, 0)
                nc.scalar.copy(zs[0:64, :], x_mid[0:64, ds(t * P + 1, P)]).then_inc(C["zs"].sem, 1)
                nc.scalar.copy(zs[64:P, :], x_mid[64:P, ds(t * P, P)]).then_inc(C["zs"].sem, 1)
                if more:
                    transposed(i + 1, (2, 3))
                wait(act, "var", i, 1)
                nc.scalar.activation(lnv[:, :], var[:, :], ACT.Ln).then_inc(C["lnv"].sem, 1)
                wait(act, "lnv", i, 1)
                wait(act, "xn", i, 0)
                nc.scalar.activation(rs0[:, :], lnv[:, :], ACT.Exp, scale=-0.5).then_inc(C["rs"].sem, 1)
                wait(act, "up", i, 2)
                wait(act, "hh", i, 0)
                for c, (c0, n) in enumerate(FCH):
                    nc.scalar.activation(gl[0:n, c, :], t_ps[1][0:n, c, :], ACT.Gelu,
                                         bias=b1c[0:n, ds(l, 1), 1, c]).then_inc(C["gl"].sem, 1)

            layers(act, first, body)

        @block.vector
        def _(dve):
            for n in ("ab", "ssq", "newt", "qn", "mx", "sub", "sum", "rec", "pn", "xmid", "zc", "zq", "var", "n2", "xn",
                      "xng", "hh", "xo"):
                dve.sem_inc(C[n].sem, C[n].per)
            dve.wait_ge(s_const, 14 * 16)
            nc.vector.tensor_copy(masks[:, :, :], masks_in[:, :, :])
            nc.vector.tensor_copy(identb[:, :], ident[:, :]).then_inc(s_ready, 1)
            nc.vector.tensor_copy(x_in[:, 1:], xT[:, 1:]).then_inc(s_ready, 1)
            nc.vector.memset(ln_shift[:, :], 10.0 * float(np.log(2.0))).then_inc(s_ready, 1)

            dve.wait_ge(s_ready, 3)

            def tables(l):
                wait(dve, "ab", l * TILES, 0)
                for j in range(4):
                    for half in range(2):
                        src = half if j % 2 == 0 else 1 - half
                        lo = HD // 2 * half
                        nc.vector.tensor_tensor(
                            rot_tab[:, j, :, lo:lo + 32], rot_raw[:, j, :, lo:lo + 32],
                            qk_scale[:, j // 2, ds(l, 1), 32 * src:32 * src + 32].broadcast_to([P, TILES, 32]),
                            ALU.mult).then_inc(s_tab, 1)
                dve.wait_ge(s_tab, l * 8 + 8)

            def rotate(t, i, cs):
                for c in cs:
                    wait(dve, "sq", i, c + 1)
                    wait(dve, "rot", i, c - 3)
                    ps = q_ps[c % 3][:, :].rearrange("p (h a d) -> p h a d", a=2, d=HD // 2)
                    tn = rot_tab[:, 2 * (c // 2) + 1, ds(t, 1), :].rearrange("p o (a d) -> p o a d", a=2)
                    nc.vector.tensor_tensor(pa[:, c, :, :], q_ps[c % 3][:, :].rearrange("p (h d) -> p h d", d=HD),
                                            rot_tab[:, 2 * (c // 2), ds(t, 1), :].broadcast_to([P, HPC, HD]), ALU.mult)
                    for half in range(2):
                        last = nc.vector.tensor_tensor(
                            pbm[:, c, :, 32 * half:32 * half + 32], ps[:, :, 1 - half, :],
                            tn[:, :, half, :].broadcast_to([P, HPC, 32]), ALU.mult)
                    last.then_inc(C["ab"].sem, 1)

            def sums(i):
                nc.vector.tensor_reduce(ss[:, :, :], sq[:, :, :, :], AX_X, ALU.add).then_inc(C["ssq"].sem, 1)
                wait(dve, "ssq", i, 1)
                nc.vector.tensor_scalar_max(ss[:, :, :], ss[:, :, :], 1e-24).then_inc(C["ssq"].sem, 1)

            def newton(i):
                wait(dve, "rexp", i, 1)
                nc.vector.tensor_tensor(nt[:, 0, :, :], r0[:, :, :], r0[:, :, :], ALU.mult).then_inc(C["newt"].sem, 1)
                wait(dve, "newt", i, 1)
                nc.vector.tensor_tensor(nt[:, 1, :, :], nt[:, 0, :, :], ss[:, :, :], ALU.mult).then_inc(C["newt"].sem, 1)
                wait(dve, "newt", i, 2)
                nc.vector.tensor_scalar(nt[:, 2, :, :], nt[:, 1, :, :], -0.5, 1.5, ALU.mult, ALU.add).then_inc(C["newt"].sem, 1)
                wait(dve, "newt", i, 3)
                wait(dve, "qn", i, 0)
                nc.vector.tensor_tensor(rn[:, :, :], nt[:, 2, :, :], r0[:, :, :], ALU.mult).then_inc(C["newt"].sem, 1)
                wait(dve, "newt", i, 4)

            def normalise(i, cs):
                for c in cs:
                    wait(dve, "rot", i, c + 1)
                    wait(dve, "tr", i, c - 3)
                    nc.vector.tensor_tensor(qkn[:, c, :, :], rot[:, c, :, :],
                                            rn[:, c, :].rearrange("p (h o) -> p h o", o=1).broadcast_to([P, HPC, HD]),
                                            ALU.mult).then_inc(C["qn"].sem, 1)

            def first(l):
                i = l * TILES
                tables(l)
                rotate(0, i, range(4))
                sums(i)
                newton(i)
                normalise(i, range(4))

            def body(l, t, i, more):
                if more:
                    rotate(t + 1, i + 1, range(3))
                wait(dve, "s", i, 1)
                nc.vector.tensor_reduce(smax[:, :], s_v, AX_X, ALU.max).then_inc(C["mx"].sem, 1)
                wait(dve, "mx", i, 1)
                wait(dve, "exp", i, 0)
                nc.vector.tensor_tensor(ssub[:, :, :], s_v,
                                        smax[:, :].rearrange("p (h o) -> p h o", o=1).broadcast_to([P, HEADS, 2 * WIN]),
                                        ALU.subtract).then_inc(C["sub"].sem, 1)
                if more:
                    rotate(t + 1, i + 1, (3,))
                    sums(i + 1)
                wait(dve, "exp", i, 1)
                nc.vector.tensor_reduce(psum_[:, :], pexp[:, :, :], AX_X, ALU.add).then_inc(C["sum"].sem, 1)
                wait(dve, "sum", i, 1)
                nc.vector.reciprocal(prec[:, :], psum_[:, :]).then_inc(C["rec"].sem, 1)
                wait(dve, "rec", i, 1)
                wait(dve, "ptr", i, 0)
                nc.vector.tensor_tensor(pn[:, :, :].rearrange("p (h a) k -> p a h k", a=2),
                                        pexp[:, :, :].rearrange("p (a h) k -> p a h k", a=2),
                                        prec[:, :].rearrange("p (a h o) -> p a h o", a=2, o=1
                                                             ).broadcast_to([P, 2, PAIRS, 2 * WIN]),
                                        ALU.mult).then_inc(C["pn"].sem, 1)
                if more:
                    newton(i + 1)
                    normalise(i + 1, (0, 1))
                wait(dve, "wo", i, 1)
                nc.vector.tensor_tensor(x_mid[:, ds(t * P + 1, P)], m_ps[:, 0, :], x_in[:, ds(t * P + 1, P)],
                                        ALU.add).then_inc(C["xmid"].sem, 1)
                if more:
                    normalise(i + 1, (2, 3))
                wait(dve, "mean", i, 1)
                nc.vector.tensor_tensor(zc[:, :], zs[:, :], m_ps[:, 1, :], ALU.subtract).then_inc(C["zc"].sem, 1)
                wait(dve, "zc", i, 1)
                nc.vector.tensor_tensor(zq[:, :], zc[:, :], zc[:, :], ALU.mult).then_inc(C["zq"].sem, 1)
                wait(dve, "varm", i, 1)
                nc.vector.tensor_scalar_add(var[:, :], m_ps[:, 2, :], EPS).then_inc(C["var"].sem, 1)
                wait(dve, "rs", i, 1)
                nc.vector.tensor_tensor(rt[:, 0, :], rs0[:, :], rs0[:, :], ALU.mult).then_inc(C["n2"].sem, 1)
                wait(dve, "n2", i, 1)
                nc.vector.tensor_tensor(rt[:, 1, :], rt[:, 0, :], var[:, :], ALU.mult).then_inc(C["n2"].sem, 1)
                wait(dve, "n2", i, 2)
                nc.vector.tensor_scalar(rt[:, 2, :], rt[:, 1, :], -0.5, 1.5, ALU.mult, ALU.add).then_inc(C["n2"].sem, 1)
                wait(dve, "n2", i, 3)
                nc.vector.tensor_tensor(rt[:, 0, :], rt[:, 2, :], rs0[:, :], ALU.mult).then_inc(C["n2"].sem, 1)
                wait(dve, "n2", i, 4)
                nc.vector.tensor_tensor(xn[:, :], zc[:, :], rt[:, 0, :], ALU.mult).then_inc(C["xn"].sem, 1)
                wait(dve, "xn", i, 1)
                wait(dve, "up", i, 0)
                nc.vector.tensor_scalar(xng[:, :], xn[:, :], gc[:, ds(l, 1)], bc[:, ds(l, 1)], ALU.mult,
                                        ALU.add).then_inc(C["xng"].sem, 1)
                for c, (c0, n) in enumerate(FCH):
                    wait(dve, "gl", i, c + 1)
                    wait(dve, "dn", i, 0)
                    nc.vector.scalar_tensor_tensor(hh[0:n, c, :], t_ps[0][0:n, c, :], b1c[0:n, ds(l, 1), 0, c],
                                                   gl[0:n, c, :], ALU.add, ALU.mult).then_inc(C["hh"].sem, 1)
                wait(dve, "dn", i, 1)
                if more:
                    wait(dve, "xs", i + 1, 2)
                nc.vector.scalar_tensor_tensor(x_out[:, ds(t * P + 1, P)], m_ps[:, 3, :], b2c[:, ds(l, 1)],
                                               x_mid[:, ds(t * P + 1, P)], ALU.add, ALU.add).then_inc(C["xo"].sem, 1)

            layers(dve, first, body)

        @block.tensor
        def _(pe):
            for n in ("qkv", "tr", "s", "ptr", "pv", "wo", "mean", "varm", "up", "dn"):
                pe.sem_inc(C[n].sem, C[n].per)
            pe.wait_ge(s_zero, 4)
            pe.wait_ge(s_ready, 3)

            def project(i, cs):
                for c in cs:
                    if c == 0:
                        wait(pe, "xs", i, 2)
                    if c in (0, 3):
                        wait(pe, "ab", i, c // 3)
                    elif c in (1, 2):
                        wait(pe, "v", i, 0)
                    else:
                        wait(pe, "ab", i, c - 2)
                    nc.tensor.matmul(q_ps[c % 3][:, :], xs[:, :], wqkv[:, c * CH:(c + 1) * CH], start=True,
                                     stop=True).then_inc(C["qkv"].sem, 1)

            def turn(i, fs):
                for f in fs:
                    wait(pe, "qn", i, f + 1)
                    wait(pe, "qkT", i, f - 1)
                    for k in range(4):
                        last = nc.tensor.transpose(t_ps[f % 2][:, k, :],
                                                   qkn[:, f, 2 * k:2 * k + 2, :].rearrange("p a d -> p (a d)"), ident[:, :])
                    last.then_inc(C["tr"].sem, 1)

            def first(l):
                pe.wait_ge(s_wqkv, l * 48 + 48)
                pe.wait_ge(s_wrest, l * 80 + 80)
                i = l * TILES
                project(i, range(6))
                wait(pe, "hh", i, 0)
                turn(i, range(4))

            def body(l, t, i, more):
                if more:
                    project(i + 1, range(3))
                wait(pe, "oc", i, 0)
                wait(pe, "qkT", i, 4)
                for b in range(2):
                    mt = masks[:, ds(t, 1), :] if more else masks[:, t:t + 1, :]
                    nc.tensor.matmul(s_ps[:, b * CH:(b + 1) * CH], identb[:, :],
                                     mt.broadcast_to([P, HPC, 2 * WIN]), start=True, stop=False,
                                     skip_group_check=True)
                for hp in range(PAIRS):
                    for a in range(2):
                        for j in range(WPT):
                            last = nc.tensor.matmul(
                                s_v[WIN * j:WIN * (j + 1), a * PAIRS + hp, :],
                                qT[64 * a:64 * a + 64, hp, WIN * j:WIN * (j + 1)],
                                kT[64 * a:64 * a + 64, hp, WIN * j:WIN * (j + 2)],
                                start=False, stop=True, skip_group_check=True)
                last.then_inc(C["s"].sem, 1)
                if more:
                    project(i + 1, range(3, 6))
                wait(pe, "pn", i, 1)
                for f in range(2):
                    wait(pe, "hh", i, 0)
                    for k in range(4):
                        hp = 4 * f + k
                        last = nc.tensor.transpose(t_ps[f][:, k, :],
                                                   pn[:, 2 * hp:2 * hp + 2, :].rearrange("p a d -> p (a d)"), ident[:, :])
                    last.then_inc(C["ptr"].sem, 1)
                wait(pe, "ptc", i, 2)
                wait(pe, "vdma", i, 2 * ND * 16)
                pe.sem_inc(s_gate, 1)
                for half in range(2):
                    for hp in range(4 * half, 4 * half + 4):
                        for a in range(2):
                            for j in range(WPT):
                                last = nc.tensor.matmul(
                                    o_v[64 * a:64 * a + 64, hp, WIN * j:WIN * (j + 1)],
                                    v_win[64 * a:64 * a + 64, j, HD * hp:HD * (hp + 1)],
                                    pT[64 * a:64 * a + 64, hp, WIN * j:WIN * (j + 1)], start=True, stop=True)
                    last.then_inc(C["pv"].sem, 1)
                if more:
                    turn(i + 1, (0, 1))
                wait(pe, "oc", i, 2)
                wait(pe, "xo", i, 0)
                for hp in range(PAIRS):
                    last = nc.tensor.matmul(m_ps[:, 0, :], wo[:, hp, :], oT[:, hp, :], start=hp == 0, stop=hp == PAIRS - 1)
                last.then_inc(C["wo"].sem, 1)
                if more:
                    turn(i + 1, (2, 3))
                wait(pe, "zs", i, 2)
                nc.tensor.matmul(m_ps[:, 1, :], meanw[:, :], zs[:, :], start=True, stop=True).then_inc(C["mean"].sem, 1)
                wait(pe, "zq", i, 1)
                nc.tensor.matmul(m_ps[:, 2, :], meanw[:, :], zq[:, :], start=True, stop=True).then_inc(C["varm"].sem, 1)
                wait(pe, "xng", i, 1)
                if more:
                    wait(pe, "qkT", i + 1, 4)
                for g in range(2):
                    for c, (c0, n) in enumerate(FCH):
                        last = nc.tensor.matmul(t_ps[g][0:n, c, :], w1[:, g * FF + c0:g * FF + c0 + n], xng[:, :],
                                                start=True, stop=True)
                    last.then_inc(C["up"].sem, 1)
                wait(pe, "hh", i, 3)
                for c, (c0, n) in enumerate(FCH):
                    last = nc.tensor.matmul(m_ps[:, 3, :], w2[0:n, c, :], hh[0:n, c, :], start=c == 0, stop=c == 2)
                last.then_inc(C["dn"].sem, 1)

            layers(pe, first, body)


def residual_layernorm(nc, tag, xT, f, out, first=0):
    ctx = ExitStack()
    with ctx:
        def sb(name, shape, dt=F32):
            return ctx.enter_context(nc.sbuf_tensor(f"{tag}_{name}", shape, dt))
        meanw = sb("meanw", [P, P])
        eps = sb("eps", [P, 1])
        s = sb("s", [P, 2, CH])
        sc = sb("sc", [P, 2, CH])
        sq = sb("sq", [P, 2, CH])
        lnv = sb("lnv", [P, 2, CH])
        r0 = sb("r0", [P, 2, CH])
        t1 = sb("t1", [P, 2, CH])
        t2 = sb("t2", [P, 2, CH])
        m_ps = [ctx.enter_context(nc.psum_tensor(f"{tag}_mean{i}", [P, CH], F32)) for i in range(2)]
        v_ps = [ctx.enter_context(nc.psum_tensor(f"{tag}_var{i}", [P, CH], F32)) for i in range(2)]
        sem = lambda n: ctx.enter_context(nc.semaphore(f"{tag}_{n}"))
        s_set, s_sum, s_mean, s_cen, s_sq, s_var, s_ln, s_r0, s_nt, s_out = (
            sem(n) for n in ("set", "sum", "mean", "centred", "squared", "variance", "ln", "r0", "newton", "out"))
        block = ctx.enter_context(nc.Block())

        @block.gpsimd
        def _(pool):
            nc.gpsimd.memset(meanw[:, :], 1.0 / DIM).then_inc(s_set, 1)
            nc.gpsimd.memset(eps[:, :], EPS).then_inc(s_set, 1)

        @block.vector
        def _(dve):
            def head(c):
                x_c = xT[:, 1 + c * CH:1 + (c + 1) * CH]
                nc.vector.tensor_tensor(s[:, c % 2, :], x_c, f[:, first + c * CH:first + (c + 1) * CH], ALU.add).then_inc(s_sum, 1)

            def centre(c):
                dve.wait_ge(s_mean, c + 1)
                if c >= 2:
                    dve.wait_ge(s_out, c - 1)
                nc.vector.tensor_tensor(sc[:, c % 2, :], s[:, c % 2, :], m_ps[c % 2][:, :], ALU.subtract).then_inc(s_cen, 1)

            head(0)
            head(1)
            centre(0)
            for c in range(CHUNKS):
                if c + 1 < CHUNKS:
                    centre(c + 1)
                dve.wait_ge(s_r0, c + 1)
                nc.vector.tensor_tensor(t1[:, c % 2, :], r0[:, c % 2, :], r0[:, c % 2, :], ALU.mult).then_inc(s_nt, 1)
                dve.wait_ge(s_nt, 4 * c + 1)
                nc.vector.scalar_tensor_tensor(t2[:, c % 2, :], v_ps[c % 2][:, :], EPS, t1[:, c % 2, :], ALU.add,
                                               ALU.mult).then_inc(s_nt, 1)
                dve.wait_ge(s_nt, 4 * c + 2)
                nc.vector.tensor_scalar(t1[:, c % 2, :], t2[:, c % 2, :], -0.5, 1.5, ALU.mult, ALU.add).then_inc(s_nt, 1)
                dve.wait_ge(s_nt, 4 * c + 3)
                nc.vector.tensor_tensor(t2[:, c % 2, :], t1[:, c % 2, :], r0[:, c % 2, :], ALU.mult).then_inc(s_nt, 1)
                if c + 2 < CHUNKS:
                    head(c + 2)
                dve.wait_ge(s_nt, 4 * c + 4)
                nc.vector.tensor_tensor(out[:, 1 + c * CH:1 + (c + 1) * CH], sc[:, c % 2, :], t2[:, c % 2, :],
                                        ALU.mult).then_inc(s_out, 1)

        @block.scalar
        def _(act):
            nc.scalar.preload_act_table_set("natural_log_exp_and_others")
            act.wait_ge(s_set, 2)

            def square(c):
                act.wait_ge(s_cen, c + 1)
                nc.scalar.activation(sq[:, c % 2, :], sc[:, c % 2, :], ACT.Square).then_inc(s_sq, 1)

            square(0)
            for c in range(CHUNKS):
                if c + 1 < CHUNKS:
                    square(c + 1)
                act.wait_ge(s_var, c + 1)
                nc.scalar.activation(lnv[:, c % 2, :], v_ps[c % 2][:, :], ACT.Ln, bias=eps[:, 0:1]).then_inc(s_ln, 1)
                act.wait_ge(s_ln, c + 1)
                if c >= 2:
                    act.wait_ge(s_nt, 4 * (c - 1))
                nc.scalar.activation(r0[:, c % 2, :], lnv[:, c % 2, :], ACT.Exp, scale=-0.5).then_inc(s_r0, 1)

        @block.tensor
        def _(pe):
            pe.wait_ge(s_set, 2)

            def mean(c):
                pe.wait_ge(s_sum, c + 1)
                if c >= 2:
                    pe.wait_ge(s_cen, c - 1)
                nc.tensor.matmul(m_ps[c % 2][:, :], meanw[:, :], s[:, c % 2, :], start=True, stop=True).then_inc(s_mean, 1)

            mean(0)
            mean(1)
            for c in range(CHUNKS):
                pe.wait_ge(s_sq, c + 1)
                if c >= 2:
                    pe.wait_ge(s_nt, 4 * (c - 2) + 2)
                nc.tensor.matmul(v_ps[c % 2][:, :], meanw[:, :], sq[:, c % 2, :], start=True, stop=True).then_inc(s_var, 1)
                if c + 2 < CHUNKS:
                    mean(c + 2)


def selective_scan(nc, xT, y, w):
    NST = w["A_log"].shape[1]
    RANK = w["W_dt"].shape[1]
    ctx = ExitStack()
    with ctx:
        def sb(name, shape, dt=F32):
            return ctx.enter_context(nc.sbuf_tensor("c_" + name, shape, dt))
        w_bc = sb("w_bc", [DIM, 2 * NST])
        w_dt = sb("w_dt", [DIM, RANK])
        w_pr = sb("w_pr", [RANK, DIM])
        b_dt = sb("b_dt", [DIM, 1])
        a_log = sb("a_log", [DIM, NST])
        a_neg = sb("a_neg", [DIM, NST])
        a_exp = sb("a_exp", [DIM, NST])
        d_par = sb("d_par", [DIM, 1])
        w_b = sb("w_b", [DIM, 2, P])
        w_c = sb("w_c", [DIM, 2, P])
        low = sb("low", [RANK, SEQ])
        z = sb("z", [DIM, SEQ])
        za = sb("za", [DIM, SEQ])
        e = sb("e", [DIM, SEQ])
        delta = sb("delta", [DIM, SEQ])
        dx = sb("dx", [DIM, SEQ])
        abar = sb("abar", [DIM, 2, SEQ])
        bx = sb("bx", [DIM, SEQ])
        h = sb("h", [DIM, SEQ])
        yc = sb("yc", [DIM, 2, SEQ])
        ps = [ctx.enter_context(nc.psum_tensor(f"c_ps{i}", [P, SEQ], F32)) for i in range(2)]
        sem = lambda n: ctx.enter_context(nc.semaphore("c_" + n))
        s_in, s_low, s_lowc, s_pr, s_z, s_e, s_l, s_dl, s_dx, s_a, s_y0, s_sp = (
            sem(n) for n in ("in", "low", "lowc", "pr", "z", "e", "l", "dl", "dx", "a", "y0", "sp"))

        class Count:
            def __init__(self, name, per):
                self.sem, self.per = ctx.enter_context(nc.semaphore("c_" + name)), per

        C = {n: Count(n, per) for n, per in dict(wcol=2, b=1, c=1, abar=1, bx=1, h=1, yc=1, acc=1).items()}

        def wait(eng, name, n, k):
            eng.wait_ge(C[name].sem, n * C[name].per + (C[name].per + k))

        block = ctx.enter_context(nc.Block())

        @block.sync
        def _(sp):
            for dst, src in ((w_bc, w["W_bc"]), (w_dt, w["W_dt"]), (w_pr, w["W_dtproj"]), (a_log, w["A_log"]),
                             (b_dt, w["b_dtproj"].rearrange("(p o) -> p o", o=1)),
                             (d_par, w["D_param"].rearrange("(p o) -> p o", o=1))):
                sp.dma_start(dst[:, :], src).then_inc(s_in, 16)

        @block.gpsimd
        def _(pool):
            pool.sem_inc(C["wcol"].sem, 2)
            pool.sem_inc(C["acc"].sem, 2)
            pool.wait_ge(s_in, 96)
            nc.gpsimd.tensor_scalar(y[:, :], xT[:, 1:1 + SEQ], d_par[:, 0:1], None, ALU.mult).then_inc(s_y0, 1)
            pool.wait_ge(s_y0, 1)
            with pool.Fori(0, NST // 2) as m:
                for par in range(2):
                    n = m * 2 + par
                    wait(pool, "b", n, 0)
                    nc.gpsimd.tensor_copy(w_b[:, par, :], w_bc[:, ds(n, 1)].broadcast_to([DIM, P])).then_inc(C["wcol"].sem, 1)
                    wait(pool, "c", n, 0)
                    nc.gpsimd.tensor_copy(w_c[:, par, :], w_bc[:, ds(n + NST, 1)].broadcast_to([DIM, P])).then_inc(C["wcol"].sem, 1)
                for par in range(2):
                    n = m * 2 + par
                    wait(pool, "yc", n, 1)
                    wait(pool, "acc", n, 1)
                    nc.gpsimd.tensor_tensor(y[:, :], y[:, :], yc[:, par, :], ALU.add).then_inc(C["acc"].sem, 1)
            wait(pool, "acc", NST, 1)

        @block.scalar
        def _(act):
            act.sem_inc(C["abar"].sem, C["abar"].per)
            nc.scalar.preload_act_table_set("natural_log_exp_and_others")
            act.wait_ge(s_in, 96)
            nc.scalar.activation(a_exp[:, :], a_log[:, :], ACT.Exp).then_inc(s_a, 1)
            act.wait_ge(s_low, 4)
            nc.scalar.copy(low[:, :], ps[0][0:RANK, :]).then_inc(s_lowc, 1)
            act.wait_ge(s_pr, 4)
            nc.scalar.activation(za[:, :], ps[1][:, :], ACT.Abs, bias=b_dt[:, 0:1]).then_inc(s_z, 1)
            act.wait_ge(s_z, 1)
            nc.scalar.activation(e[:, :], za[:, :], ACT.Exp, scale=-1.0).then_inc(s_e, 1)
            act.wait_ge(s_dl, 1)
            with act.Fori(0, NST // 2) as m:
                for par in range(2):
                    n = m * 2 + par
                    wait(act, "h", n, 0)
                    nc.scalar.activation(abar[:, par, :], delta[:, :], ACT.Exp, scale=a_neg[:, ds(n, 1)]
                                         ).then_inc(C["abar"].sem, 1)

        @block.vector
        def _(dve):
            for n in ("bx", "h", "yc"):
                dve.sem_inc(C[n].sem, C[n].per)
            dve.sem_inc(C["h"].sem, 1)
            chain = [0]

            def link(ins):
                chain[0] += 1
                ins.then_inc(s_sp, 1)
                dve.wait_ge(s_sp, chain[0])

            dve.wait_ge(s_a, 1)
            link(nc.vector.tensor_scalar(a_neg[:, :], a_exp[:, :], -1.0, None, ALU.mult))
            dve.wait_ge(s_z, 1)
            link(nc.vector.tensor_scalar(z[:, :], ps[1][:, :], b_dt[:, 0:1], 0.0, ALU.add, ALU.max))
            dve.wait_ge(s_e, 1)
            link(nc.vector.tensor_scalar(h[:, :], e[:, :], 2.0, None, ALU.add))
            link(nc.vector.reciprocal(bx[:, :], h[:, :]))
            link(nc.vector.tensor_tensor(h[:, :], e[:, :], bx[:, :], ALU.mult))
            link(nc.vector.tensor_tensor(bx[:, :], h[:, :], h[:, :], ALU.mult))
            link(nc.vector.tensor_scalar(za[:, :], bx[:, :], 2.0 / 15, 2.0 / 13, ALU.mult, ALU.add))
            for k in (11, 9, 7, 5, 3):
                link(nc.vector.tensor_tensor(dx[:, :], za[:, :], bx[:, :], ALU.mult))
                link(nc.vector.tensor_scalar(za[:, :], dx[:, :], 2.0 / k, None, ALU.add))
            link(nc.vector.tensor_tensor(dx[:, :], za[:, :], bx[:, :], ALU.mult))
            link(nc.vector.scalar_tensor_tensor(za[:, :], dx[:, :], 2.0, h[:, :], ALU.add, ALU.mult))
            nc.vector.tensor_tensor(delta[:, :], z[:, :], za[:, :], ALU.add).then_inc(s_dl, 1)
            dve.wait_ge(s_dl, 1)
            link(nc.vector.tensor_tensor(dx[:, :], delta[:, :], xT[:, 1:1 + SEQ], ALU.mult))
            dve.sem_inc(s_dx, 1)
            with dve.Fori(0, NST // 2) as m:
                for par in range(2):
                    n = m * 2 + par
                    wait(dve, "b", n, 2)
                    nc.vector.tensor_tensor(bx[:, :], dx[:, :], ps[0][:, :], ALU.mult).then_inc(C["bx"].sem, 1)
                    wait(dve, "bx", n, 1)
                    wait(dve, "abar", n, 1)
                    nc.vector.tensor_tensor_scan(h[:, :], abar[:, par, :], bx[:, :], 0.0, ALU.mult, ALU.add
                                                 ).then_inc(C["h"].sem, 1)
                    wait(dve, "h", n, 2)
                    wait(dve, "c", n, 2)
                    wait(dve, "acc", n, 0)
                    nc.vector.tensor_tensor(yc[:, par, :], h[:, :], ps[1][:, :], ALU.mult).then_inc(C["yc"].sem, 1)

        @block.tensor
        def _(pe):
            for n in ("b", "c"):
                pe.sem_inc(C[n].sem, C[n].per)
                pe.sem_inc(C[n].sem, 1)
            pe.wait_ge(s_in, 96)
            for c in range(CHUNKS):
                nc.tensor.matmul(ps[0][0:RANK, c * CH:(c + 1) * CH], w_dt[:, :], xT[:, 1 + c * CH:1 + (c + 1) * CH],
                                 start=True, stop=True).then_inc(s_low, 1)
            pe.wait_ge(s_lowc, 1)
            for c in range(CHUNKS):
                nc.tensor.matmul(ps[1][:, c * CH:(c + 1) * CH], w_pr[:, :], low[:, c * CH:(c + 1) * CH],
                                 start=True, stop=True).then_inc(s_pr, 1)
            pe.wait_ge(s_dx, 1)
            with pe.Fori(0, NST // 2) as m:
                for par in range(2):
                    n = m * 2 + par
                    for k, (name, reader, wt) in enumerate((("b", "bx", w_b), ("c", "yc", w_c))):
                        wait(pe, reader, n, 0)
                        wait(pe, "wcol", n, 1 + k)
                        for c in range(CHUNKS):
                            last = nc.tensor.matmul(ps[k][:, c * CH:(c + 1) * CH], wt[:, par, :],
                                                    xT[:, 1 + c * CH:1 + (c + 1) * CH], start=True, stop=True)
                        last.then_inc(C[name].sem, 1)


def routed_experts(nc, xT, moe, w, const):
    EXPERTS, _, HID = w["Wup"].shape
    HALF = SEQ // 2
    GROUP = 64
    GPE = SEQ // GROUP
    BUDGET = GPE * 16
    EPT = P // HID
    ETILES = EXPERTS // EPT
    GPH = GPE // 2
    outer = ExitStack()
    with outer:
        def sbo(name, shape, dt=F32):
            return outer.enter_context(nc.sbuf_tensor("d_" + name, shape, dt))
        fsn = sbo("fsn", [EXPERTS, SEQ])
        w_up = sbo("w_up", [DIM, ETILES, P])
        w_gate = sbo("w_gate", [DIM, ETILES, P])
        w_down = sbo("w_down", [P, ETILES, DIM])
        b_up = sbo("b_up", [P, ETILES])
        b_gate = sbo("b_gate", [P, ETILES])
        b_down = sbo("b_down", [EXPERTS, DIM])
        spread = sbo("spread", [EXPERTS, ETILES, P])
        s_w = outer.enter_context(nc.semaphore("d_weights"))
        NW = 10

        ctx = ExitStack()
        with ctx:
            def sb(name, shape, dt=F32):
                return ctx.enter_context(nc.sbuf_tensor("d0_" + name, shape, dt))
            ident = sb("ident", [P, P])
            w_r = sb("w_r", [DIM, EXPERTS])
            b_r = sb("b_r", [P, EXPERTS])
            pairs = sb("pairs", [P, P])
            tril = sb("tril", [P, 2, P])
            gidx = sb("gidx", [P, GPH])
            lg = sb("lg", [P, 8, 2, EXPERTS])
            mx = sb("mx", [P, 8, 2])
            sx = sb("sx", [P, 8, 2])
            rx = sb("rx", [P, 8, 2])
            sc = sb("sc", [P, HALF])
            srt = [sb(f"srt{i}", [P, HALF]) for i in range(2)]
            low = sb("low", [64, HALF])
            gsum = sb("gsum", [P, GPH])
            gsT = sb("gsT", [GPH, P])
            gall = sb("gall", [P, SEQ])
            grow = sb("grow", [TILES, P])
            gcol = sb("gcol", [P, TILES])
            cmpo = sb("cmpo", [P, SEQ])
            cmp2 = sb("cmp2", [P, P])
            cnts = sb("cnts", [P, 4, TILES])
            rank = sb("rank", [P, TILES])
            sel_ = sb("sel", [P, TILES])
            col = sb("col", [P, 16])
            one = sb("one", [P, 2, GPH])
            ends = sb("ends", [P, GPH])
            gt = sb("gt", [P, HALF])
            eq = sb("eq", [P, HALF])
            pre = sb("pre", [P, HALF])
            ones = sb("ones", [P, HALF])
            fs = sb("fs", [P, HALF])
            den = sb("den", [P, HALF])
            lg_ps = ctx.enter_context(nc.psum_tensor("d0_lgps", [P, 2, 8, EXPERTS], F32))
            sc_ps = ctx.enter_context(nc.psum_tensor("d0_scps", [P, HALF], F32))
            t_ps = ctx.enter_context(nc.psum_tensor("d0_tps", [P, CH], F32))
            n_ps = ctx.enter_context(nc.psum_tensor("d0_nps", [P, CH], F32))
            dn_ps = ctx.enter_context(nc.psum_tensor("d0_dnps", [P, HALF], F32))
            g_dram = nc.dram_tensor("d0_groups", [GPE, EXPERTS], F32).ap()
            sem = lambda n: ctx.enter_context(nc.semaphore("d0_" + n))
            (s_in, s_lg, s_dve, s_exp, s_scT, s_cp, s_flip, s_gT, s_gw, s_gr, s_rowT, s_n, s_swap, s_sum, s_set) = (
                sem(n) for n in ("in", "lg", "dve", "exp", "scT", "cp", "flip", "gT", "gw", "gr", "rowT", "n", "swap",
                                 "sum", "set"))
            marks = {}
            n_swap = [0]
            block = ctx.enter_context(nc.Block())

            @block.vector
            def _(dve):
                count = [0]

                def link(ins, mark=None):
                    count[0] += 1
                    ins.then_inc(s_dve, 1)
                    dve.wait_ge(s_dve, count[0])
                    if mark:
                        marks[mark] = count[0]

                link(nc.vector.memset(ones[:, :], 1.0))
                dve.wait_ge(s_in, 16 * 6)
                dve.wait_ge(s_lg, 1)
                for a in range(2):
                    link(nc.vector.tensor_tensor(lg[:, :, a, :], lg_ps[:, a, :, :],
                                                 b_r[:, :].rearrange("p (o e) -> p o e", o=1).broadcast_to([P, 8, EXPERTS]), ALU.add))
                link(nc.vector.tensor_reduce(mx[:, :, :], lg[:, :, :, :], AX_X, ALU.max))
                wide = lambda t: t[:, :, :].rearrange("p t (a o) -> p t a o", o=1).broadcast_to([P, 8, 2, EXPERTS])
                link(nc.vector.tensor_tensor(lg[:, :, :, :], lg[:, :, :, :], wide(mx), ALU.subtract), "shifted")
                dve.wait_ge(s_exp, 1)
                link(nc.vector.tensor_reduce(sx[:, :, :], lg[:, :, :, :], AX_X, ALU.add))
                link(nc.vector.reciprocal(rx[:, :, :], sx[:, :, :]))
                link(nc.vector.tensor_tensor(lg[:, :, :, :], lg[:, :, :, :], wide(rx), ALU.mult), "scores")
                dve.wait_ge(s_scT, 1)
                link(nc.vector.tensor_copy(sc[:, :], sc_ps[:, :]))

                cur = [sc]

                def halves(t, p, d):
                    v = t[0:p, :].rearrange("p (b s d) -> p b s d", s=2, d=d)
                    return v[:, :, 0, :], v[:, :, 1, :]

                def flip_step(size):
                    nxt = srt[0] if cur[0] is not srt[0] else srt[1]
                    d = size // 2
                    a, b = halves(cur[0], P, d)
                    oa, ob = halves(nxt, P, d)
                    nc.vector.tensor_tensor(oa, a, b[:, :, ::-1], ALU.max)
                    link(nc.vector.tensor_tensor(ob[:, :, ::-1], a, b[:, :, ::-1], ALU.min))
                    cur[0] = nxt

                def step(d):
                    nxt = srt[0] if cur[0] is not srt[0] else srt[1]
                    a, b = halves(cur[0], P, d)
                    oa, ob = halves(nxt, P, d)
                    nc.vector.tensor_tensor(oa, a, b, ALU.max)
                    link(nc.vector.tensor_tensor(ob, a, b, ALU.min))
                    cur[0] = nxt

                size = 2
                while size <= HALF:
                    flip_step(size)
                    d = size // 4
                    while d >= 1:
                        step(d)
                        d //= 2
                    size *= 2
                marks["halves"] = count[0]
                marks["halves_in"] = cur[0]
                dve.wait_ge(s_flip, 16)
                nxt = srt[0] if cur[0] is not srt[0] else srt[1]
                nc.vector.tensor_tensor(nxt[0:64, :], cur[0][0:64, :], low[:, ::-1], ALU.max)
                link(nc.vector.tensor_tensor(nxt[64:P, :], cur[0][0:64, :], low[:, ::-1], ALU.min))
                cur[0] = nxt
                d = HALF // 2
                while d >= 1:
                    step(d)
                    d //= 2
                order = cur[0][:, :].rearrange("p (g n) -> p g n", n=GROUP)
                link(nc.vector.tensor_reduce(gsum[:, :], order, AX_X, ALU.add), "gsum")
                link(nc.vector.tensor_copy(ends[:, :], order[:, :, GROUP - 1]))
                dve.wait_ge(s_gT, 1)
                link(nc.vector.tensor_copy(gsT[:, :], t_ps[0:GPH, 0:P]), "gsT")
                dve.wait_ge(s_rowT, 1)
                link(nc.vector.tensor_copy(gcol[:, :], n_ps[:, 0:TILES]))
                link(nc.vector.memset(cnts[:, :, :], 0.0))
                for c in range(TILES):
                    g = gcol[:, c:c + 1]
                    if c:
                        nc.vector.tensor_scalar(cmpo[:, 0:c * P], gall[:, 0:c * P], g, 0.0, ALU.is_ge, ALU.add,
                                                accum_out=cnts[:, 0, c:c + 1])
                    if c < TILES - 1:
                        nc.vector.tensor_scalar(cmpo[:, (c + 1) * P:], gall[:, (c + 1) * P:], g, 0.0, ALU.is_gt, ALU.add,
                                                accum_out=cnts[:, 1, c:c + 1])
                    blk = gall[:, c * P:(c + 1) * P]
                    for k, op in enumerate((ALU.is_ge, ALU.is_gt)):
                        last = nc.vector.scalar_tensor_tensor(cmpo[:, c * P:(c + 1) * P] if k == 0 else cmp2[:, :], blk, g,
                                                              tril[:, k, :], op, ALU.mult, accum_out=cnts[:, 2 + k, c:c + 1])
                        link(last)
                link(nc.vector.tensor_reduce(rank[:, :], cnts[:, :, :].rearrange("p k c -> p c k"), AX_X, ALU.add))
                link(nc.vector.tensor_scalar(sel_[:, :], rank[:, :], float(BUDGET), None, ALU.is_lt))
                link(nc.vector.tensor_reduce(col[:, 0:1], sel_[:, :], AX_X, ALU.add), "swap0")
                add = lambda o, x, y: link(nc.vector.tensor_tensor(col[:, o:o + 1], col[:, x:x + 1], col[:, y:y + 1], ALU.add))
                dve.wait_ge(s_swap, 32)
                add(2, 0, 1)
                link(nc.vector.tensor_scalar(one[:, 0, :], gidx[:, :], col[:, 2:3], None, ALU.is_equal))
                link(nc.vector.tensor_tensor(one[:, 1, :], one[:, 0, :], ends[:, :], ALU.mult))
                link(nc.vector.tensor_reduce(col[:, 3:4], one[:, 1, :], AX_X, ALU.add), "swap1")
                dve.wait_ge(s_swap, 64)
                add(5, 3, 4)
                link(nc.vector.tensor_scalar(col[:, 13:14], col[:, 2:3], 0.0, BIG, ALU.is_equal, ALU.mult))
                add(5, 5, 13)
                link(nc.vector.tensor_scalar(gt[:, :], sc[:, :], col[:, 5:6], 0.0, ALU.is_gt, ALU.add, accum_out=col[:, 6:7]))
                link(nc.vector.tensor_scalar(eq[:, :], sc[:, :], col[:, 5:6], 0.0, ALU.is_equal, ALU.add,
                                             accum_out=col[:, 10:11]), "swap2")
                link(nc.vector.tensor_tensor_scan(pre[:, :], ones[:, :], eq[:, :], 0.0, ALU.mult, ALU.add))
                dve.wait_ge(s_swap, 128)
                add(8, 6, 7)
                link(nc.vector.tensor_scalar(col[:, 14:15], col[:, 2:3], float(GROUP), None, ALU.mult))
                link(nc.vector.tensor_tensor(col[:, 9:10], col[:, 14:15], col[:, 8:9], ALU.subtract))
                link(nc.vector.tensor_tensor(col[64:P, 9:10], col[64:P, 9:10], col[64:P, 11:12], ALU.subtract))
                link(nc.vector.scalar_tensor_tensor(den[:, :], pre[:, :], col[:, 9:10], eq[:, :], ALU.is_le, ALU.mult))
                link(nc.vector.tensor_tensor(gt[:, :], gt[:, :], den[:, :], ALU.add))
                link(nc.vector.tensor_tensor(fs[:, :], sc[:, :], gt[:, :], ALU.mult), "fs")
                dve.wait_ge(s_sum, 1)
                link(nc.vector.tensor_scalar(den[:, :], dn_ps[:, :], 1e-6, None, ALU.add))
                link(nc.vector.reciprocal(eq[:, :], den[:, :]))
                for a in range(2):
                    link(nc.vector.tensor_tensor(fsn[:, a * HALF:(a + 1) * HALF], fs[64 * a:64 * a + 64, :],
                                                 eq[64 * a:64 * a + 64, :], ALU.mult))

            @block.sync
            def _(sp):
                for dst, src in ((ident, const["ident"]), (w_r, w["Wr"]),
                                 (b_r, w["br"].rearrange("(o e) -> o e", o=1).broadcast_to([P, EXPERTS])),
                                 (pairs, const["pairs"]), (gidx, const["gidx"])):
                    sp.dma_start(dst[:, :], src).then_inc(s_in, 16)
                sp.dma_start(tril[:, :, :], const["tril"]).then_inc(s_in, 16)
                for dst, src in ((w_up, "Wup"), (w_gate, "Wgate")):
                    sp.dma_start(dst[:, :, :].rearrange("d t (e h) -> d (t e) h", h=HID), w[src].rearrange("e d h -> d e h")
                                 ).then_inc(s_w, 16)
                sp.dma_start(w_down[:, :, :], w["Wdown"].rearrange("(t e) h d -> (e h) t d", e=EPT)).then_inc(s_w, 16)
                for dst, src in ((b_up, "bup"), (b_gate, "bgate")):
                    sp.dma_start(dst[:, :], w[src].rearrange("(t e) h -> (e h) t", e=EPT),
                                 allow_slow_non_contiguous=True).then_inc(s_w, 16)
                sp.dma_start(b_down[:, :], w["bdown"]).then_inc(s_w, 16)
                sp.dma_start(spread[:, :, :], const["spread"]).then_inc(s_w, 16)
                sp.wait_ge(s_dve, marks["halves"])
                sp.dma_start(low[:, :], marks["halves_in"][64:P, :]).then_inc(s_flip, 16)
                sp.wait_ge(s_dve, marks["gsT"])
                for a in range(2):
                    sp.dma_start(g_dram[GPH * a:GPH * (a + 1), :], gsT[:, 64 * a:64 * a + 64]).then_inc(s_gw, 16)
                sp.wait_ge(s_gw, 32)
                flat = g_dram.rearrange("g e -> (g e)")
                sp.dma_start(grow[:, :], flat.rearrange("(c p) -> c p", p=P)).then_inc(s_gr, 16)
                sp.dma_start(gall[:, :], flat.rearrange("(o n) -> o n", o=1).broadcast_to([P, SEQ])).then_inc(s_gr, 16)
                for mark, moves in (("swap0", ((1, 0),)), ("swap1", ((4, 3),)), ("swap2", ((7, 6), (11, 10)))):
                    sp.wait_ge(s_dve, marks[mark])
                    for o, x in moves:
                        for a in range(2):
                            sp.dma_start(col[64 * a:64 * a + 64, o:o + 1], col[64 - 64 * a:P - 64 * a, x:x + 1]).then_inc(s_swap, 16)
                sp.wait_ge(s_swap, 128)
                sp.wait_ge(s_w, 16 * 7)

            @block.scalar
            def _(act):
                act.wait_ge(s_dve, marks["shifted"])
                nc.scalar.activation(lg[:, :, :, :], lg[:, :, :, :], ACT.Exp).then_inc(s_exp, 1)

            @block.tensor
            def _(pe):
                pe.wait_ge(s_in, 16 * 6)
                for t in range(TILES):
                    last = nc.tensor.matmul(lg_ps[:, t // 8, t % 8, :], xT[:, 1 + t * P:1 + (t + 1) * P], w_r[:, :],
                                            start=True, stop=True)
                last.then_inc(s_lg, 1)
                pe.wait_ge(s_dve, marks["scores"])
                for t in range(8):
                    last = nc.tensor.transpose(sc_ps[:, t * P:(t + 1) * P], lg[:, t, :, :].rearrange("p a e -> p (a e)"), ident[:, :])
                last.then_inc(s_scT, 1)
                pe.wait_ge(s_dve, marks["gsum"])
                nc.tensor.transpose(t_ps[0:GPH, 0:P], gsum[:, :], ident[:, :]).then_inc(s_gT, 1)
                pe.wait_ge(s_gr, 32)
                nc.tensor.transpose(n_ps[:, 0:TILES], grow[:, :], ident[0:TILES, 0:TILES]).then_inc(s_rowT, 1)
                pe.wait_ge(s_dve, marks["fs"])
                for k in range(2):
                    last = nc.tensor.matmul(dn_ps[:, k * CH:(k + 1) * CH], pairs[:, :], fs[:, k * CH:(k + 1) * CH],
                                            start=True, stop=True)
                last.then_inc(s_sum, 1)

        ctx = ExitStack()
        with ctx:
            def sb(name, shape, dt=F32):
                return ctx.enter_context(nc.sbuf_tensor("d1_" + name, shape, dt))
            silu = sb("silu", [P, 2, CH])
            ug = sb("ug", [P, 2, CH])
            hid = sb("hid", [P, 2, CH])
            up_ps = [ctx.enter_context(nc.psum_tensor(f"d1_up{i}", [P, CH], F32)) for i in range(2)]
            gt_ps = [ctx.enter_context(nc.psum_tensor(f"d1_gate{i}", [P, CH], F32)) for i in range(2)]
            fs_ps = [ctx.enter_context(nc.psum_tensor(f"d1_fs{i}", [P, CH], F32)) for i in range(2)]
            o_ps = [ctx.enter_context(nc.psum_tensor(f"d1_o{i}", [P, CH], F32)) for i in range(1)]

            class Count:
                def __init__(self, name, per):
                    self.sem, self.per = ctx.enter_context(nc.semaphore("d1_" + name)), per

            s_gate = ctx.enter_context(nc.semaphore("d1_checkpoint"))
            C = {n: Count(n, per) for n, per in dict(up=ETILES, gate=ETILES, fs=ETILES, silu=ETILES, ug=ETILES, hid=ETILES,
                                                     out=1, cp=1, dn=ETILES).items()}
            block = ctx.enter_context(nc.Block())

            def wait(eng, name, c, k):
                eng.wait_ge(C[name].sem, c * C[name].per + (C[name].per + k))

            def chunks(eng, body):
                with eng.Fori(0, CHUNKS) as c:
                    body(c)

            @block.scalar
            def _(act):
                act.sem_inc(C["silu"].sem, ETILES)

                def body(c):
                    for t in range(ETILES):
                        wait(act, "up", c, t + 1)
                        wait(act, "ug", c, t - 1)
                        nc.scalar.activation(silu[:, t % 2, :], up_ps[t % 2][:, :], ACT.Silu, bias=b_up[:, t:t + 1]
                                             ).then_inc(C["silu"].sem, 1)
                chunks(act, body)

            @block.vector
            def _(dve):
                for n in ("ug", "hid", "cp"):
                    dve.sem_inc(C[n].sem, C[n].per)

                def body(c):
                    for t in range(ETILES):
                        wait(dve, "gate", c, t + 1)
                        wait(dve, "silu", c, t + 1)
                        nc.vector.scalar_tensor_tensor(ug[:, t % 2, :], gt_ps[t % 2][:, :], b_gate[:, t:t + 1],
                                                       silu[:, t % 2, :], ALU.add, ALU.mult).then_inc(C["ug"].sem, 1)
                        wait(dve, "ug", c, t + 1)
                        wait(dve, "fs", c, t + 1)
                        wait(dve, "dn", c, t - 1)
                        nc.vector.tensor_tensor(hid[:, t % 2, :], ug[:, t % 2, :], fs_ps[t % 2][:, :], ALU.mult
                                                ).then_inc(C["hid"].sem, 1)
                    wait(dve, "out", c, 1)
                    nc.vector.tensor_copy(moe[:, ds(c * CH, CH)], o_ps[0][:, :]).then_inc(C["cp"].sem, 1)
                chunks(dve, body)

            @block.tensor
            def _(pe):
                for n in ("up", "gate", "fs", "out", "dn"):
                    pe.sem_inc(C[n].sem, C[n].per)

                def down(c, t):
                    wait(pe, "hid", c, t + 1)
                    nc.tensor.matmul(o_ps[0][:, :], w_down[:, t, :], hid[:, t % 2, :], start=False, stop=t == ETILES - 1
                                     ).then_inc(C["dn"].sem, 1)

                def body(c):
                    x_c = xT[:, ds(c * CH + 1, CH)]
                    f_c = fsn[:, ds(c * CH, CH)]
                    wait(pe, "cp", c, 0)
                    pe.sem_inc(s_gate, 1)
                    nc.tensor.matmul(o_ps[0][:, :], b_down[:, :], f_c, start=True, stop=False)
                    for t in range(ETILES):
                        wait(pe, "silu", c, t - 1)
                        nc.tensor.matmul(up_ps[t % 2][:, :], w_up[:, t, :], x_c, start=True, stop=True).then_inc(C["up"].sem, 1)
                        wait(pe, "ug", c, t - 1)
                        nc.tensor.matmul(gt_ps[t % 2][:, :], w_gate[:, t, :], x_c, start=True, stop=True).then_inc(C["gate"].sem, 1)
                        wait(pe, "hid", c, t - 1)
                        pe.sem_inc(s_gate, 1)
                        nc.tensor.matmul(fs_ps[t % 2][:, :], spread[:, t, :], f_c, start=True, stop=True
                                         ).then_inc(C["fs"].sem, 1)
                        if t:
                            down(c, t - 1)
                    down(c, ETILES - 1)
                    pe.sem_inc(s_gate, 1)
                    wait(pe, "dn", c, ETILES)
                    pe.sem_inc(C["out"].sem, 1)
                chunks(pe, body)


def store(nc, xT, out, const):
    with ExitStack() as ctx:
        ident = ctx.enter_context(nc.sbuf_tensor("e_ident", [P, P], F32))
        tok = ctx.enter_context(nc.sbuf_tensor("e_tok", [P, TILES, DIM], F32))
        ps = [ctx.enter_context(nc.psum_tensor(f"e_ps{c}", [P, 4, DIM], F32)) for c in range(CHUNKS)]
        s_id, s_tr, s_tok, s_out = (ctx.enter_context(nc.semaphore("e_" + n)) for n in ("ident", "turned", "tok", "out"))
        block = ctx.enter_context(nc.Block())

        @block.sync
        def _(sp):
            sp.dma_start(ident[:, :], const["ident"]).then_inc(s_id, 16)
            for c in range(CHUNKS):
                sp.wait_ge(s_tok, c + 1)
                sp.dma_start(out[c * CH:(c + 1) * CH, :].rearrange("(t p) d -> p t d", p=P), tok[:, 4 * c:4 * c + 4, :]
                             ).then_inc(s_out, 16)
            sp.wait_ge(s_out, 16 * CHUNKS)

        @block.tensor
        def _(pe):
            pe.wait_ge(s_id, 16)
            for c in range(CHUNKS):
                for k in range(4):
                    t = 4 * c + k
                    last = nc.tensor.transpose(ps[c][:, k, :], xT[:, 1 + t * P:1 + (t + 1) * P], ident[:, :])
                last.then_inc(s_tr, 1)

        @block.vector
        def _(dve):
            for c in range(CHUNKS):
                dve.wait_ge(s_tr, c + 1)
                nc.vector.tensor_copy(tok[:, 4 * c:4 * c + 4, :], ps[c][:, :, :]).then_inc(s_tok, 1)


def program(nc, aps, const, out):
    part = lambda prefix: {n[len(prefix):]: ap for n, ap in aps.items() if n.startswith(prefix)}
    with nc.sbuf_tensor("xT", [DIM, 1 + SEQ], F32) as xT, nc.sbuf_tensor("delta", [DIM, SEQ], F32) as delta:
        nc.disable_value_cache = True
        causal_attention(nc, xT, delta, part("L0_attn_"), const)
        nc.disable_value_cache = False
        residual_layernorm(nc, "ln0", xT, delta, xT)
        with nc.sbuf_tensor("x_layers", [DIM, 1 + SEQ], F32) as x_layers:
            local_layers(nc, xT, x_layers, part("L0_ffn_"), const)
            residual_layernorm(nc, "ln1", xT, x_layers, xT, first=1)
        selective_scan(nc, xT, delta, part("L1_attn_"))
        residual_layernorm(nc, "ln2", xT, delta, xT)
        routed_experts(nc, xT, delta, part("L1_ffn_"), const)
        residual_layernorm(nc, "ln3", xT, delta, xT)
        store(nc, xT, out, const)


def shape_constants():
    f = np.float32
    p = np.arange(P)
    c = {"ident": np.eye(P, dtype=f)}
    sel, denb = np.zeros((P, 4, P), f), np.zeros((P, P), f)
    for g in range(4):
        for j in range(4):
            for d in range(8):
                sel[8 * (4 * g + j) + d, g, 32 * j + d] = 1
            denb[32 * j + 8, 32 * j:32 * j + 32] = 1
    c["sel"], c["denb"] = sel, denb
    later = np.where(p[None, :] > p[:, None], -BIG, 0.0).astype(f)
    c["tri"] = np.stack([later, later.T], 1)
    key, query = np.arange(64), p % 32
    seen = (key[None, :] >= query[:, None]) & (key[None, :] <= query[:, None] + 32)
    masks = np.repeat(np.where(seen, 0.0, -BIG).astype(f)[:, None, :], TILES, 1)
    masks[0:32, 0, 0:32] = -BIG
    c["masks"] = masks
    half = np.arange(0, 64, 2, dtype=f)
    inv_freq = (f(1.0) / f(10000.0) ** (half / f(64))).astype(f)
    t = np.arange(SEQ, dtype=f)
    freqs = np.concatenate([t[:, None] * inv_freq[None, :]] * 2, -1).astype(f)
    base = ((half + f(0.4 * 64)) / f(1.4 * 64)).astype(f)
    power = ((t - SEQ // 2) / 16).astype(f)
    scale = np.concatenate([base[None, :] ** power[:, None]] * 2, -1).astype(f)
    sign = np.concatenate([-np.ones(32, f), np.ones(32, f)])
    cos, sin = np.cos(freqs), np.sin(freqs) * sign
    rot = np.stack([cos * scale, sin * scale, cos * (f(1) / scale), sin * (f(1) / scale)]).astype(f)
    c["rot"] = rot.reshape(4, TILES, P, 64).transpose(2, 0, 1, 3)
    c["pairs"] = (p[:, None] // 64 == p[None, :] // 64).astype(f)
    c["tril"] = np.stack([p[None, :] < p[:, None], p[None, :] >= p[:, None]], 1).astype(f)
    c["gidx"] = (1 + 16 * (p // 64)[:, None] + np.arange(16)[None, :]).astype(f)
    spread = np.zeros((64, 16, P), f)
    for e in range(64):
        spread[e, e // 4, 32 * (e % 4):32 * (e % 4) + 32] = 1
    c["spread"] = spread
    return {n: np.ascontiguousarray(a) for n, a in c.items()}


def kernel(**inputs):
    import concourse.bacc as bacc
    from concourse.bass_utils import run_bass_kernel_spmd

    nc = bacc.Bacc("TRN2", target_bir_lowering=False, num_devices=1)
    arrays, aps, const = {}, {}, {}
    for name, value in inputs.items():
        a = np.ascontiguousarray(value)
        arrays["in_" + name] = a
        aps[name] = nc.dram_tensor("in_" + name, a.shape, mybir.dt.from_np(a.dtype), kind="ExternalInput").ap()
    for name, a in shape_constants().items():
        arrays["const_" + name] = a
        const[name] = nc.dram_tensor("const_" + name, a.shape, mybir.dt.from_np(a.dtype), kind="ExternalInput").ap()
    out = nc.dram_tensor("out", [SEQ, DIM], F32, kind="ExternalOutput").ap()
    program(nc, aps, const, out)
    r = run_bass_kernel_spmd(nc, [arrays], core_ids=[0])
    return r.results[0]["out"].reshape(1, SEQ, DIM)
```

```python
import numpy as np
from contextlib import ExitStack
import concourse.bass as bass
from concourse import mybir

F32 = mybir.dt.float32
BF16 = mybir.dt.bfloat16
ALU = mybir.AluOpType
ACT = mybir.ActivationFunctionType
AX_X = mybir.AxisListType.X
ds = bass.ds

P = 128
SEQ = 2048
DIM = 128
TILES = SEQ // P
CH = 512
CHUNKS = SEQ // CH
EPS = 1e-5
BIG = 1e30


def semaphores(nc, ctx):
    given = []

    def give(name):
        given.append(nc.alloc_semaphore(name=name))
        return given[-1]

    def clear():
        nc.clear_and_free_semaphores(given)
        nc.all_engine_barrier()

    ctx.callback(clear)
    return give


def causal_attention(nc, xT, att, w, const):
    HEADS, HD = 16, 8
    GROUPS = 4
    GH = HEADS // GROUPS
    SLOT = 32
    Q_PARTS = (0, 0, 1, 0, 1, 2)
    K_PARTS = (0, 1, 0, 2, 1, 0)
    SPLIT_ROWS = HD * len(Q_PARTS)
    outer = ExitStack()
    with outer:
        def sbo(name, shape, dt=F32):
            return outer.enter_context(nc.sbuf_tensor("a_" + name, shape, dt))
        qa = sbo("qa", [P, HEADS, SEQ], BF16)
        ka = sbo("ka", [P, HEADS, SEQ], BF16)
        v_all = sbo("v_all", [P, TILES, DIM])
        wo_pad = sbo("wo_pad", [P, GROUPS, DIM])
        ident = sbo("ident", [P, P])
        identb = sbo("identb", [P, P], BF16)
        tri = sbo("tri", [P, 2, P], BF16)
        denb = sbo("denb", [P, P])
        eb = sbo("eb", [P, GROUPS])
        loaded = [outer.enter_context(nc.semaphore(f"a_group_loaded{g}")) for g in range(GROUPS)]

        ctx = ExitStack()
        with ctx:
            def sb(name, shape, dt=F32):
                return ctx.enter_context(nc.sbuf_tensor("a0_" + name, shape, dt))
            xtok = sb("xtok", [P, 4, DIM])
            wraw = sb("wraw", [P, 4, DIM])
            wT = sb("wT", [P, 4, DIM])
            sel = sb("sel", [P, GROUPS, P])
            tri_in = sb("tri_in", [P, 2, P])
            bo = sb("bo", [P, 1])
            part = sb("part", [P, 2, 3, SEQ // 2], BF16)
            rest = sb("rest", [P, 2, CH])
            ps = [ctx.enter_context(nc.psum_tensor(f"a0_ps{i}", [P, 4, P], F32)) for i in range(4)]
            scratch = nc.dram_tensor("a0_parts", [2, 3, DIM, SEQ], BF16).ap()
            sem = lambda n: ctx.enter_context(nc.semaphore("a0_" + n))
            s_in, s_x, s_zero, s_pe, s_act, s_dve, s_part, s_store, s_xfree = (
                sem(n) for n in ("in", "x", "zero", "pe", "act", "dve", "part", "store", "xfree"))
            block = ctx.enter_context(nc.Block())

            @block.sync
            def _(sp):
                for j, n in enumerate(("Wq", "Wk", "Wv", "Wo")):
                    sp.dma_start(wraw[:, j, :], w[n]).then_inc(s_in, 16)
                sp.dma_start(ident[:, :], const["ident"]).then_inc(s_in, 16)
                sp.dma_start(sel[:, :, :], const["sel"]).then_inc(s_in, 16)
                sp.dma_start(tri_in[:, :, :], const["tri"]).then_inc(s_in, 16)
                sp.dma_start(denb[:, :], const["denb"]).then_inc(s_in, 16)
                sp.dma_start(bo[:, :], w["bo"].rearrange("(p o) -> p o", o=1)).then_inc(s_in, 16)
                for j in range(GH):
                    sp.dma_start(eb[SLOT * j:SLOT * (j + 1), :],
                                 w["denom_bias"].rearrange("o (g j) a b -> (o a b) j g", j=GH)[:, j, :].broadcast_to([SLOT, GROUPS]),
                                 allow_slow_non_contiguous=True).then_inc(s_in, 16)
                for c in range(4):
                    if c:
                        sp.wait_ge(s_xfree, c)
                    sp.dma_start(xtok[:, :, :], w["x"][0, c * CH:(c + 1) * CH, :].rearrange("(t p) d -> p t d", p=P)
                                 ).then_inc(s_x, 16)
                for half in range(2):
                    for s in range(2):
                        sp.wait_ge(s_part, 4 * half + 2 * s + 2)
                        sp.dma_start(scratch[s, :, :, half * 1024:(half + 1) * 1024].rearrange("k p n -> p k n"),
                                     part[:, s, :, :]).then_inc(s_store, 16)
                sp.wait_ge(s_store, 64)
                for g in range(GROUPS):
                    for s, (dst, parts) in enumerate(((qa, Q_PARTS), (ka, K_PARTS))):
                        for r, k in enumerate(parts):
                            sp.dma_start(dst[HD * r:HD * (r + 1), GH * g:GH * (g + 1), :],
                                         scratch[s, k, GH * HD * g:GH * HD * (g + 1), :].rearrange("(h r) n -> r h n", r=HD)
                                         ).then_inc(loaded[g], 16)

            @block.gpsimd
            def _(pool):
                nc.gpsimd.memset(qa[:, :, :], 0.0).then_inc(s_zero, 1)
                nc.gpsimd.memset(xT[:, 0:1], 0.0).then_inc(s_zero, 1)

            @block.scalar
            def _(act):
                act.wait_ge(s_in, 13 * 16)
                nc.scalar.activation(eb[:, :], eb[:, :], ACT.Exp).then_inc(s_act, 1)
                for c in range(4):
                    act.wait_ge(s_pe, c + 1)
                    nc.scalar.copy(xT[:, 1 + c * CH:1 + (c + 1) * CH], ps[c][:, :, :].rearrange("p t d -> p (t d)")).then_inc(s_act, 1)
                act.wait_ge(s_pe, 5)
                nc.scalar.copy(wT[:, :, :], ps[0][:, :, :]).then_inc(s_act, 1)
                act.wait_ge(s_pe, 6)
                nc.scalar.copy(wo_pad[:, :, :], ps[1][:, :, :]).then_inc(s_act, 1)
                for c in range(4):
                    act.wait_ge(s_pe, 7 + c)
                    nc.scalar.copy(v_all[:, 4 * c:4 * c + 4, :], ps[c][:, :, :]).then_inc(s_act, 1)
                for n in range(8):
                    half, s, k = n // 4, (n // 2) % 2, n % 2
                    act.wait_ge(s_pe, 11 + n)
                    if half:
                        act.wait_ge(s_store, 32)
                    dst = part[:, s, :, k * CH:(k + 1) * CH]
                    nc.scalar.copy(dst[:, 0, :], ps[n % 4][:, :, :].rearrange("p t d -> p (t d)")).then_inc(s_act, 1)
                    act.wait_ge(s_dve, 2 * n + 2)
                    nc.scalar.copy(dst[:, 1, :], rest[:, n % 2, :]).then_inc(s_act, 1)

            @block.vector
            def _(dve):
                dve.wait_ge(s_zero, 2)
                nc.vector.memset(ka[:, :, :], -1.0).then_inc(s_zero, 1)
                dve.wait_ge(s_in, 13 * 16)
                nc.vector.tensor_copy(tri[:, :, :], tri_in[:, :, :])
                nc.vector.tensor_copy(identb[:, :], ident[:, :]).then_inc(s_dve, 1)
                for n in range(8):
                    half, s, k = n // 4, (n // 2) % 2, n % 2
                    dst = part[:, s, :, k * CH:(k + 1) * CH]
                    dve.wait_ge(s_act, 11 + 2 * n + 1)
                    nc.vector.tensor_tensor(rest[:, n % 2, :], ps[n % 4][:, :, :].rearrange("p t d -> p (t d)"), dst[:, 0, :],
                                            ALU.subtract).then_inc(s_dve, 1)
                    dve.wait_ge(s_act, 11 + 2 * n + 2)
                    nc.vector.tensor_tensor(dst[:, 2, :], rest[:, n % 2, :], dst[:, 1, :], ALU.subtract).then_inc(s_dve, 1)
                    dve.wait_ge(s_dve, 2 * n + 3)
                    dve.sem_inc(s_part, 1)

            @block.tensor
            def _(pe):
                pe.wait_ge(s_in, 13 * 16)
                for c in range(4):
                    pe.wait_ge(s_x, 16 * (c + 1))
                    for k in range(4):
                        last = nc.tensor.transpose(ps[c][:, k, :], xtok[:, k, :], ident[:, :])
                    last.then_inc(s_pe, 1)
                    pe.wait_ge(s_pe, c + 1)
                    pe.sem_inc(s_xfree, 1)
                pe.wait_ge(s_act, 2)
                for k in range(4):
                    last = nc.tensor.transpose(ps[0][:, k, :], wraw[:, k, :], ident[:, :])
                last.then_inc(s_pe, 1)
                pe.wait_ge(s_act, 6)
                for g in range(GROUPS):
                    last = nc.tensor.matmul(ps[1][:, g, :], sel[:, g, :], wT[:, 3, :], start=True, stop=True)
                last.then_inc(s_pe, 1)
                pe.wait_ge(s_act, 7)
                for c in range(4):
                    for k in range(4):
                        t = 4 * c + k
                        last = nc.tensor.matmul(ps[c][:, k, :], xT[:, 1 + t * P:1 + (t + 1) * P], wT[:, 2, :], start=True, stop=True)
                    last.then_inc(s_pe, 1)
                for n in range(8):
                    half, s, k = n // 4, (n // 2) % 2, n % 2
                    if n < 4:
                        pe.wait_ge(s_act, 8 + n)
                    else:
                        pe.wait_ge(s_dve, 1 + 2 * (n - 4) + 1)
                    c0 = 1 + half * 1024 + k * CH
                    nc.tensor.matmul(ps[n % 4][:, :, :].rearrange("p t d -> p (t d)"), wT[:, s, :], xT[:, c0:c0 + CH],
                                     start=True, stop=True).then_inc(s_pe, 1)

        ctx = ExitStack()
        with ctx:
            def sb(name, shape, dt=F32):
                return ctx.enter_context(nc.sbuf_tensor("a1_" + name, shape, dt))
            bo = sb("bo", [P, 1])
            v_grp = sb("v_grp", [P, TILES, GH, SLOT])
            wo_grp = sb("wo_grp", [P, DIM])
            mpart = sb("mpart", [P, 2, TILES, CHUNKS])
            mrow = sb("mrow", [P, TILES])
            msp = sb("msp", [P, 3, TILES])
            mspb = sb("mspb", [P, 3, TILES], BF16)
            mr = sb("mr", [P, 2, TILES])
            mT = sb("mT", [3 * TILES, P], BF16)
            prob = sb("prob", [P, 2, GH, CH])
            acc = sb("acc", [P, CH])
            den = sb("den", [P, CH])
            rec = sb("rec", [P, CH])
            onrm = sb("onrm", [P, CH])
            st_ps = [ctx.enter_context(nc.psum_tensor(f"a1_st{i}", [P, 2, CH], F32)) for i in range(2)]
            mx_ps = [ctx.enter_context(nc.psum_tensor(f"a1_mx{i}", [P, CH], F32)) for i in range(2)]
            acc_ps = ctx.enter_context(nc.psum_tensor("a1_accps", [P, CH], F32))
            x_ps = ctx.enter_context(nc.psum_tensor("a1_xps", [P, CH], F32))

            STEPS = [(c, kt) for c in range(CHUNKS) for kt in range(4 * c + 4)]
            UNITS = [(j, qt, kc) for j in range(GH) for qt in range(TILES) for kc in range(qt // 4 + 1)]
            NS, NU = len(STEPS), len(UNITS)
            PER = NU // NS
            HEAD_UNITS = NU // GH
            LAST = [4, 12, 24, 40]

            class Count:
                def __init__(self, name, per):
                    self.sem, self.per = ctx.enter_context(nc.semaphore("a1_" + name)), per

            C = {n: Count(n, per) for n, per in dict(st=2 * NS, ex=2 * NS, pv=NS, un=NU, red=NU, mrow=2 * GH, msp=6 * GH,
                                                     mt=GH, mtc=GH, mdma=48 * GH, vg=1, wg=1, ev=4, dn=4, rc=8, on=4, wo=4,
                                                     ac=4).items()}
            s_set = ctx.enter_context(nc.semaphore("a1_values_set"))
            s_att = ctx.enter_context(nc.semaphore("a1_att"))
            s_gate = ctx.enter_context(nc.semaphore("a1_gate"))
            s_bo = ctx.enter_context(nc.semaphore("a1_bo"))

            def wait(eng, name, g, k):
                eng.wait_ge(C[name].sem, g * C[name].per + (C[name].per + k))

            def schedule(do1, do2):
                for s in range(NS + 6):
                    if s < NS:
                        for jp in range(2):
                            if do2:
                                yield "scores", (s, jp)
                            if do1:
                                for u in range(PER * s + PER // 2 * jp, PER * s + PER // 2 * (jp + 1)):
                                    yield "unit", u
                    if do1 and s % 10 == 9 and s < NS:
                        yield "rowmax", s // 10
                    if do2 and 1 <= s <= NS:
                        yield "values", s - 1
                    if do2 and s in [x + 0 for x in LAST]:
                        yield "evacuate", LAST.index(s)
                    if do2 and s - 2 in LAST:
                        yield "denominator", LAST.index(s - 2)
                    if do2 and s - 4 in LAST:
                        yield "project", LAST.index(s - 4)
                    if do1 and s in (11, 21, 31, 41):
                        yield "maxima", s // 10 - 1

            def run(eng, do):
                def g_body(g, do1, do2):
                    for what, arg in schedule(do1, do2):
                        if what in do:
                            do[what](g + 1 if what in ("unit", "maxima", "rowmax") else g, arg, do1 and do2)
                if "start1" in do:
                    do["start1"](0)
                for what, arg in schedule(True, False):
                    if what in do:
                        do[what](0, arg, False)
                with eng.Fori(0, GROUPS - 1) as g:
                    if "start2" in do:
                        do["start2"](g)
                    g_body(g, True, True)
                if "start2" in do:
                    do["start2"](GROUPS - 1)
                g_body(GROUPS - 1, False, True)

            block = ctx.enter_context(nc.Block())

            @block.sync
            def _(sp):
                sp.sem_inc(C["mdma"].sem, C["mdma"].per)
                sp.dma_start(bo[:, :], w["bo"].rearrange("(p o) -> p o", o=1)).then_inc(s_bo, 16)

                def maxima(g, j, both):
                    wait(sp, "mtc", g, j + 1)
                    for s in range(3):
                        sp.dma_start(qa[SPLIT_ROWS + s:SPLIT_ROWS + s + 1, ds(g * GH + j, 1), :].rearrange("o h (t p) -> o (h t) p", p=P),
                                     mT[TILES * s:TILES * (s + 1), :]).then_inc(C["mdma"].sem, 16)

                run(sp, {"maxima": maxima})
                wait(sp, "mdma", GROUPS, 0)

            @block.gpsimd
            def _(pool):
                for n in ("vg", "wg"):
                    pool.sem_inc(C[n].sem, C[n].per)
                nc.gpsimd.memset(v_grp[:, :, :, :], 0.0).then_inc(s_set, 1)
                pool.wait_ge(s_set, 1)
                nc.gpsimd.memset(v_grp[:, :, :, HD:HD + 1], 1.0).then_inc(s_set, 1)
                pool.wait_ge(s_set, 2)

                def start2(g):
                    wait(pool, "pv", g, 0)
                    nc.gpsimd.tensor_copy(v_grp[:, :, :, 0:HD],
                                          v_all[:, :, ds(g * GH * HD, GH * HD)].rearrange("p t (h d) -> p t h d", d=HD)
                                          ).then_inc(C["vg"].sem, 1)
                    wait(pool, "wo", g, 0)
                    nc.gpsimd.tensor_copy(wo_grp[:, :], wo_pad[:, ds(g, 1), :].rearrange("p o d -> p (o d)")
                                          ).then_inc(C["wg"].sem, 1)

                run(pool, {"start2": start2})

            @block.scalar
            def _(act):
                act.sem_inc(C["ex"].sem, C["ex"].per)

                def scores(g, arg, both):
                    s, jp = arg
                    c, kt = STEPS[s]
                    off = max(0, kt * P - c * CH)
                    wait(act, "st", g, 2 * s + jp + 1)
                    wait(act, "pv", g, s - 1)
                    nc.scalar.activation(prob[:, s % 2, 2 * jp:2 * jp + 2, off:CH], st_ps[jp][:, :, off:CH], ACT.Exp,
                                         scale=HD ** -0.5).then_inc(C["ex"].sem, 1)

                run(act, {"scores": scores})

            @block.vector
            def _(dve):
                for n in ("red", "mrow", "msp", "mtc", "ev", "rc", "on", "ac"):
                    dve.sem_inc(C[n].sem, C[n].per)
                dve.wait_ge(s_bo, 16)
                nc.vector.memset(att[:, :], 0.0).then_inc(s_att, 1)
                dve.wait_ge(s_att, 1)

                def unit(g, u, both):
                    j, qt, kc = UNITS[u]
                    n = min(CH, (qt + 1) * P - kc * CH)
                    wait(dve, "un", g, u + 1)
                    nc.vector.tensor_reduce(mpart[:, j % 2, qt, kc:kc + 1], mx_ps[u % 2][:, 0:n], AX_X, ALU.max).then_inc(C["red"].sem, 1)

                def rowmax(g, j, both):
                    wait(dve, "red", g, HEAD_UNITS * (j + 1))
                    for c in range(CHUNKS):
                        last = nc.vector.tensor_reduce(mrow[:, 4 * c:4 * c + 4], mpart[:, j % 2, 4 * c:4 * c + 4, 0:c + 1], AX_X, ALU.max)
                    last.then_inc(C["mrow"].sem, 2)

                def maxima(g, j, both):
                    wait(dve, "mrow", g, 2 * j + 2)
                    k = [6 * j]

                    def step(ins):
                        k[0] += 1
                        ins.then_inc(C["msp"].sem, 1)
                        wait(dve, "msp", g, k[0])
                    wait(dve, "mt", g, j)
                    step(nc.vector.tensor_copy(mspb[:, 0, :], mrow[:, :]))
                    step(nc.vector.tensor_tensor(mr[:, 0, :], mrow[:, :], mspb[:, 0, :], ALU.subtract))
                    step(nc.vector.tensor_copy(mspb[:, 1, :], mr[:, 0, :]))
                    step(nc.vector.tensor_tensor(mr[:, 1, :], mr[:, 0, :], mspb[:, 1, :], ALU.subtract))
                    step(nc.vector.tensor_copy(mspb[:, 2, :], mr[:, 1, :]))
                    step(nc.vector.tensor_copy(msp[:, :, :], mspb[:, :, :]))
                    wait(dve, "mt", g, j + 1)
                    wait(dve, "mdma", g, 48 * j)
                    nc.vector.tensor_copy(mT[:, :], x_ps[0:3 * TILES, 0:P]).then_inc(C["mtc"].sem, 1)

                def evacuate(g, c, both):
                    wait(dve, "pv", g, LAST[c])
                    wait(dve, "wo", g, c)
                    nc.vector.tensor_copy(acc[:, :], acc_ps[:, :]).then_inc(C["ev"].sem, 1)

                def denominator(g, c, both):
                    wait(dve, "dn", g, c + 1)
                    nc.vector.tensor_scalar(den[:, :], x_ps[:, :], eb[:, ds(g, 1)] if g is not GROUPS - 1 else eb[:, g:g + 1],
                                            None, ALU.add).then_inc(C["rc"].sem, 1)
                    wait(dve, "rc", g, 2 * c + 1)
                    nc.vector.reciprocal(rec[:, :], den[:, :]).then_inc(C["rc"].sem, 1)
                    wait(dve, "rc", g, 2 * c + 2)
                    nc.vector.tensor_tensor(onrm[:, :], acc[:, :], rec[:, :], ALU.mult).then_inc(C["on"].sem, 1)

                def project(g, c, both):
                    wait(dve, "wo", g, c + 1)
                    nc.vector.tensor_tensor(att[:, c * CH:(c + 1) * CH], x_ps[:, :], att[:, c * CH:(c + 1) * CH],
                                            ALU.add).then_inc(C["ac"].sem, 1)

                run(dve, {"unit": unit, "rowmax": rowmax, "maxima": maxima, "evacuate": evacuate, "denominator": denominator,
                          "project": project})
                wait(dve, "ac", GROUPS, 0)
                nc.vector.tensor_scalar(att[:, :], att[:, :], bo[:, 0:1], None, ALU.add).then_inc(s_att, 1)

            @block.tensor
            def _(pe):
                for n in ("st", "pv", "un", "mt", "dn", "wo"):
                    pe.sem_inc(C[n].sem, C[n].per)
                pe.wait_ge(s_set, 2)
                for g in range(GROUPS):
                    pe.wait_ge(loaded[g], 12 * 16)

                def head(g, j):
                    return g * GH + j

                def unit(g, u, both):
                    j, qt, kc = UNITS[u]
                    n = min(CH, (qt + 1) * P - kc * CH)
                    diag = kc == qt // 4
                    wait(pe, "red", g, u - 1)
                    last = nc.tensor.matmul(mx_ps[u % 2][:, 0:n],
                                            qa[:, ds(head(g, j), 1), qt * P:(qt + 1) * P].rearrange("p o n -> p (o n)"),
                                            ka[:, ds(head(g, j), 1), kc * CH:kc * CH + n].rearrange("p o n -> p (o n)"),
                                            start=True, stop=not diag)
                    if diag:
                        last = nc.tensor.matmul(mx_ps[u % 2][:, n - P:n], identb[:, :], tri[:, 0, :], start=False, stop=True)
                    last.then_inc(C["un"].sem, 1)

                def scores(g, arg, both):
                    s, jp = arg
                    c, kt = STEPS[s]
                    off = max(0, kt * P - c * CH)
                    diag = kt >= 4 * c
                    if s == 0:
                        wait(pe, "mdma", g, 48 * GH)
                    wait(pe, "ex", g, 2 * s + jp - 1)
                    for k in range(2):
                        h = head(g, 2 * jp + k)
                        last = nc.tensor.matmul(st_ps[jp][:, k, off:CH],
                                                ka[:, ds(h, 1), kt * P:(kt + 1) * P].rearrange("p o n -> p (o n)"),
                                                qa[:, ds(h, 1), c * CH + off:(c + 1) * CH].rearrange("p o n -> p (o n)"),
                                                start=True, stop=not diag)
                        if diag:
                            last = nc.tensor.matmul(st_ps[jp][:, k, off:off + P], identb[:, :], tri[:, 1, :], start=False, stop=True)
                    last.then_inc(C["st"].sem, 1)

                def values(g, s, both):
                    c, kt = STEPS[s]
                    off = max(0, kt * P - c * CH)
                    if s == 0:
                        wait(pe, "vg", g, 1)
                    if kt == 0:
                        wait(pe, "ev", g, c)
                    wait(pe, "ex", g, 2 * s + 2)
                    pe.sem_inc(s_gate, 1)
                    for j in range(GH):
                        last = nc.tensor.matmul(acc_ps[SLOT * j:SLOT * (j + 1), off:CH], v_grp[:, kt, j, :],
                                                prob[:, s % 2, j, off:CH], start=kt == 0, stop=kt == 4 * c + 3)
                    last.then_inc(C["pv"].sem, 1)

                def denominator(g, c, both):
                    wait(pe, "ev", g, c + 1)
                    wait(pe, "ac", g, c)
                    if both:
                        wait(pe, "mtc", g + 1, (0, 1, 2, 4)[c])
                    else:
                        wait(pe, "mtc", g, GH)
                    nc.tensor.matmul(x_ps[:, :], denb[:, :], acc[:, :], start=True, stop=True).then_inc(C["dn"].sem, 1)

                def project(g, c, both):
                    wait(pe, "wg", g, 1)
                    wait(pe, "on", g, c + 1)
                    nc.tensor.matmul(x_ps[:, :], wo_grp[:, :], onrm[:, :], start=True, stop=True).then_inc(C["wo"].sem, 1)

                def maxima(g, j, both):
                    wait(pe, "msp", g, 6 * j + 6)
                    wait(pe, "mtc", g, j)
                    if both:
                        wait(pe, "ac", g - 1, min(j + 1, 3))
                    pe.sem_inc(s_gate, 1)
                    nc.tensor.transpose(x_ps[0:3 * TILES, 0:P], msp[:, :, :].rearrange("p s t -> p (s t)"), ident[:, :]
                                        ).then_inc(C["mt"].sem, 1)

                run(pe, {"unit": unit, "scores": scores, "values": values, "denominator": denominator,
                         "project": project, "maxima": maxima})


def local_layers(nc, xT, x_in, w, const):
    x_out = x_in
    DEPTH, _, QKV = w["Wqkv"].shape
    HEADS, HD, WIN = 16, 64, 32
    INNER = HEADS * HD
    PAIRS = HEADS // 2
    WPT = P // WIN
    FF = w["W2"].shape[1]
    FCH = [(0, 128), (128, 128), (256, FF - 256)]
    CH = 512
    CHUNKS = SEQ // CH
    HPC = CH // HD
    ctx = ExitStack()
    with ctx:
        new_semaphore = semaphores(nc, ctx)

        def sb(name, shape, dt=F32):
            return ctx.enter_context(nc.sbuf_tensor("b_" + name, shape, dt))

        def pb(name, shape):
            return ctx.enter_context(nc.psum_tensor("b_" + name, shape, F32))

        class Count:
            def __init__(self, name, per):
                self.sem, self.per = new_semaphore("b_" + name), per

            def at(self, i, k):
                return i * self.per + (self.per + k)

        x_mid = sb("x_mid", [DIM, 1 + SEQ])
        wqkv = sb("wqkv", [DIM, QKV])
        wo = sb("wo", [P, PAIRS, DIM])
        w1 = sb("w1", [DIM, 2 * FF])
        w2 = sb("w2", [P, 3, DIM])
        rot_raw = sb("rot_raw", [P, 4, TILES, HD])
        rot_tab = sb("rot_tab", [P, 4, TILES, HD])
        qk_scale = sb("qk_scale", [P, 2, DEPTH, HD])
        b1c = sb("b1c", [P, DEPTH, 2, 3])
        b2c = sb("b2c", [DIM, DEPTH])
        gc = sb("gc", [DIM, DEPTH])
        bc = sb("bc", [DIM, DEPTH])
        ident = sb("ident", [P, P])
        identb = sb("identb", [P, P], BF16)
        meanw = sb("meanw", [P, P])
        masks = sb("masks", [P, TILES, 2 * WIN], BF16)
        xs = sb("xs", [DIM, P])
        sq = sb("sq", [P, 4, HPC, HD])
        masks_in = sq[:, 0:2, :, :].rearrange("p c h d -> p (c h) d")
        pa = sb("pa", [P, 4, HPC, HD])
        pbm = sb("pbm", [P, 4, HPC, HD])
        rot = sb("rot", [P, 4, HPC, HD])
        qkn = sb("qkn", [P, 4, HPC, HD])
        ln_shift = sb("ln_shift", [P, 1])
        ss = sb("ss", [P, 4, HPC])
        lnss = sb("lnss", [P, 4, HPC])
        r0 = sb("r0", [P, 4, HPC])
        nt = sb("nt", [P, 3, 4, HPC])
        rn = sb("rn", [P, 4, HPC])
        v_tok = sb("v_tok", [P, 2, INNER])
        v_win = sb("v_win", [P, WPT, INNER // 2])
        qT = sb("qT", [P, PAIRS, P])
        kT = sb("kT", [P, PAIRS, 2, WIN + P])
        smax = sb("smax", [P, HEADS])
        ssub = sb("ssub", [P, HEADS, 2 * WIN])
        pexp = sb("pexp", [P, HEADS, 2 * WIN])
        psum_ = sb("psum_", [P, HEADS])
        prec = sb("prec", [P, HEADS])
        pn = sb("pn", [P, HEADS, 2 * WIN])
        pT = sb("pT", [P, PAIRS, 2, P])
        oT = sb("oT", [P, PAIRS, P])
        zc = sb("zc", [DIM, CH])
        zq = sb("zq", [DIM, CH])
        lnv = sb("lnv", [DIM, CH])
        rs0 = sb("rs0", [DIM, CH])
        rt = sb("rt", [DIM, 3, CH])
        zs = sb("zs", [DIM, CH])
        xn = sb("xn", [DIM, CH])
        xng = sb("xng", [DIM, CH])
        gl, hh = (t[:, 0:3, :, :].rearrange("p c h d -> p c (h d)") for t in (pa, pbm))
        g_half = sb("g_half", [DIM, DEPTH])
        eps_col = sb("eps_col", [DIM, 1])

        banks = pb("banks", [P, 8, CH])
        q_ps = [banks[:, b, :] for b in (0, 1, 2)]
        t_ps = [banks[:, b, :].rearrange("p (k n) -> p k n", k=4) for b in (3, 4)]
        s_ps = banks[:, 5:7, :].rearrange("p b n -> p (b n)")
        wo_ps = banks[:, 7, 0:P]
        value_ps, gate_ps, stat_ps, down_ps = [banks[:, b, :] for b in (0, 1, 2)], [banks[:, b, :] for b in (3, 4, 5)], \
            banks[:, 6, :], banks[:, 7, :]
        s_v = s_ps.rearrange("p (h k) -> p h k", h=HEADS)
        o_v = s_ps.rearrange("p (g a k) -> p g a k", g=PAIRS // 2, a=2)

        sem = lambda n: new_semaphore("b_" + n)
        s_const = sem("const")
        s_zero = sem("zero")
        s_pool = sem("pool_set")
        s_ready = sem("constants_ready")
        s_sp_gate = sem("load_gate")
        s_gate = sem("gate")
        s_wqkv = sem("wqkv_loaded")
        s_wo = sem("wo_loaded")
        s_wffn = sem("wffn_loaded")
        s_tab = sem("tables_ready")
        C = {}
        for name, per in dict(xs=2, qkv=6, sq=4, ab=4, ssq=2, lns=1, rexp=1, newt=4, rot=4, qn=4, tr=4, qkT=4,
                              halo=1, v=2, vdma=14 * 16, vhalo=2 * 16, s=2, mx=2, sub=2, exp=2, sum=2, rec=1, pn=1, ptr=2,
                              ptc=2, pv=2, oc=2, wo=1, xmid=1, zs=2, mean=1, zc=1, zq=1, varm=1, lnv=1, rs=1,
                              n2=3, xn=1, xng=1, up=3, gl=3, hh=3, dn=1, xo=1).items():
            C[name] = Count(name, per)

        block = ctx.enter_context(nc.Block())

        def wait(eng, name, i, k):
            eng.wait_ge(C[name].sem, C[name].at(i, k))

        @block.sync
        def _(sp):
            for n in ("vdma", "vhalo"):
                sp.sem_inc(C[n].sem, C[n].per)
            sp.dma_start(rot_raw[:, :, :, :], const["rot"]).then_inc(s_const, 16)
            sp.dma_start(ident[:, :], const["ident"]).then_inc(s_const, 16)
            sp.dma_start(masks_in, const["masks"]).then_inc(s_const, 16)
            for j, n in enumerate(("q_scale", "k_scale")):
                sp.dma_start(qk_scale[:, j, :, :],
                             w[n].rearrange("(o l) d -> o l d", o=1).broadcast_to([P, DEPTH, HD])).then_inc(s_const, 16)
            for c, (c0, n) in enumerate(FCH):
                for g in range(2):
                    sp.dma_start(b1c[0:n, :, g, c:c + 1],
                                 w["b1"][:, g * FF + c0:g * FF + c0 + n].rearrange("l (p o) -> p l o", o=1),
                                 allow_slow_non_contiguous=True).then_inc(s_const, 16)
            for n, t in (("b2", b2c), ("ln_g", gc), ("ln_b", bc)):
                sp.dma_start(t[:, :], w[n].rearrange("l d -> d l"), allow_slow_non_contiguous=True).then_inc(s_const, 16)
            with sp.Fori(0, DEPTH) as l:
                wait(sp, "qkv", l * TILES, 0)
                sp.sem_inc(s_sp_gate, 1)
                wl = w["Wqkv"][ds(l, 1), :, :].rearrange("o d n -> (o d) n")
                sp.dma_start(wqkv[:, 0:2 * INNER], wl[:, 0:2 * INNER]).then_inc(s_wqkv, 16)
                for a in range(2):
                    sp.dma_start(wqkv[:, 2 * INNER + a * CH:2 * INNER + (a + 1) * CH].rearrange("p (h d) -> p h d", d=HD),
                                 wl[:, 2 * INNER:].rearrange("p (h a d) -> p h a d", a=2, d=HD)[:, :, a, :]).then_inc(s_wqkv, 16)
                wait(sp, "wo", l * TILES, 0)
                sp.sem_inc(s_sp_gate, 1)
                for b in range(2):
                    for a in range(2):
                        sp.dma_start(wo[64 * b:64 * b + 64, :, :].rearrange("p (g a) d -> p g a d", a=2)[:, :, a, :],
                                     w["Wo"][ds(l, 1), :, :].rearrange("o (g b a p) d -> p b a (o g) d", b=2, a=2, p=HD
                                                                       )[:, b, a]).then_inc(s_wo, 16)
                wait(sp, "dn", l * CHUNKS, 0)
                sp.sem_inc(s_sp_gate, 1)
                sp.dma_start(w1[:, :], w["W1"][ds(l, 1), :, :].rearrange("o d n -> (o d) n")).then_inc(s_wffn, 16)
                for c, (c0, n) in enumerate(FCH):
                    sp.dma_start(w2[0:n, c, :], w["W2"][ds(l, 1), c0:c0 + n, :].rearrange("o d n -> (o d) n")).then_inc(s_wffn, 16)
                with sp.Fori(0, TILES) as t:
                    i = l * TILES + t
                    wait(sp, "pv", i, 0)
                    sp.sem_inc(s_sp_gate, 1)
                    wait(sp, "v", i, 2)
                    sp.sem_inc(s_sp_gate, 1)
                    this, before = v_tok[:, ds(t % 2, 1), :], v_tok[:, ds((t + 1) % 2, 1), :]
                    half = lambda a: slice(a * CH, (a + 1) * CH)
                    for a in range(2):
                        sp.dma_start(v_win[64 * a:64 * a + WIN, 0:1, :], before[P - WIN:P, :, half(a)]
                                     ).then_inc(C["vhalo"].sem, 16)
                    for a in range(2):
                        r = 64 * a
                        for j in range(WPT):
                            own = this[WIN * j:WIN * (j + 1), :, half(a)]
                            sp.dma_start(v_win[r + WIN:r + 2 * WIN, j:j + 1, :], own).then_inc(C["vdma"].sem, 16)
                            if j < WPT - 1:
                                sp.dma_start(v_win[r:r + WIN, j + 1:j + 2, :], own).then_inc(C["vdma"].sem, 16)
            wait(sp, "vdma", DEPTH * TILES, 0)
            wait(sp, "vhalo", DEPTH * TILES, 0)

        @block.gpsimd
        def _(pool):
            pool.sem_inc(C["rot"].sem, C["rot"].per)
            for n, (part, value) in enumerate(((kT[:, :, :, :], 0.0), (pT[:, :, :, :], 0.0), (v_tok[P - WIN:P, 1, :], 0.0), (x_mid[:, 0:1], 0.0),
                                               (x_out[:, 0:1], 0.0), (meanw[:, :], 1.0 / DIM))):
                if n:
                    pool.wait_ge(s_pool, n)
                nc.gpsimd.memset(part, value).then_inc(s_pool, 1)
            pool.wait_ge(s_pool, 6)
            pool.sem_inc(s_zero, 6)
            pool.wait_ge(s_const, 14 * 16)
            with pool.Fori(0, DEPTH) as l:
                wait(pool, "ab", l * TILES, 0)
                for j in range(4):
                    for half in range(2):
                        src = half if j % 2 == 0 else 1 - half
                        lo = HD // 2 * half
                        nc.gpsimd.tensor_tensor(
                            rot_tab[:, j, :, lo:lo + 32], rot_raw[:, j, :, lo:lo + 32],
                            qk_scale[:, j // 2, ds(l, 1), 32 * src:32 * src + 32].broadcast_to([P, TILES, 32]),
                            ALU.mult).then_inc(s_tab, 1)
                with pool.Fori(0, TILES) as t:
                    i = l * TILES + t
                    for c in range(4):
                        wait(pool, "ab", i, c + 1)
                        wait(pool, "qn", i, c - 3)
                        nc.gpsimd.tensor_tensor(rot[:, c, :, :], pa[:, c, :, :], pbm[:, c, :, :],
                                                ALU.add).then_inc(C["rot"].sem, 1)

        def layers(eng, first, attend, statistics, feed):
            with eng.Fori(0, DEPTH) as l:
                first(l)
                with eng.Fori(0, TILES - 2) as t:
                    attend(l, t, l * TILES + t, 2)
                for t in range(TILES - 2, TILES):
                    attend(l, t, l * TILES + t, TILES - 1 - t)
                statistics(l, 0, l * CHUNKS)
                with eng.Fori(0, CHUNKS - 1) as n:
                    feed(l, n, l * CHUNKS + n, True)
                feed(l, CHUNKS - 1, l * CHUNKS + (CHUNKS - 1), False)

        @block.scalar
        def _(act):
            for n in ("xs", "sq", "lns", "rexp", "qkT", "v", "exp", "ptc", "oc", "zs", "zq", "lnv", "rs", "gl", "halo"):
                act.sem_inc(C[n].sem, C[n].per)
            act.wait_ge(s_zero, 6)
            act.wait_ge(s_ready, 3)

            def shifted(l, t, i):
                wait(act, "qkv", i - 1, 6)
                nc.scalar.copy(xs[0:64, :], x_in[0:64, ds(t * P + 1, P)]).then_inc(C["xs"].sem, 1)
                nc.scalar.copy(xs[64:P, :], x_in[64:P, ds(t * P, P)]).then_inc(C["xs"].sem, 1)

            def squares(i, cs):
                for c in cs:
                    wait(act, "qkv", i, c + 1)
                    wait(act, "ssq", i, 0)
                    nc.scalar.activation(sq[:, c, :, :], q_ps[c % 3].rearrange("p (h d) -> p h d", d=HD),
                                         ACT.Square).then_inc(C["sq"].sem, 1)

            def values(t, i):
                wait(act, "vdma", i - 1, 0)
                wait(act, "vhalo", i, 0)
                for c in range(2):
                    wait(act, "qkv", i, 5 + c)
                    nc.scalar.copy(v_tok[:, ds(t % 2, 1), c * CH:(c + 1) * CH].rearrange("p o n -> p (o n)"), q_ps[(4 + c) % 3]
                                   ).then_inc(C["v"].sem, 1)

            def norms(i):
                wait(act, "ssq", i, 2)
                wait(act, "newt", i, 0)
                nc.scalar.activation(lnss[:, :, :], ss[:, :, :], ACT.Ln, scale=2.0 ** 20).then_inc(C["lns"].sem, 1)
                wait(act, "lns", i, 1)
                nc.scalar.activation(r0[:, :, :], lnss[:, :, :], ACT.Exp, scale=-0.5, bias=ln_shift[:, 0:1]
                                     ).then_inc(C["rexp"].sem, 1)

            def halo(i, first=False):
                wait(act, "s", i, 0)
                wait(act, "qkT", i, 0)
                before = (x_mid[:, 0:1].rearrange("p (o a k) -> p o a k", o=1, a=1).broadcast_to([P, PAIRS, 2, WIN]) if first
                          else kT[:, :, :, P:WIN + P])
                nc.scalar.copy(kT[:, :, :, 0:WIN], before).then_inc(C["halo"].sem, 1)
                wait(act, "halo", i, 1)

            def transposed(i, fs):
                for f in fs:
                    wait(act, "tr", i, f + 1)
                    if f < 2:
                        last = nc.scalar.copy(qT[:, 4 * f:4 * f + 4, :], t_ps[f % 2])
                    else:
                        for a in range(2):
                            rows = slice(64 * a, 64 * a + 64)
                            last = nc.scalar.copy(kT[rows, 4 * f - 8:4 * f - 4, a, WIN:WIN + P], t_ps[f % 2][rows])
                    last.then_inc(C["qkT"].sem, 1)

            def first(l):
                nc.scalar.preload_act_table_set("natural_log_exp_and_others")
                i = l * TILES
                wait(act, "xo", l * CHUNKS, 0)
                shifted(l, 0, i)
                squares(i, range(4))
                values(0, i)
                norms(i)
                halo(i, True)
                transposed(i, range(4))
                shifted(l, 1, i + 1)
                squares(i + 1, range(4))
                norms(i + 1)

            def attend(l, t, i, left):
                if left:
                    halo(i + 1)
                    transposed(i + 1, (0, 1))
                for a in range(2):
                    wait(act, "sub", i, a + 1)
                    h = slice(a * PAIRS, (a + 1) * PAIRS)
                    nc.scalar.activation(pexp[:, h, :], ssub[:, h, :], ACT.Exp, scale=8.0).then_inc(C["exp"].sem, 1)
                if left == 2:
                    shifted(l, t + 2, i + 2)
                if left:
                    values(t + 1, i + 1)
                    transposed(i + 1, (2, 3))
                if left == 2:
                    squares(i + 2, (0, 1))
                for f in range(2):
                    wait(act, "ptr", i, f + 1)
                    wait(act, "pv", i, 0)
                    for a in range(2):
                        rows = slice(64 * a, 64 * a + 64)
                        last = nc.scalar.copy(pT[rows, 4 * f:4 * f + 4, a, :], t_ps[f][rows])
                    last.then_inc(C["ptc"].sem, 1)
                if left == 2:
                    squares(i + 2, (2, 3))
                wait(act, "wo", i, 0)
                for f in range(2):
                    wait(act, "pv", i, f + 1)
                    nc.scalar.copy(oT[:, 4 * f:4 * f + 4, :].rearrange("p (g a) k -> p g a k", a=2),
                                   o_v[:, 2 * f:2 * f + 2, :, :]).then_inc(C["oc"].sem, 1)
                if left == 2:
                    norms(i + 2)

            def statistics(l, n, j):
                if isinstance(n, int) and n == 0:
                    wait(act, "xmid", l * TILES + (TILES - 1), 1)
                wait(act, "zc", j, 0)
                nc.scalar.copy(zs[0:64, :], x_mid[0:64, ds(n * CH + 1, CH)]).then_inc(C["zs"].sem, 1)
                nc.scalar.copy(zs[64:P, :], x_mid[64:P, ds(n * CH, CH)]).then_inc(C["zs"].sem, 1)
                wait(act, "zc", j, 1)
                nc.scalar.activation(zq[:, :], zc[:, :], ACT.Square).then_inc(C["zq"].sem, 1)
                nc.scalar.preload_act_table_set("natural_log_exp_and_others")
                wait(act, "varm", j, 1)
                nc.scalar.activation(lnv[:, :], stat_ps, ACT.Ln, bias=eps_col[:, 0:1]).then_inc(C["lnv"].sem, 1)
                wait(act, "lnv", j, 1)
                wait(act, "xn", j, 0)
                nc.scalar.activation(rs0[:, :], lnv[:, :], ACT.Exp, scale=-0.5).then_inc(C["rs"].sem, 1)

            def feed(l, n, j, more):
                if more:
                    statistics(l, n + 1, j + 1)
                for c, (c0, m) in enumerate(FCH):
                    wait(act, "up", j, c + 1)
                    wait(act, "hh", j, c - 2)
                    nc.scalar.activation(gl[0:m, c, :], gate_ps[c][0:m, :], ACT.Gelu,
                                         bias=b1c[0:m, ds(l, 1), 1, c]).then_inc(C["gl"].sem, 1)

            layers(act, first, attend, statistics, feed)

        @block.vector
        def _(dve):
            for n in ("ab", "ssq", "newt", "qn", "mx", "sub", "sum", "rec", "pn", "xmid", "zc", "n2", "xn",
                      "xng", "hh", "xo"):
                dve.sem_inc(C[n].sem, C[n].per)
            dve.wait_ge(s_const, 14 * 16)
            nc.vector.tensor_copy(masks[:, :, :], masks_in)
            nc.vector.tensor_copy(identb[:, :], ident[:, :]).then_inc(s_ready, 1)
            nc.vector.tensor_copy(x_in[:, 1:], xT[:, 1:]).then_inc(s_ready, 1)
            nc.vector.memset(ln_shift[:, :], 10.0 * float(np.log(2.0)))
            nc.vector.memset(eps_col[:, :], EPS)
            nc.vector.tensor_scalar_mul(g_half[:, :], gc[:, :], -0.5).then_inc(s_ready, 1)

            dve.wait_ge(s_ready, 3)

            def rotate(t, i, cs):
                for c in cs:
                    wait(dve, "sq", i, c + 1)
                    wait(dve, "rot", i, c - 3)
                    ps = q_ps[c % 3].rearrange("p (h a d) -> p h a d", a=2, d=HD // 2)
                    tn = rot_tab[:, 2 * (c // 2) + 1, ds(t, 1), :].rearrange("p o (a d) -> p o a d", a=2)
                    nc.vector.tensor_tensor(pa[:, c, :, :], q_ps[c % 3].rearrange("p (h d) -> p h d", d=HD),
                                            rot_tab[:, 2 * (c // 2), ds(t, 1), :].broadcast_to([P, HPC, HD]), ALU.mult)
                    for half in range(2):
                        last = nc.vector.tensor_tensor(
                            pbm[:, c, :, 32 * half:32 * half + 32], ps[:, :, 1 - half, :],
                            tn[:, :, half, :].broadcast_to([P, HPC, 32]), ALU.mult)
                    last.then_inc(C["ab"].sem, 1)

            def sums(i):
                nc.vector.tensor_reduce(ss[:, :, :], sq[:, :, :, :], AX_X, ALU.add).then_inc(C["ssq"].sem, 1)
                wait(dve, "ssq", i, 1)
                nc.vector.tensor_scalar_max(ss[:, :, :], ss[:, :, :], 1e-24).then_inc(C["ssq"].sem, 1)

            def newton(i):
                wait(dve, "rexp", i, 1)
                nc.vector.tensor_tensor(nt[:, 0, :, :], r0[:, :, :], r0[:, :, :], ALU.mult).then_inc(C["newt"].sem, 1)
                wait(dve, "newt", i, 1)
                nc.vector.tensor_tensor(nt[:, 1, :, :], nt[:, 0, :, :], ss[:, :, :], ALU.mult).then_inc(C["newt"].sem, 1)
                wait(dve, "newt", i, 2)
                nc.vector.tensor_scalar(nt[:, 2, :, :], nt[:, 1, :, :], -0.5, 1.5, ALU.mult, ALU.add).then_inc(C["newt"].sem, 1)
                wait(dve, "newt", i, 3)
                wait(dve, "qn", i, 0)
                nc.vector.tensor_tensor(rn[:, :, :], nt[:, 2, :, :], r0[:, :, :], ALU.mult).then_inc(C["newt"].sem, 1)
                wait(dve, "newt", i, 4)

            def normalise(i, cs):
                for c in cs:
                    wait(dve, "rot", i, c + 1)
                    wait(dve, "tr", i, c - 3)
                    nc.vector.tensor_tensor(qkn[:, c, :, :], rot[:, c, :, :],
                                            rn[:, c, :].rearrange("p (h o) -> p h o", o=1).broadcast_to([P, HPC, HD]),
                                            ALU.mult).then_inc(C["qn"].sem, 1)

            def first(l):
                i = l * TILES
                dve.wait_ge(s_tab, l * 8 + 8)
                for t in range(2):
                    rotate(t, i + t, range(4))
                    sums(i + t)
                    newton(i + t)
                    normalise(i + t, range(4))

            def attend(l, t, i, left):
                for a in range(2):
                    h = slice(a * PAIRS, (a + 1) * PAIRS)
                    wait(dve, "s", i, a + 1)
                    nc.vector.tensor_reduce(smax[:, h], s_v[:, h, :], AX_X, ALU.max).then_inc(C["mx"].sem, 1)
                    wait(dve, "mx", i, a + 1)
                    wait(dve, "exp", i, 0)
                    nc.vector.tensor_tensor(ssub[:, h, :], s_v[:, h, :],
                                            smax[:, h].rearrange("p (h o) -> p h o", o=1).broadcast_to([P, PAIRS, 2 * WIN]),
                                            ALU.subtract).then_inc(C["sub"].sem, 1)
                for a in range(2):
                    h = slice(a * PAIRS, (a + 1) * PAIRS)
                    wait(dve, "exp", i, a + 1)
                    nc.vector.tensor_reduce(psum_[:, h], pexp[:, h, :], AX_X, ALU.add).then_inc(C["sum"].sem, 1)
                wait(dve, "sum", i, 2)
                nc.vector.reciprocal(prec[:, :], psum_[:, :]).then_inc(C["rec"].sem, 1)
                wait(dve, "rec", i, 1)
                wait(dve, "ptr", i, 0)
                nc.vector.tensor_tensor(pn[:, :, :], pexp[:, :, :],
                                        prec[:, :].rearrange("p (h o) -> p h o", o=1).broadcast_to([P, HEADS, 2 * WIN]),
                                        ALU.mult).then_inc(C["pn"].sem, 1)
                if left == 2:
                    rotate(t + 2, i + 2, range(4))
                    sums(i + 2)
                    newton(i + 2)
                    normalise(i + 2, range(4))
                wait(dve, "wo", i, 1)
                nc.vector.tensor_tensor(x_mid[:, ds(t * P + 1, P)], wo_ps, x_in[:, ds(t * P + 1, P)],
                                        ALU.add).then_inc(C["xmid"].sem, 1)

            def centre(j):
                wait(dve, "mean", j, 1)
                nc.vector.tensor_tensor(zc[:, :], zs[:, :], stat_ps, ALU.subtract).then_inc(C["zc"].sem, 1)

            def normalised(l, j):
                wait(dve, "rs", j, 1)
                nc.vector.tensor_tensor(rt[:, 0, :], rs0[:, :], rs0[:, :], ALU.mult).then_inc(C["n2"].sem, 1)
                nc.vector.tensor_tensor(rt[:, 1, :], zc[:, :], rs0[:, :], ALU.mult).then_inc(C["n2"].sem, 1)
                wait(dve, "n2", j, 1)
                nc.vector.scalar_tensor_tensor(rt[:, 2, :], stat_ps, EPS, rt[:, 0, :], ALU.add, ALU.mult
                                               ).then_inc(C["n2"].sem, 1)
                wait(dve, "n2", j, 3)
                nc.vector.scalar_tensor_tensor(xn[:, :], rt[:, 2, :], -3.0, rt[:, 1, :], ALU.add, ALU.mult
                                               ).then_inc(C["xn"].sem, 1)
                wait(dve, "xn", j, 1)
                wait(dve, "up", j, 0)
                nc.vector.tensor_scalar(xng[:, :], xn[:, :], g_half[:, ds(l, 1)], bc[:, ds(l, 1)], ALU.mult,
                                        ALU.add).then_inc(C["xng"].sem, 1)

            def statistics(l, n, j):
                centre(j)
                normalised(l, j)

            def feed(l, n, j, more):
                if more:
                    centre(j + 1)
                for c, (c0, m) in enumerate(FCH):
                    wait(dve, "gl", j, c + 1)
                    wait(dve, "dn", j, 0)
                    nc.vector.scalar_tensor_tensor(hh[0:m, c, :], value_ps[c][0:m, :], b1c[0:m, ds(l, 1), 0, c],
                                                   gl[0:m, c, :], ALU.add, ALU.mult).then_inc(C["hh"].sem, 1)
                if more:
                    normalised(l, j + 1)
                wait(dve, "dn", j, 1)
                nc.vector.scalar_tensor_tensor(x_out[:, ds(n * CH + 1, CH)], down_ps, b2c[:, ds(l, 1)],
                                               x_mid[:, ds(n * CH + 1, CH)], ALU.add, ALU.add).then_inc(C["xo"].sem, 1)

            layers(dve, first, attend, statistics, feed)

        @block.tensor
        def _(pe):
            for n in ("qkv", "tr", "s", "ptr", "pv", "wo", "mean", "varm", "up", "dn"):
                pe.sem_inc(C[n].sem, C[n].per)
            pe.wait_ge(s_zero, 6)
            pe.wait_ge(s_ready, 3)

            def project(i, cs):
                for c in cs:
                    if c == 0:
                        wait(pe, "xs", i, 2)
                    if c in (0, 3):
                        wait(pe, "ab", i, c // 3)
                    elif c in (1, 2):
                        wait(pe, "v", i, 0)
                    else:
                        wait(pe, "ab", i, c - 2)
                    nc.tensor.matmul(q_ps[c % 3], xs[:, :], wqkv[:, c * CH:(c + 1) * CH], start=True,
                                     stop=True).then_inc(C["qkv"].sem, 1)

            def turn(i, fs):
                for f in fs:
                    wait(pe, "qn", i, f + 1)
                    wait(pe, "qkT", i, f - 1)
                    for k in range(4):
                        last = nc.tensor.transpose(t_ps[f % 2][:, k, :],
                                                   qkn[:, f, 2 * k:2 * k + 2, :].rearrange("p a d -> p (a d)"), ident[:, :])
                    last.then_inc(C["tr"].sem, 1)

            def first(l):
                pe.wait_ge(s_wqkv, l * 48 + 48)
                i = l * TILES
                project(i, range(6))
                turn(i, range(4))
                pe.wait_ge(s_wo, l * 64 + 64)
                project(i + 1, range(4))

            def attend(l, t, i, left):
                wait(pe, "oc", i, 0)
                wait(pe, "qkT", i, 4)
                mt = masks[:, t:t + 1, :] if isinstance(t, int) else masks[:, ds(t, 1), :]
                for a in range(2):
                    nc.tensor.matmul(s_ps[:, a * CH:(a + 1) * CH], identb[:, :],
                                     mt.broadcast_to([P, HPC, 2 * WIN]), start=True, stop=False,
                                     skip_group_check=True)
                    for hp in range(4 * a, 4 * a + 4):
                        for j in range(WPT):
                            last = nc.tensor.matmul(
                                s_v[WIN * j:WIN * (j + 1), 2 * hp:2 * hp + 2, :], qT[:, hp, WIN * j:WIN * (j + 1)],
                                kT[:, hp, :, WIN * j:WIN * (j + 2)], start=False, stop=True, skip_group_check=True)
                    last.then_inc(C["s"].sem, 1)
                if left:
                    turn(i + 1, (0, 1))
                    project(i + 1, (4, 5))
                    turn(i + 1, (2, 3))
                if left == 2:
                    project(i + 2, (0, 1))
                wait(pe, "pn", i, 1)
                for f in range(2):
                    if left:
                        wait(pe, "qkT", i + 1, f + 3)
                    for k in range(4):
                        hp = 4 * f + k
                        last = nc.tensor.transpose(t_ps[f][:, k, :],
                                                   pn[:, 2 * hp:2 * hp + 2, :].rearrange("p a d -> p (a d)"), ident[:, :])
                    last.then_inc(C["ptr"].sem, 1)
                if left == 2:
                    project(i + 2, (2, 3))
                wait(pe, "vhalo", i, 2 * 16)
                pe.sem_inc(s_gate, 1)
                wait(pe, "vdma", i, 14 * 16)
                pe.sem_inc(s_gate, 1)
                for half in range(2):
                    wait(pe, "ptc", i, half + 1)
                    pe.sem_inc(s_gate, 1)
                    for hp in range(4 * half, 4 * half + 4):
                        g, b = divmod(hp, 2)
                        for j in range(WPT):
                            last = nc.tensor.matmul(
                                o_v[64 * b:64 * b + 64, g, :, WIN * j:WIN * (j + 1)], v_win[:, j, HD * hp:HD * (hp + 1)],
                                pT[:, hp, :, WIN * j:WIN * (j + 1)], start=True, stop=True)
                    last.then_inc(C["pv"].sem, 1)
                wait(pe, "xmid", i, 0)
                for hp in range(PAIRS):
                    if hp % 4 == 0:
                        wait(pe, "oc", i, hp // 4 + 1)
                    last = nc.tensor.matmul(wo_ps, wo[:, hp, :], oT[:, hp, :], start=hp == 0, stop=hp == PAIRS - 1)
                last.then_inc(C["wo"].sem, 1)

            def mean(j):
                wait(pe, "zs", j, 2)
                wait(pe, "xn", j, 0)
                nc.tensor.matmul(stat_ps, meanw[:, :], zs[:, :], start=True, stop=True).then_inc(C["mean"].sem, 1)

            def variance(j):
                wait(pe, "zq", j, 1)
                nc.tensor.matmul(stat_ps, meanw[:, :], zq[:, :], start=True, stop=True).then_inc(C["varm"].sem, 1)

            def statistics(l, n, j):
                pe.wait_ge(s_wffn, l * 64 + 64)
                mean(j)
                variance(j)

            def feed(l, n, j, more):
                if more:
                    mean(j + 1)
                wait(pe, "xng", j, 1)
                for c, (c0, m) in enumerate(FCH):
                    nc.tensor.matmul(gate_ps[c][0:m, :], w1[:, FF + c0:FF + c0 + m], xng[:, :], start=True, stop=True)
                    nc.tensor.matmul(value_ps[c][0:m, :], w1[:, c0:c0 + m], xng[:, :], start=True, stop=True
                                     ).then_inc(C["up"].sem, 1)
                    if more and c == 0:
                        variance(j + 1)
                wait(pe, "xo", j, 0)
                for c, (c0, m) in enumerate(FCH):
                    wait(pe, "hh", j, c + 1)
                    last = nc.tensor.matmul(down_ps, w2[0:m, c, :], hh[0:m, c, :], start=c == 0, stop=c == 2)
                last.then_inc(C["dn"].sem, 1)

            layers(pe, first, attend, statistics, feed)


def residual_layernorm(nc, tag, xT, f, out, first=0):
    ctx = ExitStack()
    with ctx:
        def sb(name, shape, dt=F32):
            return ctx.enter_context(nc.sbuf_tensor(f"{tag}_{name}", shape, dt))
        meanw = sb("meanw", [P, P])
        eps = sb("eps", [P, 1])
        s = sb("s", [P, 2, CH])
        sc = sb("sc", [P, 2, CH])
        sq = sb("sq", [P, 2, CH])
        lnv = sb("lnv", [P, 2, CH])
        r0 = sb("r0", [P, 2, CH])
        t1 = sb("t1", [P, 2, CH])
        t2 = sb("t2", [P, 2, CH])
        m_ps = [ctx.enter_context(nc.psum_tensor(f"{tag}_mean{i}", [P, CH], F32)) for i in range(2)]
        v_ps = [ctx.enter_context(nc.psum_tensor(f"{tag}_var{i}", [P, CH], F32)) for i in range(2)]
        sem = lambda n: ctx.enter_context(nc.semaphore(f"{tag}_{n}"))
        s_set, s_sum, s_mean, s_cen, s_sq, s_var, s_ln, s_r0, s_nt, s_out = (
            sem(n) for n in ("set", "sum", "mean", "centred", "squared", "variance", "ln", "r0", "newton", "out"))
        block = ctx.enter_context(nc.Block())

        @block.gpsimd
        def _(pool):
            nc.gpsimd.memset(meanw[:, :], 1.0 / DIM).then_inc(s_set, 1)
            nc.gpsimd.memset(eps[:, :], EPS).then_inc(s_set, 1)

        @block.vector
        def _(dve):
            def head(c):
                x_c = xT[:, 1 + c * CH:1 + (c + 1) * CH]
                nc.vector.tensor_tensor(s[:, c % 2, :], x_c, f[:, first + c * CH:first + (c + 1) * CH], ALU.add).then_inc(s_sum, 1)

            def centre(c):
                dve.wait_ge(s_mean, c + 1)
                if c >= 2:
                    dve.wait_ge(s_out, c - 1)
                nc.vector.tensor_tensor(sc[:, c % 2, :], s[:, c % 2, :], m_ps[c % 2][:, :], ALU.subtract).then_inc(s_cen, 1)

            head(0)
            head(1)
            centre(0)
            for c in range(CHUNKS):
                if c + 1 < CHUNKS:
                    centre(c + 1)
                dve.wait_ge(s_r0, c + 1)
                nc.vector.tensor_tensor(t1[:, c % 2, :], r0[:, c % 2, :], r0[:, c % 2, :], ALU.mult).then_inc(s_nt, 1)
                dve.wait_ge(s_nt, 4 * c + 1)
                nc.vector.scalar_tensor_tensor(t2[:, c % 2, :], v_ps[c % 2][:, :], EPS, t1[:, c % 2, :], ALU.add,
                                               ALU.mult).then_inc(s_nt, 1)
                dve.wait_ge(s_nt, 4 * c + 2)
                nc.vector.tensor_scalar(t1[:, c % 2, :], t2[:, c % 2, :], -0.5, 1.5, ALU.mult, ALU.add).then_inc(s_nt, 1)
                dve.wait_ge(s_nt, 4 * c + 3)
                nc.vector.tensor_tensor(t2[:, c % 2, :], t1[:, c % 2, :], r0[:, c % 2, :], ALU.mult).then_inc(s_nt, 1)
                if c + 2 < CHUNKS:
                    head(c + 2)
                dve.wait_ge(s_nt, 4 * c + 4)
                nc.vector.tensor_tensor(out[:, 1 + c * CH:1 + (c + 1) * CH], sc[:, c % 2, :], t2[:, c % 2, :],
                                        ALU.mult).then_inc(s_out, 1)

        @block.scalar
        def _(act):
            nc.scalar.preload_act_table_set("natural_log_exp_and_others")
            act.wait_ge(s_set, 2)

            def square(c):
                act.wait_ge(s_cen, c + 1)
                nc.scalar.activation(sq[:, c % 2, :], sc[:, c % 2, :], ACT.Square).then_inc(s_sq, 1)

            square(0)
            for c in range(CHUNKS):
                if c + 1 < CHUNKS:
                    square(c + 1)
                act.wait_ge(s_var, c + 1)
                nc.scalar.activation(lnv[:, c % 2, :], v_ps[c % 2][:, :], ACT.Ln, bias=eps[:, 0:1]).then_inc(s_ln, 1)
                act.wait_ge(s_ln, c + 1)
                if c >= 2:
                    act.wait_ge(s_nt, 4 * (c - 1))
                nc.scalar.activation(r0[:, c % 2, :], lnv[:, c % 2, :], ACT.Exp, scale=-0.5).then_inc(s_r0, 1)

        @block.tensor
        def _(pe):
            pe.wait_ge(s_set, 2)

            def mean(c):
                pe.wait_ge(s_sum, c + 1)
                if c >= 2:
                    pe.wait_ge(s_cen, c - 1)
                nc.tensor.matmul(m_ps[c % 2][:, :], meanw[:, :], s[:, c % 2, :], start=True, stop=True).then_inc(s_mean, 1)

            mean(0)
            mean(1)
            for c in range(CHUNKS):
                pe.wait_ge(s_sq, c + 1)
                if c >= 2:
                    pe.wait_ge(s_nt, 4 * (c - 2) + 2)
                nc.tensor.matmul(v_ps[c % 2][:, :], meanw[:, :], sq[:, c % 2, :], start=True, stop=True).then_inc(s_var, 1)
                if c + 2 < CHUNKS:
                    mean(c + 2)


def selective_scan(nc, xT, y, w):
    NST = w["A_log"].shape[1]
    RANK = w["W_dt"].shape[1]
    ctx = ExitStack()
    with ctx:
        def sb(name, shape, dt=F32):
            return ctx.enter_context(nc.sbuf_tensor("c_" + name, shape, dt))
        w_bc = sb("w_bc", [DIM, 2 * NST])
        w_dt = sb("w_dt", [DIM, RANK])
        w_pr = sb("w_pr", [RANK, DIM])
        b_dt = sb("b_dt", [DIM, 1])
        a_log = sb("a_log", [DIM, NST])
        a_neg = sb("a_neg", [DIM, NST])
        a_exp = sb("a_exp", [DIM, NST])
        d_par = sb("d_par", [DIM, 1])
        w_b = sb("w_b", [DIM, 2, P])
        w_c = sb("w_c", [DIM, 2, P])
        low = sb("low", [RANK, SEQ])
        z = sb("z", [DIM, SEQ])
        za = sb("za", [DIM, SEQ])
        e = sb("e", [DIM, SEQ])
        delta = sb("delta", [DIM, SEQ])
        dx = sb("dx", [DIM, SEQ])
        abar = sb("abar", [DIM, 2, SEQ])
        bx = sb("bx", [DIM, SEQ])
        h = sb("h", [DIM, SEQ])
        yc = sb("yc", [DIM, 2, SEQ])
        ps = [ctx.enter_context(nc.psum_tensor(f"c_ps{i}", [P, SEQ], F32)) for i in range(2)]
        sem = lambda n: ctx.enter_context(nc.semaphore("c_" + n))
        s_in, s_low, s_lowc, s_pr, s_z, s_e, s_l, s_dl, s_dx, s_a, s_y0, s_sp = (
            sem(n) for n in ("in", "low", "lowc", "pr", "z", "e", "l", "dl", "dx", "a", "y0", "sp"))

        class Count:
            def __init__(self, name, per):
                self.sem, self.per = ctx.enter_context(nc.semaphore("c_" + name)), per

        C = {n: Count(n, per) for n, per in dict(wcol=2, b=1, c=1, abar=1, bx=1, h=1, yc=1, acc=1).items()}

        def wait(eng, name, n, k):
            eng.wait_ge(C[name].sem, n * C[name].per + (C[name].per + k))

        block = ctx.enter_context(nc.Block())

        @block.sync
        def _(sp):
            for dst, src in ((w_bc, w["W_bc"]), (w_dt, w["W_dt"]), (w_pr, w["W_dtproj"]), (a_log, w["A_log"]),
                             (b_dt, w["b_dtproj"].rearrange("(p o) -> p o", o=1)),
                             (d_par, w["D_param"].rearrange("(p o) -> p o", o=1))):
                sp.dma_start(dst[:, :], src).then_inc(s_in, 16)

        @block.gpsimd
        def _(pool):
            pool.sem_inc(C["wcol"].sem, 2)
            pool.sem_inc(C["acc"].sem, 2)
            pool.wait_ge(s_in, 96)
            nc.gpsimd.tensor_scalar(y[:, :], xT[:, 1:1 + SEQ], d_par[:, 0:1], None, ALU.mult).then_inc(s_y0, 1)
            pool.wait_ge(s_y0, 1)
            with pool.Fori(0, NST // 2) as m:
                for par in range(2):
                    n = m * 2 + par
                    wait(pool, "b", n, 0)
                    nc.gpsimd.tensor_copy(w_b[:, par, :], w_bc[:, ds(n, 1)].broadcast_to([DIM, P])).then_inc(C["wcol"].sem, 1)
                    wait(pool, "c", n, 0)
                    nc.gpsimd.tensor_copy(w_c[:, par, :], w_bc[:, ds(n + NST, 1)].broadcast_to([DIM, P])).then_inc(C["wcol"].sem, 1)
                for par in range(2):
                    n = m * 2 + par
                    wait(pool, "yc", n, 1)
                    wait(pool, "acc", n, 1)
                    nc.gpsimd.tensor_tensor(y[:, :], y[:, :], yc[:, par, :], ALU.add).then_inc(C["acc"].sem, 1)
            wait(pool, "acc", NST, 1)

        @block.scalar
        def _(act):
            act.sem_inc(C["abar"].sem, C["abar"].per)
            nc.scalar.preload_act_table_set("natural_log_exp_and_others")
            act.wait_ge(s_in, 96)
            nc.scalar.activation(a_exp[:, :], a_log[:, :], ACT.Exp).then_inc(s_a, 1)
            act.wait_ge(s_low, 4)
            nc.scalar.copy(low[:, :], ps[0][0:RANK, :]).then_inc(s_lowc, 1)
            act.wait_ge(s_pr, 4)
            nc.scalar.activation(za[:, :], ps[1][:, :], ACT.Abs, bias=b_dt[:, 0:1]).then_inc(s_z, 1)
            act.wait_ge(s_z, 1)
            nc.scalar.activation(e[:, :], za[:, :], ACT.Exp, scale=-1.0).then_inc(s_e, 1)
            act.wait_ge(s_dl, 1)
            with act.Fori(0, NST // 2) as m:
                for par in range(2):
                    n = m * 2 + par
                    wait(act, "h", n, 0)
                    nc.scalar.activation(abar[:, par, :], delta[:, :], ACT.Exp, scale=a_neg[:, ds(n, 1)]
                                         ).then_inc(C["abar"].sem, 1)

        @block.vector
        def _(dve):
            for n in ("bx", "h", "yc"):
                dve.sem_inc(C[n].sem, C[n].per)
            dve.sem_inc(C["h"].sem, 1)
            chain = [0]

            def link(ins):
                chain[0] += 1
                ins.then_inc(s_sp, 1)
                dve.wait_ge(s_sp, chain[0])

            dve.wait_ge(s_a, 1)
            link(nc.vector.tensor_scalar(a_neg[:, :], a_exp[:, :], -1.0, None, ALU.mult))
            dve.wait_ge(s_z, 1)
            link(nc.vector.tensor_scalar(z[:, :], ps[1][:, :], b_dt[:, 0:1], 0.0, ALU.add, ALU.max))
            dve.wait_ge(s_e, 1)
            link(nc.vector.tensor_scalar(h[:, :], e[:, :], 2.0, None, ALU.add))
            link(nc.vector.reciprocal(bx[:, :], h[:, :]))
            link(nc.vector.tensor_tensor(h[:, :], e[:, :], bx[:, :], ALU.mult))
            link(nc.vector.tensor_tensor(bx[:, :], h[:, :], h[:, :], ALU.mult))
            link(nc.vector.tensor_scalar(za[:, :], bx[:, :], 2.0 / 15, 2.0 / 13, ALU.mult, ALU.add))
            for k in (11, 9, 7, 5, 3):
                link(nc.vector.tensor_tensor(dx[:, :], za[:, :], bx[:, :], ALU.mult))
                link(nc.vector.tensor_scalar(za[:, :], dx[:, :], 2.0 / k, None, ALU.add))
            link(nc.vector.tensor_tensor(dx[:, :], za[:, :], bx[:, :], ALU.mult))
            link(nc.vector.scalar_tensor_tensor(za[:, :], dx[:, :], 2.0, h[:, :], ALU.add, ALU.mult))
            nc.vector.tensor_tensor(delta[:, :], z[:, :], za[:, :], ALU.add).then_inc(s_dl, 1)
            dve.wait_ge(s_dl, 1)
            link(nc.vector.tensor_tensor(dx[:, :], delta[:, :], xT[:, 1:1 + SEQ], ALU.mult))
            dve.sem_inc(s_dx, 1)
            with dve.Fori(0, NST // 2) as m:
                for par in range(2):
                    n = m * 2 + par
                    wait(dve, "b", n, 2)
                    nc.vector.tensor_tensor(bx[:, :], dx[:, :], ps[0][:, :], ALU.mult).then_inc(C["bx"].sem, 1)
                    wait(dve, "bx", n, 1)
                    wait(dve, "abar", n, 1)
                    nc.vector.tensor_tensor_scan(h[:, :], abar[:, par, :], bx[:, :], 0.0, ALU.mult, ALU.add
                                                 ).then_inc(C["h"].sem, 1)
                    wait(dve, "h", n, 2)
                    wait(dve, "c", n, 2)
                    wait(dve, "acc", n, 0)
                    nc.vector.tensor_tensor(yc[:, par, :], h[:, :], ps[1][:, :], ALU.mult).then_inc(C["yc"].sem, 1)

        @block.tensor
        def _(pe):
            for n in ("b", "c"):
                pe.sem_inc(C[n].sem, C[n].per)
                pe.sem_inc(C[n].sem, 1)
            pe.wait_ge(s_in, 96)
            for c in range(CHUNKS):
                nc.tensor.matmul(ps[0][0:RANK, c * CH:(c + 1) * CH], w_dt[:, :], xT[:, 1 + c * CH:1 + (c + 1) * CH],
                                 start=True, stop=True).then_inc(s_low, 1)
            pe.wait_ge(s_lowc, 1)
            for c in range(CHUNKS):
                nc.tensor.matmul(ps[1][:, c * CH:(c + 1) * CH], w_pr[:, :], low[:, c * CH:(c + 1) * CH],
                                 start=True, stop=True).then_inc(s_pr, 1)
            pe.wait_ge(s_dx, 1)
            with pe.Fori(0, NST // 2) as m:
                for par in range(2):
                    n = m * 2 + par
                    for k, (name, reader, wt) in enumerate((("b", "bx", w_b), ("c", "yc", w_c))):
                        wait(pe, reader, n, 0)
                        wait(pe, "wcol", n, 1 + k)
                        for c in range(CHUNKS):
                            last = nc.tensor.matmul(ps[k][:, c * CH:(c + 1) * CH], wt[:, par, :],
                                                    xT[:, 1 + c * CH:1 + (c + 1) * CH], start=True, stop=True)
                        last.then_inc(C[name].sem, 1)


def routed_experts(nc, xT, moe, w, const):
    EXPERTS, _, HID = w["Wup"].shape
    HALF = SEQ // 2
    GROUP = 64
    GPE = SEQ // GROUP
    BUDGET = GPE * 16
    EPT = P // HID
    ETILES = EXPERTS // EPT
    GPH = GPE // 2
    outer = ExitStack()
    with outer:
        def sbo(name, shape, dt=F32):
            return outer.enter_context(nc.sbuf_tensor("d_" + name, shape, dt))
        fsn = sbo("fsn", [EXPERTS, SEQ])
        w_up = sbo("w_up", [DIM, ETILES, P])
        w_gate = sbo("w_gate", [DIM, ETILES, P])
        w_down = sbo("w_down", [P, ETILES, DIM])
        b_up = sbo("b_up", [P, ETILES])
        b_gate = sbo("b_gate", [P, ETILES])
        b_down = sbo("b_down", [EXPERTS, DIM])
        spread = sbo("spread", [EXPERTS, ETILES, P])
        s_w = outer.enter_context(nc.semaphore("d_weights"))
        NW = 10

        ctx = ExitStack()
        with ctx:
            def sb(name, shape, dt=F32):
                return ctx.enter_context(nc.sbuf_tensor("d0_" + name, shape, dt))
            ident = sb("ident", [P, P])
            w_r = sb("w_r", [DIM, EXPERTS])
            b_r = sb("b_r", [P, EXPERTS])
            pairs = sb("pairs", [P, P])
            tril = sb("tril", [P, 2, P])
            gidx = sb("gidx", [P, GPH])
            lg = sb("lg", [P, 8, 2, EXPERTS])
            mx = sb("mx", [P, 8, 2])
            sx = sb("sx", [P, 8, 2])
            rx = sb("rx", [P, 8, 2])
            sc = sb("sc", [P, HALF])
            srt = [sb(f"srt{i}", [P, HALF]) for i in range(2)]
            low = sb("low", [64, HALF])
            gsum = sb("gsum", [P, GPH])
            gsT = sb("gsT", [GPH, P])
            gall = sb("gall", [P, SEQ])
            grow = sb("grow", [TILES, P])
            gcol = sb("gcol", [P, TILES])
            cmpo = sb("cmpo", [P, SEQ])
            cmp2 = sb("cmp2", [P, P])
            cnts = sb("cnts", [P, 4, TILES])
            rank = sb("rank", [P, TILES])
            sel_ = sb("sel", [P, TILES])
            col = sb("col", [P, 16])
            one = sb("one", [P, 2, GPH])
            ends = sb("ends", [P, GPH])
            gt = sb("gt", [P, HALF])
            eq = sb("eq", [P, HALF])
            pre = sb("pre", [P, HALF])
            ones = sb("ones", [P, HALF])
            fs = sb("fs", [P, HALF])
            den = sb("den", [P, HALF])
            lg_ps = ctx.enter_context(nc.psum_tensor("d0_lgps", [P, 2, 8, EXPERTS], F32))
            sc_ps = ctx.enter_context(nc.psum_tensor("d0_scps", [P, HALF], F32))
            t_ps = ctx.enter_context(nc.psum_tensor("d0_tps", [P, CH], F32))
            n_ps = ctx.enter_context(nc.psum_tensor("d0_nps", [P, CH], F32))
            dn_ps = ctx.enter_context(nc.psum_tensor("d0_dnps", [P, HALF], F32))
            g_dram = nc.dram_tensor("d0_groups", [GPE, EXPERTS], F32).ap()
            sem = lambda n: ctx.enter_context(nc.semaphore("d0_" + n))
            (s_in, s_lg, s_dve, s_exp, s_scT, s_cp, s_flip, s_gT, s_gw, s_gr, s_rowT, s_n, s_swap, s_sum, s_set) = (
                sem(n) for n in ("in", "lg", "dve", "exp", "scT", "cp", "flip", "gT", "gw", "gr", "rowT", "n", "swap",
                                 "sum", "set"))
            marks = {}
            n_swap = [0]
            block = ctx.enter_context(nc.Block())

            @block.vector
            def _(dve):
                count = [0]

                def link(ins, mark=None):
                    count[0] += 1
                    ins.then_inc(s_dve, 1)
                    dve.wait_ge(s_dve, count[0])
                    if mark:
                        marks[mark] = count[0]

                link(nc.vector.memset(ones[:, :], 1.0))
                dve.wait_ge(s_in, 16 * 6)
                dve.wait_ge(s_lg, 1)
                for a in range(2):
                    link(nc.vector.tensor_tensor(lg[:, :, a, :], lg_ps[:, a, :, :],
                                                 b_r[:, :].rearrange("p (o e) -> p o e", o=1).broadcast_to([P, 8, EXPERTS]), ALU.add))
                link(nc.vector.tensor_reduce(mx[:, :, :], lg[:, :, :, :], AX_X, ALU.max))
                wide = lambda t: t[:, :, :].rearrange("p t (a o) -> p t a o", o=1).broadcast_to([P, 8, 2, EXPERTS])
                link(nc.vector.tensor_tensor(lg[:, :, :, :], lg[:, :, :, :], wide(mx), ALU.subtract), "shifted")
                dve.wait_ge(s_exp, 1)
                link(nc.vector.tensor_reduce(sx[:, :, :], lg[:, :, :, :], AX_X, ALU.add))
                link(nc.vector.reciprocal(rx[:, :, :], sx[:, :, :]))
                link(nc.vector.tensor_tensor(lg[:, :, :, :], lg[:, :, :, :], wide(rx), ALU.mult), "scores")
                dve.wait_ge(s_scT, 1)
                link(nc.vector.tensor_copy(sc[:, :], sc_ps[:, :]))

                cur = [sc]

                def halves(t, p, d):
                    v = t[0:p, :].rearrange("p (b s d) -> p b s d", s=2, d=d)
                    return v[:, :, 0, :], v[:, :, 1, :]

                def flip_step(size):
                    nxt = srt[0] if cur[0] is not srt[0] else srt[1]
                    d = size // 2
                    a, b = halves(cur[0], P, d)
                    oa, ob = halves(nxt, P, d)
                    nc.vector.tensor_tensor(oa, a, b[:, :, ::-1], ALU.max)
                    link(nc.vector.tensor_tensor(ob[:, :, ::-1], a, b[:, :, ::-1], ALU.min))
                    cur[0] = nxt

                def step(d):
                    nxt = srt[0] if cur[0] is not srt[0] else srt[1]
                    a, b = halves(cur[0], P, d)
                    oa, ob = halves(nxt, P, d)
                    nc.vector.tensor_tensor(oa, a, b, ALU.max)
                    link(nc.vector.tensor_tensor(ob, a, b, ALU.min))
                    cur[0] = nxt

                size = 2
                while size <= HALF:
                    flip_step(size)
                    d = size // 4
                    while d >= 1:
                        step(d)
                        d //= 2
                    size *= 2
                marks["halves"] = count[0]
                marks["halves_in"] = cur[0]
                dve.wait_ge(s_flip, 16)
                nxt = srt[0] if cur[0] is not srt[0] else srt[1]
                nc.vector.tensor_tensor(nxt[0:64, :], cur[0][0:64, :], low[:, ::-1], ALU.max)
                link(nc.vector.tensor_tensor(nxt[64:P, :], cur[0][0:64, :], low[:, ::-1], ALU.min))
                cur[0] = nxt
                d = HALF // 2
                while d >= 1:
                    step(d)
                    d //= 2
                order = cur[0][:, :].rearrange("p (g n) -> p g n", n=GROUP)
                link(nc.vector.tensor_reduce(gsum[:, :], order, AX_X, ALU.add), "gsum")
                link(nc.vector.tensor_copy(ends[:, :], order[:, :, GROUP - 1]))
                dve.wait_ge(s_gT, 1)
                link(nc.vector.tensor_copy(gsT[:, :], t_ps[0:GPH, 0:P]), "gsT")
                dve.wait_ge(s_rowT, 1)
                link(nc.vector.tensor_copy(gcol[:, :], n_ps[:, 0:TILES]))
                link(nc.vector.memset(cnts[:, :, :], 0.0))
                for c in range(TILES):
                    g = gcol[:, c:c + 1]
                    if c:
                        nc.vector.tensor_scalar(cmpo[:, 0:c * P], gall[:, 0:c * P], g, 0.0, ALU.is_ge, ALU.add,
                                                accum_out=cnts[:, 0, c:c + 1])
                    if c < TILES - 1:
                        nc.vector.tensor_scalar(cmpo[:, (c + 1) * P:], gall[:, (c + 1) * P:], g, 0.0, ALU.is_gt, ALU.add,
                                                accum_out=cnts[:, 1, c:c + 1])
                    blk = gall[:, c * P:(c + 1) * P]
                    for k, op in enumerate((ALU.is_ge, ALU.is_gt)):
                        last = nc.vector.scalar_tensor_tensor(cmpo[:, c * P:(c + 1) * P] if k == 0 else cmp2[:, :], blk, g,
                                                              tril[:, k, :], op, ALU.mult, accum_out=cnts[:, 2 + k, c:c + 1])
                        link(last)
                link(nc.vector.tensor_reduce(rank[:, :], cnts[:, :, :].rearrange("p k c -> p c k"), AX_X, ALU.add))
                link(nc.vector.tensor_scalar(sel_[:, :], rank[:, :], float(BUDGET), None, ALU.is_lt))
                link(nc.vector.tensor_reduce(col[:, 0:1], sel_[:, :], AX_X, ALU.add), "swap0")
                add = lambda o, x, y: link(nc.vector.tensor_tensor(col[:, o:o + 1], col[:, x:x + 1], col[:, y:y + 1], ALU.add))
                dve.wait_ge(s_swap, 32)
                add(2, 0, 1)
                link(nc.vector.tensor_scalar(one[:, 0, :], gidx[:, :], col[:, 2:3], None, ALU.is_equal))
                link(nc.vector.tensor_tensor(one[:, 1, :], one[:, 0, :], ends[:, :], ALU.mult))
                link(nc.vector.tensor_reduce(col[:, 3:4], one[:, 1, :], AX_X, ALU.add), "swap1")
                dve.wait_ge(s_swap, 64)
                add(5, 3, 4)
                link(nc.vector.tensor_scalar(col[:, 13:14], col[:, 2:3], 0.0, BIG, ALU.is_equal, ALU.mult))
                add(5, 5, 13)
                link(nc.vector.tensor_scalar(gt[:, :], sc[:, :], col[:, 5:6], 0.0, ALU.is_gt, ALU.add, accum_out=col[:, 6:7]))
                link(nc.vector.tensor_scalar(eq[:, :], sc[:, :], col[:, 5:6], 0.0, ALU.is_equal, ALU.add,
                                             accum_out=col[:, 10:11]), "swap2")
                link(nc.vector.tensor_tensor_scan(pre[:, :], ones[:, :], eq[:, :], 0.0, ALU.mult, ALU.add))
                dve.wait_ge(s_swap, 128)
                add(8, 6, 7)
                link(nc.vector.tensor_scalar(col[:, 14:15], col[:, 2:3], float(GROUP), None, ALU.mult))
                link(nc.vector.tensor_tensor(col[:, 9:10], col[:, 14:15], col[:, 8:9], ALU.subtract))
                link(nc.vector.tensor_tensor(col[64:P, 9:10], col[64:P, 9:10], col[64:P, 11:12], ALU.subtract))
                link(nc.vector.scalar_tensor_tensor(den[:, :], pre[:, :], col[:, 9:10], eq[:, :], ALU.is_le, ALU.mult))
                link(nc.vector.tensor_tensor(gt[:, :], gt[:, :], den[:, :], ALU.add))
                link(nc.vector.tensor_tensor(fs[:, :], sc[:, :], gt[:, :], ALU.mult), "fs")
                dve.wait_ge(s_sum, 1)
                link(nc.vector.tensor_scalar(den[:, :], dn_ps[:, :], 1e-6, None, ALU.add))
                link(nc.vector.reciprocal(eq[:, :], den[:, :]))
                for a in range(2):
                    link(nc.vector.tensor_tensor(fsn[:, a * HALF:(a + 1) * HALF], fs[64 * a:64 * a + 64, :],
                                                 eq[64 * a:64 * a + 64, :], ALU.mult))

            @block.sync
            def _(sp):
                for dst, src in ((ident, const["ident"]), (w_r, w["Wr"]),
                                 (b_r, w["br"].rearrange("(o e) -> o e", o=1).broadcast_to([P, EXPERTS])),
                                 (pairs, const["pairs"]), (gidx, const["gidx"])):
                    sp.dma_start(dst[:, :], src).then_inc(s_in, 16)
                sp.dma_start(tril[:, :, :], const["tril"]).then_inc(s_in, 16)
                for dst, src in ((w_up, "Wup"), (w_gate, "Wgate")):
                    sp.dma_start(dst[:, :, :].rearrange("d t (e h) -> d (t e) h", h=HID), w[src].rearrange("e d h -> d e h")
                                 ).then_inc(s_w, 16)
                sp.dma_start(w_down[:, :, :], w["Wdown"].rearrange("(t e) h d -> (e h) t d", e=EPT)).then_inc(s_w, 16)
                for dst, src in ((b_up, "bup"), (b_gate, "bgate")):
                    sp.dma_start(dst[:, :], w[src].rearrange("(t e) h -> (e h) t", e=EPT),
                                 allow_slow_non_contiguous=True).then_inc(s_w, 16)
                sp.dma_start(b_down[:, :], w["bdown"]).then_inc(s_w, 16)
                sp.dma_start(spread[:, :, :], const["spread"]).then_inc(s_w, 16)
                sp.wait_ge(s_dve, marks["halves"])
                sp.dma_start(low[:, :], marks["halves_in"][64:P, :]).then_inc(s_flip, 16)
                sp.wait_ge(s_dve, marks["gsT"])
                for a in range(2):
                    sp.dma_start(g_dram[GPH * a:GPH * (a + 1), :], gsT[:, 64 * a:64 * a + 64]).then_inc(s_gw, 16)
                sp.wait_ge(s_gw, 32)
                flat = g_dram.rearrange("g e -> (g e)")
                sp.dma_start(grow[:, :], flat.rearrange("(c p) -> c p", p=P)).then_inc(s_gr, 16)
                sp.dma_start(gall[:, :], flat.rearrange("(o n) -> o n", o=1).broadcast_to([P, SEQ])).then_inc(s_gr, 16)
                for mark, moves in (("swap0", ((1, 0),)), ("swap1", ((4, 3),)), ("swap2", ((7, 6), (11, 10)))):
                    sp.wait_ge(s_dve, marks[mark])
                    for o, x in moves:
                        for a in range(2):
                            sp.dma_start(col[64 * a:64 * a + 64, o:o + 1], col[64 - 64 * a:P - 64 * a, x:x + 1]).then_inc(s_swap, 16)
                sp.wait_ge(s_swap, 128)
                sp.wait_ge(s_w, 16 * 7)

            @block.scalar
            def _(act):
                act.wait_ge(s_dve, marks["shifted"])
                nc.scalar.activation(lg[:, :, :, :], lg[:, :, :, :], ACT.Exp).then_inc(s_exp, 1)

            @block.tensor
            def _(pe):
                pe.wait_ge(s_in, 16 * 6)
                for t in range(TILES):
                    last = nc.tensor.matmul(lg_ps[:, t // 8, t % 8, :], xT[:, 1 + t * P:1 + (t + 1) * P], w_r[:, :],
                                            start=True, stop=True)
                last.then_inc(s_lg, 1)
                pe.wait_ge(s_dve, marks["scores"])
                for t in range(8):
                    last = nc.tensor.transpose(sc_ps[:, t * P:(t + 1) * P], lg[:, t, :, :].rearrange("p a e -> p (a e)"), ident[:, :])
                last.then_inc(s_scT, 1)
                pe.wait_ge(s_dve, marks["gsum"])
                nc.tensor.transpose(t_ps[0:GPH, 0:P], gsum[:, :], ident[:, :]).then_inc(s_gT, 1)
                pe.wait_ge(s_gr, 32)
                nc.tensor.transpose(n_ps[:, 0:TILES], grow[:, :], ident[0:TILES, 0:TILES]).then_inc(s_rowT, 1)
                pe.wait_ge(s_dve, marks["fs"])
                for k in range(2):
                    last = nc.tensor.matmul(dn_ps[:, k * CH:(k + 1) * CH], pairs[:, :], fs[:, k * CH:(k + 1) * CH],
                                            start=True, stop=True)
                last.then_inc(s_sum, 1)

        ctx = ExitStack()
        with ctx:
            def sb(name, shape, dt=F32):
                return ctx.enter_context(nc.sbuf_tensor("d1_" + name, shape, dt))
            silu = sb("silu", [P, 2, CH])
            ug = sb("ug", [P, 2, CH])
            hid = sb("hid", [P, 2, CH])
            up_ps = [ctx.enter_context(nc.psum_tensor(f"d1_up{i}", [P, CH], F32)) for i in range(2)]
            gt_ps = [ctx.enter_context(nc.psum_tensor(f"d1_gate{i}", [P, CH], F32)) for i in range(2)]
            fs_ps = [ctx.enter_context(nc.psum_tensor(f"d1_fs{i}", [P, CH], F32)) for i in range(2)]
            o_ps = [ctx.enter_context(nc.psum_tensor(f"d1_o{i}", [P, CH], F32)) for i in range(1)]

            class Count:
                def __init__(self, name, per):
                    self.sem, self.per = ctx.enter_context(nc.semaphore("d1_" + name)), per

            s_gate = ctx.enter_context(nc.semaphore("d1_checkpoint"))
            C = {n: Count(n, per) for n, per in dict(up=ETILES, gate=ETILES, fs=ETILES, silu=ETILES, ug=ETILES, hid=ETILES,
                                                     out=1, cp=1, dn=ETILES).items()}
            block = ctx.enter_context(nc.Block())

            def wait(eng, name, c, k):
                eng.wait_ge(C[name].sem, c * C[name].per + (C[name].per + k))

            def chunks(eng, body):
                with eng.Fori(0, CHUNKS) as c:
                    body(c)

            @block.scalar
            def _(act):
                act.sem_inc(C["silu"].sem, ETILES)

                def body(c):
                    for t in range(ETILES):
                        wait(act, "up", c, t + 1)
                        wait(act, "ug", c, t - 1)
                        nc.scalar.activation(silu[:, t % 2, :], up_ps[t % 2][:, :], ACT.Silu, bias=b_up[:, t:t + 1]
                                             ).then_inc(C["silu"].sem, 1)
                chunks(act, body)

            @block.vector
            def _(dve):
                for n in ("ug", "hid", "cp"):
                    dve.sem_inc(C[n].sem, C[n].per)

                def body(c):
                    for t in range(ETILES):
                        wait(dve, "gate", c, t + 1)
                        wait(dve, "silu", c, t + 1)
                        nc.vector.scalar_tensor_tensor(ug[:, t % 2, :], gt_ps[t % 2][:, :], b_gate[:, t:t + 1],
                                                       silu[:, t % 2, :], ALU.add, ALU.mult).then_inc(C["ug"].sem, 1)
                        wait(dve, "ug", c, t + 1)
                        wait(dve, "fs", c, t + 1)
                        wait(dve, "dn", c, t - 1)
                        nc.vector.tensor_tensor(hid[:, t % 2, :], ug[:, t % 2, :], fs_ps[t % 2][:, :], ALU.mult
                                                ).then_inc(C["hid"].sem, 1)
                    wait(dve, "out", c, 1)
                    nc.vector.tensor_copy(moe[:, ds(c * CH, CH)], o_ps[0][:, :]).then_inc(C["cp"].sem, 1)
                chunks(dve, body)

            @block.tensor
            def _(pe):
                for n in ("up", "gate", "fs", "out", "dn"):
                    pe.sem_inc(C[n].sem, C[n].per)

                def down(c, t):
                    wait(pe, "hid", c, t + 1)
                    nc.tensor.matmul(o_ps[0][:, :], w_down[:, t, :], hid[:, t % 2, :], start=False, stop=t == ETILES - 1
                                     ).then_inc(C["dn"].sem, 1)

                def body(c):
                    x_c = xT[:, ds(c * CH + 1, CH)]
                    f_c = fsn[:, ds(c * CH, CH)]
                    wait(pe, "cp", c, 0)
                    pe.sem_inc(s_gate, 1)
                    nc.tensor.matmul(o_ps[0][:, :], b_down[:, :], f_c, start=True, stop=False)
                    for t in range(ETILES):
                        wait(pe, "silu", c, t - 1)
                        nc.tensor.matmul(up_ps[t % 2][:, :], w_up[:, t, :], x_c, start=True, stop=True).then_inc(C["up"].sem, 1)
                        wait(pe, "ug", c, t - 1)
                        nc.tensor.matmul(gt_ps[t % 2][:, :], w_gate[:, t, :], x_c, start=True, stop=True).then_inc(C["gate"].sem, 1)
                        wait(pe, "hid", c, t - 1)
                        pe.sem_inc(s_gate, 1)
                        nc.tensor.matmul(fs_ps[t % 2][:, :], spread[:, t, :], f_c, start=True, stop=True
                                         ).then_inc(C["fs"].sem, 1)
                        if t:
                            down(c, t - 1)
                    down(c, ETILES - 1)
                    pe.sem_inc(s_gate, 1)
                    wait(pe, "dn", c, ETILES)
                    pe.sem_inc(C["out"].sem, 1)
                chunks(pe, body)


def store(nc, xT, out, const):
    with ExitStack() as ctx:
        ident = ctx.enter_context(nc.sbuf_tensor("e_ident", [P, P], F32))
        tok = ctx.enter_context(nc.sbuf_tensor("e_tok", [P, TILES, DIM], F32))
        ps = [ctx.enter_context(nc.psum_tensor(f"e_ps{c}", [P, 4, DIM], F32)) for c in range(CHUNKS)]
        s_id, s_tr, s_tok, s_out = (ctx.enter_context(nc.semaphore("e_" + n)) for n in ("ident", "turned", "tok", "out"))
        block = ctx.enter_context(nc.Block())

        @block.sync
        def _(sp):
            sp.dma_start(ident[:, :], const["ident"]).then_inc(s_id, 16)
            for c in range(CHUNKS):
                sp.wait_ge(s_tok, c + 1)
                sp.dma_start(out[c * CH:(c + 1) * CH, :].rearrange("(t p) d -> p t d", p=P), tok[:, 4 * c:4 * c + 4, :]
                             ).then_inc(s_out, 16)
            sp.wait_ge(s_out, 16 * CHUNKS)

        @block.tensor
        def _(pe):
            pe.wait_ge(s_id, 16)
            for c in range(CHUNKS):
                for k in range(4):
                    t = 4 * c + k
                    last = nc.tensor.transpose(ps[c][:, k, :], xT[:, 1 + t * P:1 + (t + 1) * P], ident[:, :])
                last.then_inc(s_tr, 1)

        @block.vector
        def _(dve):
            for c in range(CHUNKS):
                dve.wait_ge(s_tr, c + 1)
                nc.vector.tensor_copy(tok[:, 4 * c:4 * c + 4, :], ps[c][:, :, :]).then_inc(s_tok, 1)


def program(nc, aps, const, out):
    part = lambda prefix: {n[len(prefix):]: ap for n, ap in aps.items() if n.startswith(prefix)}
    with nc.sbuf_tensor("xT", [DIM, 1 + SEQ], F32) as xT:
        with nc.sbuf_tensor("attended", [DIM, SEQ], F32) as attended:
            nc.disable_value_cache = True
            causal_attention(nc, xT, attended, part("L0_attn_"), const)
            nc.disable_value_cache = False
            residual_layernorm(nc, "ln0", xT, attended, xT)
        with nc.sbuf_tensor("x_layers", [DIM, 1 + SEQ], F32) as x_layers:
            local_layers(nc, xT, x_layers, part("L0_ffn_"), const)
            residual_layernorm(nc, "ln1", xT, x_layers, xT, first=1)
        with nc.sbuf_tensor("scanned", [DIM, SEQ], F32) as scanned:
            selective_scan(nc, xT, scanned, part("L1_attn_"))
            residual_layernorm(nc, "ln2", xT, scanned, xT)
        with nc.sbuf_tensor("expert_sum", [DIM, SEQ], F32) as expert_sum:
            routed_experts(nc, xT, expert_sum, part("L1_ffn_"), const)
            residual_layernorm(nc, "ln3", xT, expert_sum, xT)
        store(nc, xT, out, const)


def shape_constants():
    f = np.float32
    p = np.arange(P)
    c = {"ident": np.eye(P, dtype=f)}
    sel, denb = np.zeros((P, 4, P), f), np.zeros((P, P), f)
    for g in range(4):
        for j in range(4):
            for d in range(8):
                sel[8 * (4 * g + j) + d, g, 32 * j + d] = 1
            denb[32 * j + 8, 32 * j:32 * j + 32] = 1
    c["sel"], c["denb"] = sel, denb
    later = np.where(p[None, :] > p[:, None], -BIG, 0.0).astype(f)
    c["tri"] = np.stack([later, later.T], 1)
    key, query = np.arange(64), p % 32
    seen = (key[None, :] >= query[:, None]) & (key[None, :] <= query[:, None] + 32)
    masks = np.repeat(np.where(seen, 0.0, -BIG).astype(f)[:, None, :], TILES, 1)
    masks[0:32, 0, 0:32] = -BIG
    c["masks"] = masks
    half = np.arange(0, 64, 2, dtype=f)
    inv_freq = (f(1.0) / f(10000.0) ** (half / f(64))).astype(f)
    t = np.arange(SEQ, dtype=f)
    freqs = np.concatenate([t[:, None] * inv_freq[None, :]] * 2, -1).astype(f)
    base = ((half + f(0.4 * 64)) / f(1.4 * 64)).astype(f)
    power = ((t - SEQ // 2) / 16).astype(f)
    scale = np.concatenate([base[None, :] ** power[:, None]] * 2, -1).astype(f)
    sign = np.concatenate([-np.ones(32, f), np.ones(32, f)])
    cos, sin = np.cos(freqs), np.sin(freqs) * sign
    rot = np.stack([cos * scale, sin * scale, cos * (f(1) / scale), sin * (f(1) / scale)]).astype(f)
    c["rot"] = rot.reshape(4, TILES, P, 64).transpose(2, 0, 1, 3)
    c["pairs"] = (p[:, None] // 64 == p[None, :] // 64).astype(f)
    c["tril"] = np.stack([p[None, :] < p[:, None], p[None, :] >= p[:, None]], 1).astype(f)
    c["gidx"] = (1 + 16 * (p // 64)[:, None] + np.arange(16)[None, :]).astype(f)
    spread = np.zeros((64, 16, P), f)
    for e in range(64):
        spread[e, e // 4, 32 * (e % 4):32 * (e % 4) + 32] = 1
    c["spread"] = spread
    return {n: np.ascontiguousarray(a) for n, a in c.items()}


def kernel(**inputs):
    import concourse.bacc as bacc
    from concourse.bass_utils import run_bass_kernel_spmd

    nc = bacc.Bacc("TRN2", target_bir_lowering=False, num_devices=1)
    arrays, aps, const = {}, {}, {}
    for name, value in inputs.items():
        a = np.ascontiguousarray(value)
        arrays["in_" + name] = a
        aps[name] = nc.dram_tensor("in_" + name, a.shape, mybir.dt.from_np(a.dtype), kind="ExternalInput").ap()
    for name, a in shape_constants().items():
        arrays["const_" + name] = a
        const[name] = nc.dram_tensor("const_" + name, a.shape, mybir.dt.from_np(a.dtype), kind="ExternalInput").ap()
    out = nc.dram_tensor("out", [SEQ, DIM], F32, kind="ExternalOutput").ap()
    program(nc, aps, const, out)
    r = run_bass_kernel_spmd(nc, [arrays], core_ids=[0])
    return r.results[0]["out"].reshape(1, SEQ, DIM)
```

```python
import numpy as np
from contextlib import ExitStack
import concourse.bass as bass
from concourse import mybir

F32 = mybir.dt.float32
BF16 = mybir.dt.bfloat16
ALU = mybir.AluOpType
ACT = mybir.ActivationFunctionType
AX_X = mybir.AxisListType.X
ds = bass.ds

P = 128
SEQ = 2048
DIM = 128
TILES = SEQ // P
CH = 512
CHUNKS = SEQ // CH
EPS = 1e-5
BIG = 1e30


def semaphores(nc, ctx):
    given = []

    def give(name):
        given.append(nc.alloc_semaphore(name=name))
        return given[-1]

    def clear():
        nc.clear_and_free_semaphores(given)
        nc.all_engine_barrier()

    ctx.callback(clear)
    return give


def causal_attention(nc, xT, att, w, const):
    HEADS, HD = 16, 8
    GROUPS = 4
    GH = HEADS // GROUPS
    SLOT = 32
    Q_PARTS = (0, 0, 1, 0, 1, 2)
    K_PARTS = (0, 1, 0, 2, 1, 0)
    SPLIT_ROWS = HD * len(Q_PARTS)
    outer = ExitStack()
    with outer:
        def sbo(name, shape, dt=F32):
            return outer.enter_context(nc.sbuf_tensor("a_" + name, shape, dt))
        qa = sbo("qa", [P, HEADS, SEQ], BF16)
        ka = sbo("ka", [P, HEADS, SEQ], BF16)
        v_all = sbo("v_all", [P, TILES, DIM])
        wo_pad = sbo("wo_pad", [P, GROUPS, DIM])
        ident = sbo("ident", [P, P])
        identb = sbo("identb", [P, P], BF16)
        tri = sbo("tri", [P, 2, P], BF16)
        denb = sbo("denb", [P, P])
        eb = sbo("eb", [P, GROUPS])
        loaded = [outer.enter_context(nc.semaphore(f"a_group_loaded{g}")) for g in range(GROUPS)]

        ctx = ExitStack()
        with ctx:
            def sb(name, shape, dt=F32):
                return ctx.enter_context(nc.sbuf_tensor("a0_" + name, shape, dt))
            xtok = sb("xtok", [P, 4, DIM])
            wraw = sb("wraw", [P, 4, DIM])
            wT = sb("wT", [P, 4, DIM])
            sel = sb("sel", [P, GROUPS, P])
            tri_in = sb("tri_in", [P, 2, P])
            bo = sb("bo", [P, 1])
            part = sb("part", [P, 2, 3, SEQ // 2], BF16)
            rest = sb("rest", [P, 2, CH])
            ps = [ctx.enter_context(nc.psum_tensor(f"a0_ps{i}", [P, 4, P], F32)) for i in range(4)]
            KA_POOL = 8
            scratch = nc.dram_tensor("a0_parts", [2, 3, DIM, SEQ], BF16).ap()
            sem = lambda n: ctx.enter_context(nc.semaphore("a0_" + n))
            s_in, s_x, s_zero, s_pe, s_act, s_dve, s_part, s_store, s_xfree, s_kset = (
                sem(n) for n in ("in", "x", "zero", "pe", "act", "dve", "part", "store", "xfree", "kset"))
            block = ctx.enter_context(nc.Block())

            def load_parts(sp, g):
                for s, (dst, parts) in enumerate(((qa, Q_PARTS), (ka, K_PARTS))):
                    for r, k in enumerate(parts):
                        sp.dma_start(dst[HD * r:HD * (r + 1), GH * g:GH * (g + 1), :],
                                     scratch[s, k, GH * HD * g:GH * HD * (g + 1), :].rearrange("(h r) n -> r h n", r=HD)
                                     ).then_inc(loaded[g], 16)

            @block.sync
            def _(sp):
                for j, n in enumerate(("Wq", "Wk", "Wv", "Wo")):
                    sp.dma_start(wraw[:, j, :], w[n]).then_inc(s_in, 16)
                sp.dma_start(ident[:, :], const["ident"]).then_inc(s_in, 16)
                sp.dma_start(sel[:, :, :], const["sel"]).then_inc(s_in, 16)
                sp.dma_start(tri_in[:, :, :], const["tri"]).then_inc(s_in, 16)
                sp.dma_start(denb[:, :], const["denb"]).then_inc(s_in, 16)
                sp.dma_start(bo[:, :], w["bo"].rearrange("(p o) -> p o", o=1)).then_inc(s_in, 16)
                for j in range(GH):
                    sp.dma_start(eb[SLOT * j:SLOT * (j + 1), :],
                                 w["denom_bias"].rearrange("o (g j) a b -> (o a b) j g", j=GH)[:, j, :].broadcast_to([SLOT, GROUPS]),
                                 allow_slow_non_contiguous=True).then_inc(s_in, 16)
                for c in range(4):
                    if c:
                        sp.wait_ge(s_xfree, c)
                    sp.dma_start(xtok[:, :, :], w["x"][0, c * CH:(c + 1) * CH, :].rearrange("(t p) d -> p t d", p=P)
                                 ).then_inc(s_x, 16)
                for half in range(2):
                    for s in range(2):
                        sp.wait_ge(s_part, 4 * half + 2 * s + 2)
                        sp.dma_start(scratch[s, :, :, half * 1024:(half + 1) * 1024].rearrange("k p n -> p k n"),
                                     part[:, s, :, :]).then_inc(s_store, 16)
                sp.wait_ge(s_store, 64)
                sp.wait_ge(s_zero, 3)
                sp.wait_ge(s_kset, 1)
                load_parts(sp, 0)

            @block.gpsimd
            def _(pool):
                nc.gpsimd.memset(xT[:, 0:1], 0.0).then_inc(s_zero, 1)
                nc.gpsimd.memset(qa[:, :, :], 0.0).then_inc(s_zero, 1)
                nc.gpsimd.memset(ka[:, 0:KA_POOL, :], -1.0).then_inc(s_zero, 1)

            @block.scalar
            def _(act):
                act.wait_ge(s_in, 13 * 16)
                nc.scalar.activation(eb[:, :], eb[:, :], ACT.Exp).then_inc(s_act, 1)
                for c in range(4):
                    act.wait_ge(s_pe, c + 1)
                    nc.scalar.copy(xT[:, 1 + c * CH:1 + (c + 1) * CH], ps[c][:, :, :].rearrange("p t d -> p (t d)")).then_inc(s_act, 1)
                act.wait_ge(s_pe, 5)
                nc.scalar.copy(wT[:, :, :], ps[0][:, :, :]).then_inc(s_act, 1)
                act.wait_ge(s_pe, 6)
                nc.scalar.copy(wo_pad[:, :, :], ps[1][:, :, :]).then_inc(s_act, 1)
                for c in range(4):
                    act.wait_ge(s_pe, 7 + c)
                    nc.scalar.copy(v_all[:, 4 * c:4 * c + 4, :], ps[c][:, :, :]).then_inc(s_act, 1)
                for n in range(8):
                    half, s, k = n // 4, (n // 2) % 2, n % 2
                    act.wait_ge(s_pe, 11 + n)
                    if half:
                        act.wait_ge(s_store, 32)
                    dst = part[:, s, :, k * CH:(k + 1) * CH]
                    nc.scalar.copy(dst[:, 0, :], ps[n % 4][:, :, :].rearrange("p t d -> p (t d)")).then_inc(s_act, 1)
                    act.wait_ge(s_dve, 2 * n + 2)
                    nc.scalar.copy(dst[:, 1, :], rest[:, n % 2, :]).then_inc(s_act, 1)

            @block.vector
            def _(dve):
                nc.vector.memset(ka[:, KA_POOL:, :], -1.0).then_inc(s_kset, 1)
                dve.wait_ge(s_in, 13 * 16)
                nc.vector.tensor_copy(tri[:, :, :], tri_in[:, :, :])
                nc.vector.tensor_copy(identb[:, :], ident[:, :]).then_inc(s_dve, 1)
                for n in range(8):
                    half, s, k = n // 4, (n // 2) % 2, n % 2
                    dst = part[:, s, :, k * CH:(k + 1) * CH]
                    dve.wait_ge(s_act, 11 + 2 * n + 1)
                    nc.vector.tensor_tensor(rest[:, n % 2, :], ps[n % 4][:, :, :].rearrange("p t d -> p (t d)"), dst[:, 0, :],
                                            ALU.subtract).then_inc(s_dve, 1)
                    dve.wait_ge(s_act, 11 + 2 * n + 2)
                    nc.vector.tensor_tensor(dst[:, 2, :], rest[:, n % 2, :], dst[:, 1, :], ALU.subtract).then_inc(s_dve, 1)
                    dve.wait_ge(s_dve, 2 * n + 3)
                    dve.sem_inc(s_part, 1)

            @block.tensor
            def _(pe):
                pe.wait_ge(s_in, 13 * 16)
                for c in range(4):
                    pe.wait_ge(s_x, 16 * (c + 1))
                    for k in range(4):
                        last = nc.tensor.transpose(ps[c][:, k, :], xtok[:, k, :], ident[:, :])
                    last.then_inc(s_pe, 1)
                    pe.wait_ge(s_pe, c + 1)
                    pe.sem_inc(s_xfree, 1)
                pe.wait_ge(s_act, 2)
                for k in range(4):
                    last = nc.tensor.transpose(ps[0][:, k, :], wraw[:, k, :], ident[:, :])
                last.then_inc(s_pe, 1)
                pe.wait_ge(s_act, 6)
                for g in range(GROUPS):
                    last = nc.tensor.matmul(ps[1][:, g, :], sel[:, g, :], wT[:, 3, :], start=True, stop=True)
                last.then_inc(s_pe, 1)
                pe.wait_ge(s_act, 7)
                for c in range(4):
                    for k in range(4):
                        t = 4 * c + k
                        last = nc.tensor.matmul(ps[c][:, k, :], xT[:, 1 + t * P:1 + (t + 1) * P], wT[:, 2, :], start=True, stop=True)
                    last.then_inc(s_pe, 1)
                for n in range(8):
                    half, s, k = n // 4, (n // 2) % 2, n % 2
                    if n < 4:
                        pe.wait_ge(s_act, 8 + n)
                    else:
                        pe.wait_ge(s_dve, 1 + 2 * (n - 4) + 1)
                    c0 = 1 + half * 1024 + k * CH
                    nc.tensor.matmul(ps[n % 4][:, :, :].rearrange("p t d -> p (t d)"), wT[:, s, :], xT[:, c0:c0 + CH],
                                     start=True, stop=True).then_inc(s_pe, 1)

        ctx = ExitStack()
        with ctx:
            def sb(name, shape, dt=F32):
                return ctx.enter_context(nc.sbuf_tensor("a1_" + name, shape, dt))
            bo = sb("bo", [P, 1])
            v_grp = sb("v_grp", [P, TILES, GH, SLOT])
            wo_grp = sb("wo_grp", [P, DIM])
            mpart = sb("mpart", [P, 2, TILES, CHUNKS])
            mrow = sb("mrow", [P, TILES])
            msp = sb("msp", [P, 3, TILES])
            mspb = sb("mspb", [P, 3, TILES], BF16)
            mr = sb("mr", [P, 2, TILES])
            mT = sb("mT", [3 * TILES, P], BF16)
            prob = sb("prob", [P, 2, GH, CH])
            acc = sb("acc", [P, CH])
            log_den = sb("log_den", [P, CH])
            rec = sb("rec", [P, CH])
            rec_part = sb("rec_part", [P, 2, CH])
            onrm = sb("onrm", [P, CH])
            st_ps = [ctx.enter_context(nc.psum_tensor(f"a1_st{i}", [P, 2, CH], F32)) for i in range(2)]
            mx_ps = [ctx.enter_context(nc.psum_tensor(f"a1_mx{i}", [P, CH], F32)) for i in range(2)]
            acc_ps = ctx.enter_context(nc.psum_tensor("a1_accps", [P, CH], F32))
            x_ps = ctx.enter_context(nc.psum_tensor("a1_xps", [P, CH], F32))

            STEPS = [(c, kt) for c in range(CHUNKS) for kt in range(4 * c + 4)]
            UNITS = [(j, qt, kc) for j in range(GH) for qt in range(TILES) for kc in range(qt // 4 + 1)]
            NS, NU = len(STEPS), len(UNITS)
            PER = NU // NS
            HEAD_UNITS = NU // GH
            LAST = [4, 12, 24, 40]

            class Count:
                def __init__(self, name, per):
                    self.sem, self.per = ctx.enter_context(nc.semaphore("a1_" + name)), per

            C = {n: Count(n, per) for n, per in dict(st=2 * NS, ex=2 * NS, pv=NS, un=NU, red=NU, mrow=2 * GH, msp=6 * GH,
                                                     mt=GH, mtc=GH, mdma=48 * GH, vg=1, wg=1, ev=4, dn=4, lg=8, rc=8, on=4, wo=4,
                                                     ac=4).items()}
            s_set = ctx.enter_context(nc.semaphore("a1_values_set"))
            s_att = ctx.enter_context(nc.semaphore("a1_att"))
            s_gate = ctx.enter_context(nc.semaphore("a1_gate"))
            s_bo = ctx.enter_context(nc.semaphore("a1_bo"))

            def wait(eng, name, g, k):
                eng.wait_ge(C[name].sem, g * C[name].per + (C[name].per + k))

            def schedule(do1, do2):
                for s in range(NS + 6):
                    units = range(PER * s, PER * (s + 1)) if do1 and s < NS else ()
                    for jp in range(2):
                        if do2 and s < NS:
                            yield "scores", (s, jp)
                        for u in units[jp:jp + 1]:
                            yield "unit", u
                    if do2 and 1 <= s <= NS:
                        yield "values", s - 1
                    for u in units[2:]:
                        yield "unit", u
                    if do1 and s % 10 == 9 and s < NS:
                        yield "rowmax", s // 10
                    if do2 and s in LAST:
                        yield "evacuate", LAST.index(s)
                    if do2 and s - 2 in LAST:
                        yield "denominator", LAST.index(s - 2)
                    if do2 and s - 4 in LAST:
                        yield "project", LAST.index(s - 4)
                    if do1 and s in (11, 21, 31, 41):
                        yield "maxima", s // 10 - 1

            def run(eng, do):
                def g_body(g, do1, do2):
                    for what, arg in schedule(do1, do2):
                        if what in do:
                            do[what](g + 1 if what in ("unit", "maxima", "rowmax") else g, arg, do1 and do2)
                if "start1" in do:
                    do["start1"](0)
                for what, arg in schedule(True, False):
                    if what in do:
                        do[what](0, arg, False)
                if "other_groups" in do:
                    do["other_groups"]()
                with eng.Fori(0, GROUPS - 1) as g:
                    if "start2" in do:
                        do["start2"](g)
                    g_body(g, True, True)
                if "start2" in do:
                    do["start2"](GROUPS - 1)
                g_body(GROUPS - 1, False, True)

            block = ctx.enter_context(nc.Block())

            @block.sync
            def _(sp):
                sp.sem_inc(C["mdma"].sem, C["mdma"].per)
                sp.dma_start(bo[:, :], w["bo"].rearrange("(p o) -> p o", o=1)).then_inc(s_bo, 16)
                for g in range(1, GROUPS):
                    load_parts(sp, g)

                def maxima(g, j, both):
                    wait(sp, "mtc", g, j + 1)
                    for s in range(3):
                        sp.dma_start(qa[SPLIT_ROWS + s:SPLIT_ROWS + s + 1, ds(g * GH + j, 1), :].rearrange("o h (t p) -> o (h t) p", p=P),
                                     mT[TILES * s:TILES * (s + 1), :]).then_inc(C["mdma"].sem, 16)

                run(sp, {"maxima": maxima})
                wait(sp, "mdma", GROUPS, 0)

            @block.gpsimd
            def _(pool):
                for n in ("vg", "wg"):
                    pool.sem_inc(C[n].sem, C[n].per)
                nc.gpsimd.memset(v_grp[:, :, :, :], 0.0).then_inc(s_set, 1)
                pool.wait_ge(s_set, 1)
                nc.gpsimd.memset(v_grp[:, :, :, HD:HD + 1], 1.0).then_inc(s_set, 1)
                pool.wait_ge(s_set, 2)

                def start2(g):
                    wait(pool, "pv", g, 0)
                    nc.gpsimd.tensor_copy(v_grp[:, :, :, 0:HD],
                                          v_all[:, :, ds(g * GH * HD, GH * HD)].rearrange("p t (h d) -> p t h d", d=HD)
                                          ).then_inc(C["vg"].sem, 1)
                    wait(pool, "wo", g, 0)
                    nc.gpsimd.tensor_copy(wo_grp[:, :], wo_pad[:, ds(g, 1), :].rearrange("p o d -> p (o d)")
                                          ).then_inc(C["wg"].sem, 1)

                run(pool, {"start2": start2})

            @block.scalar
            def _(act):
                for n in ("ex", "lg"):
                    act.sem_inc(C[n].sem, C[n].per)
                nc.scalar.preload_act_table_set("natural_log_exp_and_others")

                def scores(g, arg, both):
                    s, jp = arg
                    c, kt = STEPS[s]
                    off = max(0, kt * P - c * CH)
                    wait(act, "st", g, 2 * s + jp + 1)
                    wait(act, "pv", g, s - 1)
                    nc.scalar.activation(prob[:, s % 2, 2 * jp:2 * jp + 2, off:CH], st_ps[jp][:, :, off:CH], ACT.Exp,
                                         scale=HD ** -0.5).then_inc(C["ex"].sem, 1)

                def denominator(g, c, both):
                    wait(act, "dn", g, c + 1)
                    nc.scalar.activation(log_den[:, :], x_ps[:, :], ACT.Ln,
                                         bias=eb[:, g:g + 1] if isinstance(g, int) else eb[:, ds(g, 1)]).then_inc(C["lg"].sem, 1)
                    wait(act, "lg", g, 2 * c + 1)
                    nc.scalar.activation(rec[:, :], log_den[:, :], ACT.Exp, scale=-1.0).then_inc(C["lg"].sem, 1)

                run(act, {"scores": scores, "denominator": denominator})

            @block.vector
            def _(dve):
                for n in ("red", "mrow", "msp", "mtc", "ev", "rc", "on", "ac"):
                    dve.sem_inc(C[n].sem, C[n].per)
                dve.wait_ge(s_bo, 16)
                nc.vector.memset(att[:, :], 0.0).then_inc(s_att, 1)
                dve.wait_ge(s_att, 1)

                def unit(g, u, both):
                    j, qt, kc = UNITS[u]
                    n = min(CH, (qt + 1) * P - kc * CH)
                    wait(dve, "un", g, u + 1)
                    nc.vector.tensor_reduce(mpart[:, j % 2, qt, kc:kc + 1], mx_ps[u % 2][:, 0:n], AX_X, ALU.max).then_inc(C["red"].sem, 1)

                def rowmax(g, j, both):
                    wait(dve, "red", g, HEAD_UNITS * (j + 1))
                    for c in range(CHUNKS):
                        last = nc.vector.tensor_reduce(mrow[:, 4 * c:4 * c + 4], mpart[:, j % 2, 4 * c:4 * c + 4, 0:c + 1], AX_X, ALU.max)
                    last.then_inc(C["mrow"].sem, 2)

                def maxima(g, j, both):
                    wait(dve, "mrow", g, 2 * j + 2)
                    k = [6 * j]

                    def step(ins):
                        k[0] += 1
                        ins.then_inc(C["msp"].sem, 1)
                        wait(dve, "msp", g, k[0])
                    wait(dve, "mt", g, j)
                    step(nc.vector.tensor_copy(mspb[:, 0, :], mrow[:, :]))
                    step(nc.vector.tensor_tensor(mr[:, 0, :], mrow[:, :], mspb[:, 0, :], ALU.subtract))
                    step(nc.vector.tensor_copy(mspb[:, 1, :], mr[:, 0, :]))
                    step(nc.vector.tensor_tensor(mr[:, 1, :], mr[:, 0, :], mspb[:, 1, :], ALU.subtract))
                    step(nc.vector.tensor_copy(mspb[:, 2, :], mr[:, 1, :]))
                    step(nc.vector.tensor_copy(msp[:, :, :], mspb[:, :, :]))
                    wait(dve, "mt", g, j + 1)
                    wait(dve, "mdma", g, 48 * j)
                    nc.vector.tensor_copy(mT[:, :], x_ps[0:3 * TILES, 0:P]).then_inc(C["mtc"].sem, 1)

                def evacuate(g, c, both):
                    wait(dve, "pv", g, LAST[c])
                    wait(dve, "wo", g, c)
                    nc.vector.tensor_copy(acc[:, :], acc_ps[:, :]).then_inc(C["ev"].sem, 1)

                def denominator(g, c, both):
                    wait(dve, "lg", g, 2 * c + 2)
                    nc.vector.scalar_tensor_tensor(rec_part[:, 0, :], x_ps[:, :],
                                                   eb[:, g:g + 1] if isinstance(g, int) else eb[:, ds(g, 1)], rec[:, :],
                                                   ALU.add, ALU.mult).then_inc(C["rc"].sem, 1)
                    wait(dve, "rc", g, 2 * c + 1)
                    nc.vector.scalar_tensor_tensor(rec_part[:, 1, :], rec_part[:, 0, :], -2.0, rec[:, :], ALU.add, ALU.mult
                                                   ).then_inc(C["rc"].sem, 1)
                    wait(dve, "rc", g, 2 * c + 2)
                    nc.vector.scalar_tensor_tensor(onrm[:, :], acc[:, :], -1.0, rec_part[:, 1, :], ALU.mult, ALU.mult
                                                   ).then_inc(C["on"].sem, 1)

                def project(g, c, both):
                    wait(dve, "wo", g, c + 1)
                    nc.vector.tensor_tensor(att[:, c * CH:(c + 1) * CH], x_ps[:, :], att[:, c * CH:(c + 1) * CH],
                                            ALU.add).then_inc(C["ac"].sem, 1)

                run(dve, {"unit": unit, "rowmax": rowmax, "maxima": maxima, "evacuate": evacuate, "denominator": denominator,
                          "project": project})
                wait(dve, "ac", GROUPS, 0)
                nc.vector.tensor_scalar(att[:, :], att[:, :], bo[:, 0:1], None, ALU.add).then_inc(s_att, 1)

            @block.tensor
            def _(pe):
                for n in ("st", "pv", "un", "mt", "dn", "wo"):
                    pe.sem_inc(C[n].sem, C[n].per)
                pe.wait_ge(s_set, 2)
                pe.wait_ge(loaded[0], 12 * 16)

                def other_groups():
                    for g in range(1, GROUPS):
                        pe.wait_ge(loaded[g], 12 * 16)
                    pe.sem_inc(s_gate, 1)

                def head(g, j):
                    return g * GH + j

                def unit(g, u, both):
                    j, qt, kc = UNITS[u]
                    n = min(CH, (qt + 1) * P - kc * CH)
                    diag = kc == qt // 4
                    wait(pe, "red", g, u - 1)
                    last = nc.tensor.matmul(mx_ps[u % 2][:, 0:n],
                                            qa[:, ds(head(g, j), 1), qt * P:(qt + 1) * P].rearrange("p o n -> p (o n)"),
                                            ka[:, ds(head(g, j), 1), kc * CH:kc * CH + n].rearrange("p o n -> p (o n)"),
                                            start=True, stop=not diag)
                    if diag:
                        last = nc.tensor.matmul(mx_ps[u % 2][:, n - P:n], identb[:, :], tri[:, 0, :], start=False, stop=True)
                    last.then_inc(C["un"].sem, 1)

                def scores(g, arg, both):
                    s, jp = arg
                    c, kt = STEPS[s]
                    off = max(0, kt * P - c * CH)
                    diag = kt >= 4 * c
                    if s == 0:
                        wait(pe, "mdma", g, 48 * GH)
                    wait(pe, "ex", g, 2 * s + jp - 1)
                    for k in range(2):
                        h = head(g, 2 * jp + k)
                        last = nc.tensor.matmul(st_ps[jp][:, k, off:CH],
                                                ka[:, ds(h, 1), kt * P:(kt + 1) * P].rearrange("p o n -> p (o n)"),
                                                qa[:, ds(h, 1), c * CH + off:(c + 1) * CH].rearrange("p o n -> p (o n)"),
                                                start=True, stop=not diag)
                        if diag:
                            last = nc.tensor.matmul(st_ps[jp][:, k, off:off + P], identb[:, :], tri[:, 1, :], start=False, stop=True)
                    last.then_inc(C["st"].sem, 1)

                def values(g, s, both):
                    c, kt = STEPS[s]
                    off = max(0, kt * P - c * CH)
                    if s == 0:
                        wait(pe, "vg", g, 1)
                    if kt == 0:
                        wait(pe, "ev", g, c)
                    wait(pe, "ex", g, 2 * s + 2)
                    pe.sem_inc(s_gate, 1)
                    for j in range(GH):
                        last = nc.tensor.matmul(acc_ps[SLOT * j:SLOT * (j + 1), off:CH], v_grp[:, kt, j, :],
                                                prob[:, s % 2, j, off:CH], start=kt == 0, stop=kt == 4 * c + 3)
                    last.then_inc(C["pv"].sem, 1)

                def denominator(g, c, both):
                    wait(pe, "ev", g, c + 1)
                    wait(pe, "ac", g, c)
                    if both:
                        wait(pe, "mtc", g + 1, (0, 1, 2, 4)[c])
                    else:
                        wait(pe, "mtc", g, GH)
                    nc.tensor.matmul(x_ps[:, :], denb[:, :], acc[:, :], start=True, stop=True).then_inc(C["dn"].sem, 1)

                def project(g, c, both):
                    wait(pe, "wg", g, 1)
                    wait(pe, "on", g, c + 1)
                    nc.tensor.matmul(x_ps[:, :], wo_grp[:, :], onrm[:, :], start=True, stop=True).then_inc(C["wo"].sem, 1)

                def maxima(g, j, both):
                    wait(pe, "msp", g, 6 * j + 6)
                    wait(pe, "mtc", g, j)
                    if both:
                        wait(pe, "ac", g - 1, min(j + 1, 3))
                    pe.sem_inc(s_gate, 1)
                    nc.tensor.transpose(x_ps[0:3 * TILES, 0:P], msp[:, :, :].rearrange("p s t -> p (s t)"), ident[:, :]
                                        ).then_inc(C["mt"].sem, 1)

                run(pe, {"other_groups": other_groups, "unit": unit, "scores": scores, "values": values, "denominator": denominator,
                         "project": project, "maxima": maxima})


def local_layers(nc, xT, x_in, w, const):
    x_out = x_in
    DEPTH, _, QKV = w["Wqkv"].shape
    HEADS, HD, WIN = 16, 64, 32
    INNER = HEADS * HD
    PAIRS = HEADS // 2
    WPT = P // WIN
    FF = w["W2"].shape[1]
    FCH = [(0, 128), (128, 128), (256, FF - 256)]
    CH = 512
    CHUNKS = SEQ // CH
    HPC = CH // HD
    ctx = ExitStack()
    with ctx:
        new_semaphore = semaphores(nc, ctx)

        def sb(name, shape, dt=F32):
            return ctx.enter_context(nc.sbuf_tensor("b_" + name, shape, dt))

        def pb(name, shape):
            return ctx.enter_context(nc.psum_tensor("b_" + name, shape, F32))

        class Count:
            def __init__(self, name, per):
                self.sem, self.per = new_semaphore("b_" + name), per

            def at(self, i, k):
                return i * self.per + (self.per + k)

        x_mid = sb("x_mid", [DIM, 1 + SEQ])
        wqkv = sb("wqkv", [DIM, QKV])
        wo = sb("wo", [P, PAIRS, DIM])
        w1 = sb("w1", [DIM, 2 * FF])
        w2 = sb("w2", [P, 3, DIM])
        rot_raw = sb("rot_raw", [P, 4, TILES, HD])
        rot_tab = sb("rot_tab", [P, 4, TILES, HD])
        qk_scale = sb("qk_scale", [P, 2, DEPTH, HD])
        b1c = sb("b1c", [P, DEPTH, 2, 3])
        b2c = sb("b2c", [DIM, DEPTH])
        gc = sb("gc", [DIM, DEPTH])
        bc = sb("bc", [DIM, DEPTH])
        ident = sb("ident", [P, P])
        identb = sb("identb", [P, P], BF16)
        meanw = sb("meanw", [P, P])
        masks = sb("masks", [P, TILES, 2 * WIN], BF16)
        xs = sb("xs", [DIM, P])
        sq = sb("sq", [P, 4, HPC, HD])
        masks_in = sq[:, 0:2, :, :].rearrange("p c h d -> p (c h) d")
        pa = sb("pa", [P, 4, HPC, HD])
        pbm = sb("pbm", [P, 4, HPC, HD])
        rot = sb("rot", [P, 4, HPC, HD])
        qkn = sb("qkn", [P, 4, HPC, HD])
        ln_shift = sb("ln_shift", [P, 1])
        ss = sb("ss", [P, 4, HPC])
        lnss = sb("lnss", [P, 4, HPC])
        r0 = sb("r0", [P, 4, HPC])
        nt = sb("nt", [P, 3, 4, HPC])
        rn = sb("rn", [P, 4, HPC])
        v_tok = sb("v_tok", [P, 2, INNER])
        v_win = sb("v_win", [P, WPT, INNER // 2])
        qT = sb("qT", [P, PAIRS, P])
        kT = sb("kT", [P, PAIRS, 2, WIN + P])
        smax = sb("smax", [P, HEADS])
        ssub = sb("ssub", [P, HEADS, 2 * WIN])
        pexp = sb("pexp", [P, HEADS, 2 * WIN])
        psum_ = sb("psum_", [P, HEADS])
        prec = sb("prec", [P, HEADS])
        pn = sb("pn", [P, HEADS, 2 * WIN])
        pT = sb("pT", [P, PAIRS, 2, P])
        oT = sb("oT", [P, PAIRS, P])
        zc = sb("zc", [DIM, CH])
        zq = sb("zq", [DIM, CH])
        lnv = sb("lnv", [DIM, CH])
        rs0 = sb("rs0", [DIM, CH])
        rt = sb("rt", [DIM, 3, CH])
        zs = sb("zs", [DIM, CH])
        xn = sb("xn", [DIM, CH])
        xng = sb("xng", [DIM, CH])
        gl, hh = (t[:, 0:3, :, :].rearrange("p c h d -> p c (h d)") for t in (pa, pbm))
        g_half = sb("g_half", [DIM, DEPTH])
        eps_col = sb("eps_col", [DIM, 1])

        banks = pb("banks", [P, 8, CH])
        q_ps = [banks[:, b, :] for b in (0, 1, 2)]
        t_ps = [banks[:, b, :].rearrange("p (k n) -> p k n", k=4) for b in (3, 4)]
        s_ps = banks[:, 5:7, :].rearrange("p b n -> p (b n)")
        wo_ps = banks[:, 7, 0:P]
        value_ps, gate_ps = [banks[:, b, :] for b in (1, 2, 5)], [banks[:, b, :] for b in (3, 4, 6)]
        stat_ps, down_ps = banks[:, 0, :], banks[:, 7, :]
        s_v = s_ps.rearrange("p (h k) -> p h k", h=HEADS)
        o_v = s_ps.rearrange("p (g a k) -> p g a k", g=PAIRS // 2, a=2)

        sem = lambda n: new_semaphore("b_" + n)
        s_const = sem("const")
        s_zero = sem("zero")
        s_pool = sem("pool_set")
        s_ready = sem("constants_ready")
        s_sp_gate = sem("load_gate")
        s_gate = sem("gate")
        s_wqkv = sem("wqkv_loaded")
        s_wo = sem("wo_loaded")
        s_wffn = sem("wffn_loaded")
        s_tab = sem("tables_ready")
        C = {}
        for name, per in dict(xs=2, qkv=6, sq=4, ab=4, ssq=4, lns=2, rexp=2, newt=8, rot=4, qn=4, tr=4, qkT=4,
                              halo=1, v=2, vdma=14 * 16, vhalo=2 * 16, s=2, mx=2, sub=2, exp=2, sum=2, rec=1, pn=1, ptr=2,
                              ptc=2, pv=2, oc=2, wo=1, xmid=1, zs=2, mean=1, zc=1, zq=1, varm=1, lnv=1, rs=1,
                              n2=3, xn=1, xng=1, up=3, gl=3, hh=3, dn=1, xo=1).items():
            C[name] = Count(name, per)

        block = ctx.enter_context(nc.Block())

        def wait(eng, name, i, k):
            eng.wait_ge(C[name].sem, C[name].at(i, k))

        @block.sync
        def _(sp):
            for n in ("vdma", "vhalo"):
                sp.sem_inc(C[n].sem, C[n].per)
            sp.dma_start(rot_raw[:, :, :, :], const["rot"]).then_inc(s_const, 16)
            sp.dma_start(ident[:, :], const["ident"]).then_inc(s_const, 16)
            sp.dma_start(masks_in, const["masks"]).then_inc(s_const, 16)
            for j, n in enumerate(("q_scale", "k_scale")):
                sp.dma_start(qk_scale[:, j, :, :],
                             w[n].rearrange("(o l) d -> o l d", o=1).broadcast_to([P, DEPTH, HD])).then_inc(s_const, 16)
            for c, (c0, n) in enumerate(FCH):
                for g in range(2):
                    sp.dma_start(b1c[0:n, :, g, c:c + 1],
                                 w["b1"][:, g * FF + c0:g * FF + c0 + n].rearrange("l (p o) -> p l o", o=1),
                                 allow_slow_non_contiguous=True).then_inc(s_const, 16)
            for n, t in (("b2", b2c), ("ln_g", gc), ("ln_b", bc)):
                sp.dma_start(t[:, :], w[n].rearrange("l d -> d l"), allow_slow_non_contiguous=True).then_inc(s_const, 16)
            with sp.Fori(0, DEPTH) as l:
                wait(sp, "qkv", l * TILES, 0)
                sp.sem_inc(s_sp_gate, 1)
                wl = w["Wqkv"][ds(l, 1), :, :].rearrange("o d n -> (o d) n")
                sp.dma_start(wqkv[:, 0:2 * INNER], wl[:, 0:2 * INNER]).then_inc(s_wqkv, 16)
                for a in range(2):
                    sp.dma_start(wqkv[:, 2 * INNER + a * CH:2 * INNER + (a + 1) * CH].rearrange("p (h d) -> p h d", d=HD),
                                 wl[:, 2 * INNER:].rearrange("p (h a d) -> p h a d", a=2, d=HD)[:, :, a, :]).then_inc(s_wqkv, 16)
                wait(sp, "wo", l * TILES, 0)
                sp.sem_inc(s_sp_gate, 1)
                for b in range(2):
                    for a in range(2):
                        sp.dma_start(wo[64 * b:64 * b + 64, :, :].rearrange("p (g a) d -> p g a d", a=2)[:, :, a, :],
                                     w["Wo"][ds(l, 1), :, :].rearrange("o (g b a p) d -> p b a (o g) d", b=2, a=2, p=HD
                                                                       )[:, b, a]).then_inc(s_wo, 16)
                wait(sp, "dn", l * CHUNKS, 0)
                sp.sem_inc(s_sp_gate, 1)
                sp.dma_start(w1[:, :], w["W1"][ds(l, 1), :, :].rearrange("o d n -> (o d) n")).then_inc(s_wffn, 16)
                for c, (c0, n) in enumerate(FCH):
                    sp.dma_start(w2[0:n, c, :], w["W2"][ds(l, 1), c0:c0 + n, :].rearrange("o d n -> (o d) n")).then_inc(s_wffn, 16)
                with sp.Fori(0, TILES) as t:
                    i = l * TILES + t
                    wait(sp, "pv", i, 0)
                    sp.sem_inc(s_sp_gate, 1)
                    wait(sp, "v", i, 2)
                    sp.sem_inc(s_sp_gate, 1)
                    this, before = v_tok[:, ds(t % 2, 1), :], v_tok[:, ds((t + 1) % 2, 1), :]
                    half = lambda a: slice(a * CH, (a + 1) * CH)
                    for a in range(2):
                        sp.dma_start(v_win[64 * a:64 * a + WIN, 0:1, :], before[P - WIN:P, :, half(a)]
                                     ).then_inc(C["vhalo"].sem, 16)
                    for a in range(2):
                        r = 64 * a
                        for j in range(WPT):
                            own = this[WIN * j:WIN * (j + 1), :, half(a)]
                            sp.dma_start(v_win[r + WIN:r + 2 * WIN, j:j + 1, :], own).then_inc(C["vdma"].sem, 16)
                            if j < WPT - 1:
                                sp.dma_start(v_win[r:r + WIN, j + 1:j + 2, :], own).then_inc(C["vdma"].sem, 16)
            wait(sp, "vdma", DEPTH * TILES, 0)
            wait(sp, "vhalo", DEPTH * TILES, 0)

        @block.gpsimd
        def _(pool):
            for n in ("rot", "qn"):
                pool.sem_inc(C[n].sem, C[n].per)
            for n, (part, value) in enumerate(((kT[:, :, :, :], 0.0), (pT[:, :, :, :], 0.0), (v_tok[P - WIN:P, 1, :], 0.0), (x_mid[:, 0:1], 0.0),
                                               (x_out[:, 0:1], 0.0), (meanw[:, :], 1.0 / DIM))):
                if n:
                    pool.wait_ge(s_pool, n)
                nc.gpsimd.memset(part, value).then_inc(s_pool, 1)
            pool.wait_ge(s_pool, 6)
            pool.sem_inc(s_zero, 6)
            pool.wait_ge(s_const, 14 * 16)
            pool.wait_ge(s_ready, 3)
            with pool.Fori(0, DEPTH) as l:
                wait(pool, "ab", l * TILES, 0)
                for j in range(4):
                    for half in range(2):
                        src = half if j % 2 == 0 else 1 - half
                        lo = HD // 2 * half
                        nc.gpsimd.tensor_tensor(
                            rot_tab[:, j, :, lo:lo + 32], rot_raw[:, j, :, lo:lo + 32],
                            qk_scale[:, j // 2, ds(l, 1), 32 * src:32 * src + 32].broadcast_to([P, TILES, 32]),
                            ALU.mult).then_inc(s_tab, 1)
                with pool.Fori(0, TILES) as t:
                    i = l * TILES + t
                    for h in range(2):
                        for c in (2 * h, 2 * h + 1):
                            wait(pool, "ab", i, c + 1)
                            wait(pool, "qn", i, c - 3)
                            nc.gpsimd.tensor_tensor(rot[:, c, :, :], pa[:, c, :, :], pbm[:, c, :, :],
                                                    ALU.add).then_inc(C["rot"].sem, 1)
                        for c in (2 * h, 2 * h + 1):
                            wait(pool, "newt", i, 4 * h + 4)
                            wait(pool, "rot", i, c + 1)
                            wait(pool, "tr", i, c - 3)
                            nc.gpsimd.tensor_tensor(qkn[:, c, :, :], rot[:, c, :, :],
                                                    rn[:, c, :].rearrange("p (h o) -> p h o", o=1
                                                                          ).broadcast_to([P, HPC, HD]),
                                                    ALU.mult).then_inc(C["qn"].sem, 1)

        def layers(eng, first, attend, feed):
            with eng.Fori(0, DEPTH) as l:
                first(l)
                with eng.Fori(0, TILES - 2) as t:
                    attend(l, t, l * TILES + t, 2)
                for t in range(TILES - 2, TILES):
                    attend(l, t, l * TILES + t, TILES - 1 - t)
                with eng.Fori(0, CHUNKS - 1) as n:
                    feed(l, n, l * CHUNKS + n, True)
                feed(l, CHUNKS - 1, l * CHUNKS + (CHUNKS - 1), False)

        @block.scalar
        def _(act):
            for n in ("sq", "lns", "rexp", "qkT", "v", "exp", "ptc", "oc", "zs", "zq", "lnv", "rs", "gl", "halo"):
                act.sem_inc(C[n].sem, C[n].per)
            act.wait_ge(s_zero, 6)
            act.wait_ge(s_ready, 3)

            def squares(i, cs):
                for c in cs:
                    wait(act, "qkv", i, c + 1)
                    wait(act, "ssq", i, 0)
                    nc.scalar.activation(sq[:, c, :, :], q_ps[c % 3].rearrange("p (h d) -> p h d", d=HD),
                                         ACT.Square).then_inc(C["sq"].sem, 1)

            def values(t, i):
                wait(act, "vdma", i - 1, 0)
                wait(act, "vhalo", i, 0)
                for c in range(2):
                    wait(act, "qkv", i, 5 + c)
                    nc.scalar.copy(v_tok[:, ds(t % 2, 1), c * CH:(c + 1) * CH].rearrange("p o n -> p (o n)"), q_ps[(4 + c) % 3]
                                   ).then_inc(C["v"].sem, 1)

            def norms(i, h):
                part = slice(2 * h, 2 * h + 2)
                wait(act, "ssq", i, 2 * h + 2)
                wait(act, "newt", i, 4 * h - 4)
                nc.scalar.activation(lnss[:, part, :], ss[:, part, :], ACT.Ln, scale=2.0 ** 20).then_inc(C["lns"].sem, 1)
                wait(act, "lns", i, h + 1)
                nc.scalar.activation(r0[:, part, :], lnss[:, part, :], ACT.Exp, scale=-0.5, bias=ln_shift[:, 0:1]
                                     ).then_inc(C["rexp"].sem, 1)

            def halo(i, first=False):
                wait(act, "s", i, 0)
                wait(act, "qkT", i, 0)
                before = (x_mid[:, 0:1].rearrange("p (o a k) -> p o a k", o=1, a=1).broadcast_to([P, PAIRS, 2, WIN]) if first
                          else kT[:, :, :, P:WIN + P])
                nc.scalar.copy(kT[:, :, :, 0:WIN], before).then_inc(C["halo"].sem, 1)
                wait(act, "halo", i, 1)

            def transposed(i, fs):
                for f in fs:
                    wait(act, "tr", i, f + 1)
                    if f < 2:
                        last = nc.scalar.copy(qT[:, 4 * f:4 * f + 4, :], t_ps[f % 2])
                    else:
                        for a in range(2):
                            rows = slice(64 * a, 64 * a + 64)
                            last = nc.scalar.copy(kT[rows, 4 * f - 8:4 * f - 4, a, WIN:WIN + P], t_ps[f % 2][rows])
                    last.then_inc(C["qkT"].sem, 1)

            def first(l):
                nc.scalar.preload_act_table_set("natural_log_exp_and_others")
                i = l * TILES
                squares(i, range(4))
                values(0, i)
                norms(i, 0)
                norms(i, 1)
                halo(i, True)
                transposed(i, range(4))
                squares(i + 1, range(4))
                norms(i + 1, 0)
                norms(i + 1, 1)

            def attend(l, t, i, left):
                if left:
                    halo(i + 1)
                    transposed(i + 1, (0, 1))
                for a in range(2):
                    wait(act, "sub", i, a + 1)
                    h = slice(a * PAIRS, (a + 1) * PAIRS)
                    nc.scalar.activation(pexp[:, h, :], ssub[:, h, :], ACT.Exp, scale=8.0).then_inc(C["exp"].sem, 1)
                if left:
                    values(t + 1, i + 1)
                    transposed(i + 1, (2,))
                if left == 2:
                    squares(i + 2, (0,))
                if left:
                    transposed(i + 1, (3,))
                if left == 2:
                    squares(i + 2, (1,))
                if left == 0:
                    shifted(l, 0, l * CHUNKS)
                    centred_squares(l * CHUNKS)
                for f in range(2):
                    wait(act, "ptr", i, f + 1)
                    wait(act, "pv", i, 0)
                    for a in range(2):
                        rows = slice(64 * a, 64 * a + 64)
                        last = nc.scalar.copy(pT[rows, 4 * f:4 * f + 4, a, :], t_ps[f][rows])
                    last.then_inc(C["ptc"].sem, 1)
                if left == 2:
                    squares(i + 2, (2, 3))
                    norms(i + 2, 0)
                wait(act, "wo", i, 0)
                for f in range(2):
                    wait(act, "pv", i, f + 1)
                    nc.scalar.copy(oT[:, 4 * f:4 * f + 4, :].rearrange("p (g a) k -> p g a k", a=2),
                                   o_v[:, 2 * f:2 * f + 2, :, :]).then_inc(C["oc"].sem, 1)
                if left == 2:
                    norms(i + 2, 1)
                if left == 0:
                    deviation(l * CHUNKS)

            def shifted(l, n, j):
                wait(act, "xmid", l * TILES + (TILES - 1), 0 if isinstance(n, int) and n == 0 else 1)
                wait(act, "zc", j, 0)
                nc.scalar.copy(zs[0:64, :], x_mid[0:64, ds(n * CH + 1, CH)]).then_inc(C["zs"].sem, 1)
                nc.scalar.copy(zs[64:P, :], x_mid[64:P, ds(n * CH, CH)]).then_inc(C["zs"].sem, 1)

            def centred_squares(j):
                wait(act, "zc", j, 1)
                nc.scalar.activation(zq[:, :], zc[:, :], ACT.Square).then_inc(C["zq"].sem, 1)

            def deviation(j):
                wait(act, "varm", j, 1)
                nc.scalar.activation(lnv[:, :], stat_ps, ACT.Ln, bias=eps_col[:, 0:1]).then_inc(C["lnv"].sem, 1)
                wait(act, "lnv", j, 1)
                wait(act, "xn", j, 0)
                nc.scalar.activation(rs0[:, :], lnv[:, :], ACT.Exp, scale=-0.5).then_inc(C["rs"].sem, 1)

            def feed(l, n, j, more):
                if more:
                    shifted(l, n + 1, j + 1)
                    centred_squares(j + 1)
                    nc.scalar.preload_act_table_set("natural_log_exp_and_others")
                    deviation(j + 1)
                for c, (c0, m) in enumerate(FCH):
                    wait(act, "up", j, c + 1)
                    wait(act, "hh", j, c - 2)
                    nc.scalar.activation(gl[0:m, c, :], gate_ps[c][0:m, :], ACT.Gelu,
                                         bias=b1c[0:m, ds(l, 1), 1, c]).then_inc(C["gl"].sem, 1)

            layers(act, first, attend, feed)

        @block.vector
        def _(dve):
            for n in ("xs", "ab", "ssq", "newt", "mx", "sub", "sum", "rec", "pn", "xmid", "zc", "n2", "xn",
                      "xng", "hh", "xo"):
                dve.sem_inc(C[n].sem, C[n].per)
            dve.wait_ge(s_const, 14 * 16)
            nc.vector.tensor_copy(masks[:, :, :], masks_in)
            nc.vector.tensor_copy(identb[:, :], ident[:, :]).then_inc(s_ready, 1)
            nc.vector.tensor_copy(x_in[:, 1:], xT[:, 1:]).then_inc(s_ready, 1)
            nc.vector.memset(ln_shift[:, :], 10.0 * float(np.log(2.0)))
            nc.vector.memset(eps_col[:, :], EPS)
            nc.vector.tensor_scalar_mul(g_half[:, :], gc[:, :], -0.5).then_inc(s_ready, 1)

            dve.wait_ge(s_ready, 3)

            def shifted(l, t, i):
                wait(dve, "xo", l * CHUNKS, 0)
                wait(dve, "qkv", i - 1, 6)
                nc.vector.tensor_copy(xs[0:64, :], x_in[0:64, ds(t * P + 1, P)]).then_inc(C["xs"].sem, 1)
                nc.vector.tensor_copy(xs[64:P, :], x_in[64:P, ds(t * P, P)]).then_inc(C["xs"].sem, 1)

            def rotate(t, i, cs):
                for c in cs:
                    wait(dve, "sq", i, c + 1)
                    wait(dve, "rot", i, c - 3)
                    ps = q_ps[c % 3].rearrange("p (h a d) -> p h a d", a=2, d=HD // 2)
                    tn = rot_tab[:, 2 * (c // 2) + 1, ds(t, 1), :].rearrange("p o (a d) -> p o a d", a=2)
                    nc.vector.tensor_tensor(pa[:, c, :, :], q_ps[c % 3].rearrange("p (h d) -> p h d", d=HD),
                                            rot_tab[:, 2 * (c // 2), ds(t, 1), :].broadcast_to([P, HPC, HD]), ALU.mult)
                    for half in range(2):
                        last = nc.vector.tensor_tensor(
                            pbm[:, c, :, 32 * half:32 * half + 32], ps[:, :, 1 - half, :],
                            tn[:, :, half, :].broadcast_to([P, HPC, 32]), ALU.mult)
                    last.then_inc(C["ab"].sem, 1)

            def sums(i, h):
                part = slice(2 * h, 2 * h + 2)
                nc.vector.tensor_reduce(ss[:, part, :], sq[:, part, :, :], AX_X, ALU.add).then_inc(C["ssq"].sem, 1)
                wait(dve, "ssq", i, 2 * h + 1)
                nc.vector.tensor_scalar_max(ss[:, part, :], ss[:, part, :], 1e-24).then_inc(C["ssq"].sem, 1)

            def newton(i, h):
                part = slice(2 * h, 2 * h + 2)
                r, (r2, v, u) = r0[:, part, :], (nt[:, n, part, :] for n in range(3))
                wait(dve, "rexp", i, h + 1)
                nc.vector.tensor_tensor(r2, r, r, ALU.mult).then_inc(C["newt"].sem, 1)
                wait(dve, "newt", i, 4 * h + 1)
                nc.vector.tensor_tensor(v, r2, ss[:, part, :], ALU.mult).then_inc(C["newt"].sem, 1)
                wait(dve, "newt", i, 4 * h + 2)
                nc.vector.tensor_scalar(u, v, -0.5, 1.5, ALU.mult, ALU.add).then_inc(C["newt"].sem, 1)
                wait(dve, "newt", i, 4 * h + 3)
                wait(dve, "qn", i, 2 * h - 2)
                nc.vector.tensor_tensor(rn[:, part, :], u, r, ALU.mult).then_inc(C["newt"].sem, 1)
                wait(dve, "newt", i, 4 * h + 4)

            def queries_and_keys(t, i):
                rotate(t, i, (0, 1))
                sums(i, 0)
                rotate(t, i, (2,))
                newton(i, 0)
                rotate(t, i, (3,))
                sums(i, 1)

            def first(l):
                i = l * TILES
                dve.wait_ge(s_tab, l * 8 + 8)
                for t in range(2):
                    shifted(l, t, i + t)
                    queries_and_keys(t, i + t)
                    if t == 0:
                        newton(i, 1)

            def attend(l, t, i, left):
                for a in range(2):
                    h = slice(a * PAIRS, (a + 1) * PAIRS)
                    wait(dve, "s", i, a + 1)
                    nc.vector.tensor_reduce(smax[:, h], s_v[:, h, :], AX_X, ALU.max).then_inc(C["mx"].sem, 1)
                    if a == 0 and left:
                        newton(i + 1, 1)
                    if a == 1 and left == 2:
                        shifted(l, t + 2, i + 2)
                    wait(dve, "mx", i, a + 1)
                    wait(dve, "exp", i, 0)
                    nc.vector.tensor_tensor(ssub[:, h, :], s_v[:, h, :],
                                            smax[:, h].rearrange("p (h o) -> p h o", o=1).broadcast_to([P, PAIRS, 2 * WIN]),
                                            ALU.subtract).then_inc(C["sub"].sem, 1)
                for a in range(2):
                    h = slice(a * PAIRS, (a + 1) * PAIRS)
                    wait(dve, "exp", i, a + 1)
                    nc.vector.tensor_reduce(psum_[:, h], pexp[:, h, :], AX_X, ALU.add).then_inc(C["sum"].sem, 1)
                wait(dve, "sum", i, 2)
                nc.vector.reciprocal(prec[:, :], psum_[:, :]).then_inc(C["rec"].sem, 1)
                wait(dve, "rec", i, 1)
                wait(dve, "ptr", i, 0)
                nc.vector.tensor_tensor(pn[:, :, :], pexp[:, :, :],
                                        prec[:, :].rearrange("p (h o) -> p h o", o=1).broadcast_to([P, HEADS, 2 * WIN]),
                                        ALU.mult).then_inc(C["pn"].sem, 1)
                if left == 2:
                    queries_and_keys(t + 2, i + 2)
                if left == 0:
                    centre(l * CHUNKS)
                wait(dve, "wo", i, 1)
                nc.vector.tensor_tensor(x_mid[:, ds(t * P + 1, P)], wo_ps, x_in[:, ds(t * P + 1, P)],
                                        ALU.add).then_inc(C["xmid"].sem, 1)
                if left == 0:
                    normalised(l, l * CHUNKS)

            def centre(j):
                wait(dve, "mean", j, 1)
                nc.vector.tensor_tensor(zc[:, :], zs[:, :], stat_ps, ALU.subtract).then_inc(C["zc"].sem, 1)

            def normalised(l, j):
                wait(dve, "rs", j, 1)
                nc.vector.tensor_tensor(rt[:, 0, :], rs0[:, :], rs0[:, :], ALU.mult).then_inc(C["n2"].sem, 1)
                nc.vector.tensor_tensor(rt[:, 1, :], zc[:, :], rs0[:, :], ALU.mult).then_inc(C["n2"].sem, 1)
                wait(dve, "n2", j, 1)
                nc.vector.scalar_tensor_tensor(rt[:, 2, :], stat_ps, EPS, rt[:, 0, :], ALU.add, ALU.mult
                                               ).then_inc(C["n2"].sem, 1)
                wait(dve, "n2", j, 3)
                nc.vector.scalar_tensor_tensor(xn[:, :], rt[:, 2, :], -3.0, rt[:, 1, :], ALU.add, ALU.mult
                                               ).then_inc(C["xn"].sem, 1)
                wait(dve, "xn", j, 1)
                wait(dve, "up", j, 0)
                nc.vector.tensor_scalar(xng[:, :], xn[:, :], g_half[:, ds(l, 1)], bc[:, ds(l, 1)], ALU.mult,
                                        ALU.add).then_inc(C["xng"].sem, 1)

            def feed(l, n, j, more):
                if more:
                    centre(j + 1)
                for c, (c0, m) in enumerate(FCH):
                    wait(dve, "gl", j, c + 1)
                    wait(dve, "dn", j, 0)
                    nc.vector.scalar_tensor_tensor(hh[0:m, c, :], value_ps[c][0:m, :], b1c[0:m, ds(l, 1), 0, c],
                                                   gl[0:m, c, :], ALU.add, ALU.mult).then_inc(C["hh"].sem, 1)
                if more:
                    normalised(l, j + 1)
                wait(dve, "dn", j, 1)
                nc.vector.scalar_tensor_tensor(x_out[:, ds(n * CH + 1, CH)], down_ps, b2c[:, ds(l, 1)],
                                               x_mid[:, ds(n * CH + 1, CH)], ALU.add, ALU.add).then_inc(C["xo"].sem, 1)

            layers(dve, first, attend, feed)

        @block.tensor
        def _(pe):
            for n in ("qkv", "tr", "s", "ptr", "pv", "wo", "mean", "varm", "up", "dn"):
                pe.sem_inc(C[n].sem, C[n].per)
            pe.wait_ge(s_zero, 6)
            pe.wait_ge(s_ready, 3)

            def project(i, cs):
                for c in cs:
                    if c == 0:
                        wait(pe, "xs", i, 2)
                    if c in (0, 3):
                        wait(pe, "ab", i, c // 3)
                    elif c in (1, 2):
                        wait(pe, "v", i, 0)
                    else:
                        wait(pe, "ab", i, c - 2)
                    nc.tensor.matmul(q_ps[c % 3], xs[:, :], wqkv[:, c * CH:(c + 1) * CH], start=True,
                                     stop=True).then_inc(C["qkv"].sem, 1)

            def turn(i, fs):
                for f in fs:
                    wait(pe, "qn", i, f + 1)
                    wait(pe, "qkT", i, f - 1)
                    for k in range(4):
                        last = nc.tensor.transpose(t_ps[f % 2][:, k, :],
                                                   qkn[:, f, 2 * k:2 * k + 2, :].rearrange("p a d -> p (a d)"), ident[:, :])
                    last.then_inc(C["tr"].sem, 1)

            def first(l):
                pe.wait_ge(s_wqkv, l * 48 + 48)
                i = l * TILES
                project(i, range(6))
                turn(i, range(4))
                pe.wait_ge(s_wo, l * 64 + 64)
                project(i + 1, range(4))

            def attend(l, t, i, left):
                wait(pe, "oc", i, 0)
                wait(pe, "qkT", i, 4)
                mt = masks[:, t:t + 1, :] if isinstance(t, int) else masks[:, ds(t, 1), :]
                for a in range(2):
                    nc.tensor.matmul(s_ps[:, a * CH:(a + 1) * CH], identb[:, :],
                                     mt.broadcast_to([P, HPC, 2 * WIN]), start=True, stop=False,
                                     skip_group_check=True)
                    for hp in range(4 * a, 4 * a + 4):
                        for j in range(WPT):
                            last = nc.tensor.matmul(
                                s_v[WIN * j:WIN * (j + 1), 2 * hp:2 * hp + 2, :], qT[:, hp, WIN * j:WIN * (j + 1)],
                                kT[:, hp, :, WIN * j:WIN * (j + 2)], start=False, stop=True, skip_group_check=True)
                    last.then_inc(C["s"].sem, 1)
                if left:
                    turn(i + 1, (0, 1))
                    project(i + 1, (4, 5))
                    turn(i + 1, (2, 3))
                if left == 2:
                    project(i + 2, (0, 1))
                if left == 0:
                    pe.wait_ge(s_wffn, l * 64 + 64)
                    mean(l * CHUNKS)
                wait(pe, "pn", i, 1)
                for f in range(2):
                    if left:
                        wait(pe, "qkT", i + 1, f + 3)
                    for k in range(4):
                        hp = 4 * f + k
                        last = nc.tensor.transpose(t_ps[f][:, k, :],
                                                   pn[:, 2 * hp:2 * hp + 2, :].rearrange("p a d -> p (a d)"), ident[:, :])
                    last.then_inc(C["ptr"].sem, 1)
                if left == 2:
                    project(i + 2, (2, 3))
                wait(pe, "vhalo", i, 2 * 16)
                pe.sem_inc(s_gate, 1)
                wait(pe, "vdma", i, 14 * 16)
                pe.sem_inc(s_gate, 1)
                for half in range(2):
                    wait(pe, "ptc", i, half + 1)
                    pe.sem_inc(s_gate, 1)
                    for hp in range(4 * half, 4 * half + 4):
                        g, b = divmod(hp, 2)
                        for j in range(WPT):
                            last = nc.tensor.matmul(
                                o_v[64 * b:64 * b + 64, g, :, WIN * j:WIN * (j + 1)], v_win[:, j, HD * hp:HD * (hp + 1)],
                                pT[:, hp, :, WIN * j:WIN * (j + 1)], start=True, stop=True)
                    last.then_inc(C["pv"].sem, 1)
                if left == 0:
                    variance(l * CHUNKS)
                wait(pe, "xmid", i, 0)
                for hp in range(PAIRS):
                    if hp % 4 == 0:
                        wait(pe, "oc", i, hp // 4 + 1)
                    last = nc.tensor.matmul(wo_ps, wo[:, hp, :], oT[:, hp, :], start=hp == 0, stop=hp == PAIRS - 1)
                last.then_inc(C["wo"].sem, 1)

            def mean(j):
                wait(pe, "zs", j, 2)
                wait(pe, "xn", j, 0)
                nc.tensor.matmul(stat_ps, meanw[:, :], zs[:, :], start=True, stop=True).then_inc(C["mean"].sem, 1)

            def variance(j):
                wait(pe, "zq", j, 1)
                nc.tensor.matmul(stat_ps, meanw[:, :], zq[:, :], start=True, stop=True).then_inc(C["varm"].sem, 1)

            def feed(l, n, j, more):
                if more:
                    mean(j + 1)
                wait(pe, "xng", j, 1)
                for c, (c0, m) in enumerate(FCH):
                    nc.tensor.matmul(gate_ps[c][0:m, :], w1[:, FF + c0:FF + c0 + m], xng[:, :], start=True, stop=True)
                    nc.tensor.matmul(value_ps[c][0:m, :], w1[:, c0:c0 + m], xng[:, :], start=True, stop=True
                                     ).then_inc(C["up"].sem, 1)
                    if more and c == 0:
                        variance(j + 1)
                wait(pe, "xo", j, 0)
                for c, (c0, m) in enumerate(FCH):
                    wait(pe, "hh", j, c + 1)
                    last = nc.tensor.matmul(down_ps, w2[0:m, c, :], hh[0:m, c, :], start=c == 0, stop=c == 2)
                last.then_inc(C["dn"].sem, 1)

            layers(pe, first, attend, feed)


def residual_layernorm(nc, tag, xT, f, out, first=0):
    ctx = ExitStack()
    with ctx:
        def sb(name, shape, dt=F32):
            return ctx.enter_context(nc.sbuf_tensor(f"{tag}_{name}", shape, dt))
        meanw = sb("meanw", [P, P])
        eps = sb("eps", [P, 1])
        s, sc, sq, lnv, r0, t1, t2, z = (sb(n, [P, CHUNKS, CH]) for n in ("s", "sc", "sq", "lnv", "r0", "t1", "t2", "z"))
        m_ps = [ctx.enter_context(nc.psum_tensor(f"{tag}_mean{i}", [P, CH], F32)) for i in range(CHUNKS)]
        v_ps = [ctx.enter_context(nc.psum_tensor(f"{tag}_var{i}", [P, CH], F32)) for i in range(CHUNKS)]
        sem = lambda n: ctx.enter_context(nc.semaphore(f"{tag}_{n}"))
        s_set, s_sum, s_mean, s_cen, s_sq, s_var, s_ln, s_r0, s_nt, s_out = (
            sem(n) for n in ("set", "sum", "mean", "centred", "squared", "variance", "ln", "r0", "newton", "out"))
        block = ctx.enter_context(nc.Block())

        @block.gpsimd
        def _(pool):
            nc.gpsimd.memset(meanw[:, :], 1.0 / DIM).then_inc(s_set, 1)
            nc.gpsimd.memset(eps[:, :], EPS).then_inc(s_set, 1)

        @block.vector
        def _(dve):
            for c in range(CHUNKS):
                nc.vector.tensor_tensor(s[:, c, :], xT[:, 1 + c * CH:1 + (c + 1) * CH],
                                        f[:, first + c * CH:first + (c + 1) * CH], ALU.add).then_inc(s_sum, 1)
            for c in range(CHUNKS):
                dve.wait_ge(s_mean, c + 1)
                nc.vector.tensor_tensor(sc[:, c, :], s[:, c, :], m_ps[c][:, :], ALU.subtract).then_inc(s_cen, 1)
            for c in range(CHUNKS):
                dve.wait_ge(s_r0, c + 1)
                nc.vector.tensor_tensor(t1[:, c, :], r0[:, c, :], r0[:, c, :], ALU.mult).then_inc(s_nt, 1)
                dve.wait_ge(s_cen, c + 1)
                nc.vector.scalar_tensor_tensor(z[:, c, :], sc[:, c, :], -0.5, r0[:, c, :], ALU.mult, ALU.mult).then_inc(s_nt, 1)
                dve.wait_ge(s_nt, 3 * c + 1)
                nc.vector.scalar_tensor_tensor(t2[:, c, :], v_ps[c][:, :], EPS, t1[:, c, :], ALU.add, ALU.mult
                                               ).then_inc(s_nt, 1)
                dve.wait_ge(s_nt, 3 * c + 3)
                nc.vector.scalar_tensor_tensor(out[:, 1 + c * CH:1 + (c + 1) * CH], t2[:, c, :], -3.0, z[:, c, :], ALU.add,
                                               ALU.mult).then_inc(s_out, 1)

        @block.scalar
        def _(act):
            nc.scalar.preload_act_table_set("natural_log_exp_and_others")
            act.wait_ge(s_set, 2)
            for c in range(CHUNKS):
                act.wait_ge(s_cen, c + 1)
                nc.scalar.activation(sq[:, c, :], sc[:, c, :], ACT.Square).then_inc(s_sq, 1)
            for c in range(CHUNKS):
                act.wait_ge(s_var, c + 1)
                nc.scalar.activation(lnv[:, c, :], v_ps[c][:, :], ACT.Ln, bias=eps[:, 0:1]).then_inc(s_ln, 1)
                act.wait_ge(s_ln, c + 1)
                nc.scalar.activation(r0[:, c, :], lnv[:, c, :], ACT.Exp, scale=-0.5).then_inc(s_r0, 1)

        @block.tensor
        def _(pe):
            pe.wait_ge(s_set, 2)
            for c in range(CHUNKS):
                pe.wait_ge(s_sum, c + 1)
                nc.tensor.matmul(m_ps[c][:, :], meanw[:, :], s[:, c, :], start=True, stop=True).then_inc(s_mean, 1)
            for c in range(CHUNKS):
                pe.wait_ge(s_sq, c + 1)
                nc.tensor.matmul(v_ps[c][:, :], meanw[:, :], sq[:, c, :], start=True, stop=True).then_inc(s_var, 1)


def selective_scan(nc, xT, y, w):
    NST = w["A_log"].shape[1]
    RANK = w["W_dt"].shape[1]
    ctx = ExitStack()
    with ctx:
        def sb(name, shape, dt=F32):
            return ctx.enter_context(nc.sbuf_tensor("c_" + name, shape, dt))
        w_bc = sb("w_bc", [DIM, 2 * NST])
        w_dt = sb("w_dt", [DIM, RANK])
        w_pr = sb("w_pr", [RANK, DIM])
        b_dt = sb("b_dt", [DIM, 1])
        a_log = sb("a_log", [DIM, NST])
        a_neg = sb("a_neg", [DIM, NST])
        a_exp = sb("a_exp", [DIM, NST])
        d_par = sb("d_par", [DIM, 1])
        w_b = sb("w_b", [DIM, 2, P])
        w_c = sb("w_c", [DIM, 2, P])
        low = sb("low", [RANK, SEQ])
        z = sb("z", [DIM, SEQ])
        za = sb("za", [DIM, SEQ])
        e = sb("e", [DIM, SEQ])
        delta = sb("delta", [DIM, SEQ])
        dx = sb("dx", [DIM, SEQ])
        abar = sb("abar", [DIM, 2, SEQ])
        bx = sb("bx", [DIM, SEQ])
        h = sb("h", [DIM, SEQ])
        yc = sb("yc", [DIM, 2, SEQ])
        ps = [ctx.enter_context(nc.psum_tensor(f"c_ps{i}", [P, SEQ], F32)) for i in range(2)]
        sem = lambda n: ctx.enter_context(nc.semaphore("c_" + n))
        s_in, s_low, s_lowc, s_pr, s_z, s_e, s_l, s_dl, s_dx, s_a, s_y0, s_sp = (
            sem(n) for n in ("in", "low", "lowc", "pr", "z", "e", "l", "dl", "dx", "a", "y0", "sp"))

        class Count:
            def __init__(self, name, per):
                self.sem, self.per = ctx.enter_context(nc.semaphore("c_" + name)), per

        C = {n: Count(n, per) for n, per in dict(wcol=2, b=1, c=1, abar=1, bx=1, h=1, yc=1, acc=1).items()}

        def wait(eng, name, n, k):
            eng.wait_ge(C[name].sem, n * C[name].per + (C[name].per + k))

        block = ctx.enter_context(nc.Block())

        @block.sync
        def _(sp):
            for dst, src in ((w_bc, w["W_bc"]), (w_dt, w["W_dt"]), (w_pr, w["W_dtproj"]), (a_log, w["A_log"]),
                             (b_dt, w["b_dtproj"].rearrange("(p o) -> p o", o=1)),
                             (d_par, w["D_param"].rearrange("(p o) -> p o", o=1))):
                sp.dma_start(dst[:, :], src).then_inc(s_in, 16)

        @block.gpsimd
        def _(pool):
            pool.sem_inc(C["wcol"].sem, 2)
            pool.sem_inc(C["acc"].sem, 2)
            pool.wait_ge(s_in, 96)
            nc.gpsimd.tensor_scalar(y[:, :], xT[:, 1:1 + SEQ], d_par[:, 0:1], None, ALU.mult).then_inc(s_y0, 1)
            pool.wait_ge(s_y0, 1)

            def columns(n, par):
                wait(pool, "b", n, 0)
                nc.gpsimd.tensor_copy(w_b[:, par, :], w_bc[:, ds(n, 1)].broadcast_to([DIM, P])).then_inc(C["wcol"].sem, 1)
                wait(pool, "c", n, 0)
                nc.gpsimd.tensor_copy(w_c[:, par, :], w_bc[:, ds(n + NST, 1)].broadcast_to([DIM, P])).then_inc(C["wcol"].sem, 1)

            def accumulate(n, par):
                wait(pool, "yc", n, 1)
                wait(pool, "acc", n, 1)
                nc.gpsimd.tensor_tensor(y[:, :], y[:, :], yc[:, par, :], ALU.add).then_inc(C["acc"].sem, 1)

            for n in range(2):
                columns(n, n)
            with pool.Fori(0, NST // 2 - 1) as m:
                for par in range(2):
                    columns(m * 2 + (par + 2), par)
                    accumulate(m * 2 + par, par)
            for par in range(2):
                accumulate(NST - 2 + par, par)
            wait(pool, "acc", NST, 1)

        @block.scalar
        def _(act):
            act.sem_inc(C["abar"].sem, C["abar"].per)
            nc.scalar.preload_act_table_set("natural_log_exp_and_others")
            act.wait_ge(s_in, 96)
            nc.scalar.activation(a_exp[:, :], a_log[:, :], ACT.Exp).then_inc(s_a, 1)
            act.wait_ge(s_low, 4)
            nc.scalar.copy(low[:, :], ps[0][0:RANK, :]).then_inc(s_lowc, 1)
            act.wait_ge(s_pr, 4)
            nc.scalar.activation(za[:, :], ps[1][:, :], ACT.Abs, bias=b_dt[:, 0:1]).then_inc(s_z, 1)
            act.wait_ge(s_z, 1)
            nc.scalar.activation(e[:, :], za[:, :], ACT.Exp, scale=-1.0).then_inc(s_e, 1)
            act.wait_ge(s_dl, 1)
            with act.Fori(0, NST // 2) as m:
                for par in range(2):
                    n = m * 2 + par
                    wait(act, "h", n, 0)
                    nc.scalar.activation(abar[:, par, :], delta[:, :], ACT.Exp, scale=a_neg[:, ds(n, 1)]
                                         ).then_inc(C["abar"].sem, 1)

        @block.vector
        def _(dve):
            for n in ("bx", "h", "yc"):
                dve.sem_inc(C[n].sem, C[n].per)
            dve.sem_inc(C["h"].sem, 1)
            chain = [0]

            def link(ins):
                chain[0] += 1
                ins.then_inc(s_sp, 1)
                dve.wait_ge(s_sp, chain[0])

            dve.wait_ge(s_a, 1)
            link(nc.vector.tensor_scalar(a_neg[:, :], a_exp[:, :], -1.0, None, ALU.mult))
            dve.wait_ge(s_z, 1)
            link(nc.vector.tensor_scalar(z[:, :], ps[1][:, :], b_dt[:, 0:1], 0.0, ALU.add, ALU.max))
            dve.wait_ge(s_e, 1)
            link(nc.vector.tensor_scalar(h[:, :], e[:, :], 2.0, None, ALU.add))
            link(nc.vector.reciprocal(bx[:, :], h[:, :]))
            link(nc.vector.tensor_tensor(h[:, :], e[:, :], bx[:, :], ALU.mult))
            link(nc.vector.tensor_tensor(bx[:, :], h[:, :], h[:, :], ALU.mult))
            link(nc.vector.tensor_scalar(za[:, :], bx[:, :], 2.0 / 15, None, ALU.mult))
            term, other = za, dx
            for k in (13, 11, 9, 7, 5, 3):
                link(nc.vector.scalar_tensor_tensor(other[:, :], term[:, :], 2.0 / k, bx[:, :], ALU.add, ALU.mult))
                term, other = other, term
            link(nc.vector.scalar_tensor_tensor(other[:, :], term[:, :], 2.0, h[:, :], ALU.add, ALU.mult))
            nc.vector.tensor_tensor(delta[:, :], z[:, :], other[:, :], ALU.add).then_inc(s_dl, 1)
            dve.wait_ge(s_dl, 1)
            link(nc.vector.tensor_tensor(dx[:, :], delta[:, :], xT[:, 1:1 + SEQ], ALU.mult))
            dve.sem_inc(s_dx, 1)
            with dve.Fori(0, NST // 2) as m:
                for par in range(2):
                    n = m * 2 + par
                    wait(dve, "b", n, 2)
                    nc.vector.tensor_tensor(bx[:, :], dx[:, :], ps[0][:, :], ALU.mult).then_inc(C["bx"].sem, 1)
                    wait(dve, "bx", n, 1)
                    wait(dve, "abar", n, 1)
                    nc.vector.tensor_tensor_scan(h[:, :], abar[:, par, :], bx[:, :], 0.0, ALU.mult, ALU.add
                                                 ).then_inc(C["h"].sem, 1)
                    wait(dve, "h", n, 2)
                    wait(dve, "c", n, 2)
                    wait(dve, "acc", n, 0)
                    nc.vector.tensor_tensor(yc[:, par, :], h[:, :], ps[1][:, :], ALU.mult).then_inc(C["yc"].sem, 1)

        @block.tensor
        def _(pe):
            for n in ("b", "c"):
                pe.sem_inc(C[n].sem, C[n].per)
                pe.sem_inc(C[n].sem, 1)
            pe.wait_ge(s_in, 96)
            for c in range(CHUNKS):
                nc.tensor.matmul(ps[0][0:RANK, c * CH:(c + 1) * CH], w_dt[:, :], xT[:, 1 + c * CH:1 + (c + 1) * CH],
                                 start=True, stop=True).then_inc(s_low, 1)
            pe.wait_ge(s_lowc, 1)
            for c in range(CHUNKS):
                nc.tensor.matmul(ps[1][:, c * CH:(c + 1) * CH], w_pr[:, :], low[:, c * CH:(c + 1) * CH],
                                 start=True, stop=True).then_inc(s_pr, 1)
            pe.wait_ge(s_dx, 1)
            with pe.Fori(0, NST // 2) as m:
                for par in range(2):
                    n = m * 2 + par
                    for k, (name, reader, wt) in enumerate((("b", "bx", w_b), ("c", "yc", w_c))):
                        wait(pe, reader, n, 0)
                        wait(pe, "wcol", n, 1 + k)
                        for c in range(CHUNKS):
                            last = nc.tensor.matmul(ps[k][:, c * CH:(c + 1) * CH], wt[:, par, :],
                                                    xT[:, 1 + c * CH:1 + (c + 1) * CH], start=True, stop=True)
                        last.then_inc(C[name].sem, 1)


def routed_experts(nc, xT, moe, w, const):
    EXPERTS, _, HID = w["Wup"].shape
    HALF = SEQ // 2
    GROUP = 64
    GPE = SEQ // GROUP
    BUDGET = GPE * 16
    EPT = P // HID
    ETILES = EXPERTS // EPT
    GPH = GPE // 2
    outer = ExitStack()
    with outer:
        def sbo(name, shape, dt=F32):
            return outer.enter_context(nc.sbuf_tensor("d_" + name, shape, dt))
        fsn = sbo("fsn", [EXPERTS, SEQ])
        w_up = sbo("w_up", [DIM, ETILES, P])
        w_gate = sbo("w_gate", [DIM, ETILES, P])
        w_down = sbo("w_down", [P, ETILES, DIM])
        b_up = sbo("b_up", [P, ETILES])
        b_gate = sbo("b_gate", [P, ETILES])
        b_down = sbo("b_down", [EXPERTS, DIM])
        spread = sbo("spread", [EXPERTS, ETILES, P])
        AHEAD = CHUNKS - 1
        ahead = sbo("ahead", [P, ETILES, AHEAD * CH])
        s_w = outer.enter_context(nc.semaphore("d_weights"))
        NW = 10

        ctx = ExitStack()
        with ctx:
            def sb(name, shape, dt=F32):
                return ctx.enter_context(nc.sbuf_tensor("d0_" + name, shape, dt))
            ident = sb("ident", [P, P])
            w_r = sb("w_r", [DIM, EXPERTS])
            b_r = sb("b_r", [P, EXPERTS])
            pairs = sb("pairs", [P, P])
            tril = sb("tril", [P, 2, P])
            gidx = sb("gidx", [P, GPH])
            lg = sb("lg", [P, 8, 2, EXPERTS])
            mx = sb("mx", [P, 8, 2])
            sx = sb("sx", [P, 8, 2])
            rx = sb("rx", [P, 8, 2])
            sc = sb("sc", [P, HALF])
            srt = [sb(f"srt{i}", [P, HALF]) for i in range(2)]
            low = sb("low", [64, HALF])
            gsum = sb("gsum", [P, GPH])
            gsT = sb("gsT", [GPH, P])
            gall = sb("gall", [P, SEQ])
            grow = sb("grow", [TILES, P])
            gcol = sb("gcol", [P, TILES])
            cmpo = sb("cmpo", [P, SEQ])
            cmp2 = sb("cmp2", [P, P])
            cnts = sb("cnts", [P, 4, TILES])
            rank = sb("rank", [P, TILES])
            sel_ = sb("sel", [P, TILES])
            col = sb("col", [P, 16])
            one = sb("one", [P, 2, GPH])
            ends = sb("ends", [P, GPH])
            ones = sb("ones", [P, HALF])
            gt = srt[0]
            pre, den, fs, eq = cmpo[:, 0:HALF], cmpo[:, HALF:SEQ], gall[:, 0:HALF], gall[:, HALF:SEQ]
            lg_ps = ctx.enter_context(nc.psum_tensor("d0_lgps", [P, 2, 8, EXPERTS], F32))
            sc_ps = ctx.enter_context(nc.psum_tensor("d0_scps", [P, HALF], F32))
            t_ps = ctx.enter_context(nc.psum_tensor("d0_tps", [P, CH], F32))
            n_ps = ctx.enter_context(nc.psum_tensor("d0_nps", [P, CH], F32))
            gate_ps = ctx.enter_context(nc.psum_tensor("d0_gateps", [P, 2, CH], F32))
            up_ps = lg_ps[:, :, :, :].rearrange("p a t e -> p a (t e)")
            dn_ps = sc_ps
            silu = sb("silu", [P, 2, CH])
            gate = sb("gate", [P, 2, CH])
            g_dram = nc.dram_tensor("d0_groups", [GPE, EXPERTS], F32).ap()
            sem = lambda n: ctx.enter_context(nc.semaphore("d0_" + n))
            (s_in, s_lg, s_dve, s_exp, s_scT, s_cp, s_flip, s_gT, s_gw, s_gr, s_rowT, s_n, s_swap, s_sum, s_set) = (
                sem(n) for n in ("in", "lg", "dve", "exp", "scT", "cp", "flip", "gT", "gw", "gr", "rowT", "n", "swap",
                                 "sum", "set"))
            marks = {}
            n_swap = [0]
            h_up, h_gate, h_silu, h_gated, h_mul = (sem("ahead_" + n) for n in ("up", "gate", "silu", "gated", "mul"))
            h_checkpoint = sem("ahead_checkpoint")

            def h_wait(eng, semaphore, c, k):
                eng.wait_ge(semaphore, c * ETILES + (ETILES + k))

            block = ctx.enter_context(nc.Block())

            @block.vector
            def _(dve):
                count = [0]

                def link(ins, mark=None):
                    count[0] += 1
                    ins.then_inc(s_dve, 1)
                    dve.wait_ge(s_dve, count[0])
                    if mark:
                        marks[mark] = count[0]

                link(nc.vector.memset(ones[:, :], 1.0))
                dve.wait_ge(s_in, 16 * 6)
                dve.wait_ge(s_lg, 1)
                for a in range(2):
                    link(nc.vector.tensor_tensor(lg[:, :, a, :], lg_ps[:, a, :, :],
                                                 b_r[:, :].rearrange("p (o e) -> p o e", o=1).broadcast_to([P, 8, EXPERTS]), ALU.add))
                link(nc.vector.tensor_reduce(mx[:, :, :], lg[:, :, :, :], AX_X, ALU.max))
                wide = lambda t: t[:, :, :].rearrange("p t (a o) -> p t a o", o=1).broadcast_to([P, 8, 2, EXPERTS])
                link(nc.vector.tensor_tensor(lg[:, :, :, :], lg[:, :, :, :], wide(mx), ALU.subtract), "shifted")
                dve.wait_ge(s_exp, 1)
                link(nc.vector.tensor_reduce(sx[:, :, :], lg[:, :, :, :], AX_X, ALU.add))
                link(nc.vector.reciprocal(rx[:, :, :], sx[:, :, :]))
                link(nc.vector.tensor_tensor(lg[:, :, :, :], lg[:, :, :, :], wide(rx), ALU.mult), "scores")
                dve.wait_ge(s_scT, 1)
                link(nc.vector.tensor_copy(sc[:, :], sc_ps[:, :]))

                cur = [sc]

                def halves(t, p, d):
                    v = t[0:p, :].rearrange("p (b s d) -> p b s d", s=2, d=d)
                    return v[:, :, 0, :], v[:, :, 1, :]

                def flip_step(size):
                    nxt = srt[0] if cur[0] is not srt[0] else srt[1]
                    d = size // 2
                    a, b = halves(cur[0], P, d)
                    oa, ob = halves(nxt, P, d)
                    nc.vector.tensor_tensor(oa, a, b[:, :, ::-1], ALU.max)
                    link(nc.vector.tensor_tensor(ob[:, :, ::-1], a, b[:, :, ::-1], ALU.min))
                    cur[0] = nxt

                def step(d):
                    nxt = srt[0] if cur[0] is not srt[0] else srt[1]
                    a, b = halves(cur[0], P, d)
                    oa, ob = halves(nxt, P, d)
                    nc.vector.tensor_tensor(oa, a, b, ALU.max)
                    link(nc.vector.tensor_tensor(ob, a, b, ALU.min))
                    cur[0] = nxt

                size = 2
                while size <= HALF:
                    flip_step(size)
                    d = size // 4
                    while d >= 1:
                        step(d)
                        d //= 2
                    size *= 2
                marks["halves"] = count[0]
                marks["halves_in"] = cur[0]
                dve.wait_ge(s_flip, 16)
                nxt = srt[0] if cur[0] is not srt[0] else srt[1]
                nc.vector.tensor_tensor(nxt[0:64, :], cur[0][0:64, :], low[:, ::-1], ALU.max)
                link(nc.vector.tensor_tensor(nxt[64:P, :], cur[0][0:64, :], low[:, ::-1], ALU.min))
                cur[0] = nxt
                d = HALF // 2
                while d >= 1:
                    step(d)
                    d //= 2
                order = cur[0][:, :].rearrange("p (g n) -> p g n", n=GROUP)
                link(nc.vector.tensor_reduce(gsum[:, :], order, AX_X, ALU.add), "gsum")
                link(nc.vector.tensor_copy(ends[:, :], order[:, :, GROUP - 1]))
                dve.wait_ge(s_gT, 1)
                link(nc.vector.tensor_copy(gsT[:, :], t_ps[0:GPH, 0:P]), "gsT")
                dve.wait_ge(s_rowT, 1)
                link(nc.vector.tensor_copy(gcol[:, :], n_ps[:, 0:TILES]))
                link(nc.vector.memset(cnts[:, :, :], 0.0))
                for c in range(TILES):
                    g = gcol[:, c:c + 1]
                    if c:
                        nc.vector.tensor_scalar(cmpo[:, 0:c * P], gall[:, 0:c * P], g, 0.0, ALU.is_ge, ALU.add,
                                                accum_out=cnts[:, 0, c:c + 1])
                    if c < TILES - 1:
                        nc.vector.tensor_scalar(cmpo[:, (c + 1) * P:], gall[:, (c + 1) * P:], g, 0.0, ALU.is_gt, ALU.add,
                                                accum_out=cnts[:, 1, c:c + 1])
                    blk = gall[:, c * P:(c + 1) * P]
                    for k, op in enumerate((ALU.is_ge, ALU.is_gt)):
                        last = nc.vector.scalar_tensor_tensor(cmpo[:, c * P:(c + 1) * P] if k == 0 else cmp2[:, :], blk, g,
                                                              tril[:, k, :], op, ALU.mult, accum_out=cnts[:, 2 + k, c:c + 1])
                        link(last)
                link(nc.vector.tensor_reduce(rank[:, :], cnts[:, :, :].rearrange("p k c -> p c k"), AX_X, ALU.add))
                link(nc.vector.tensor_scalar(sel_[:, :], rank[:, :], float(BUDGET), None, ALU.is_lt))
                link(nc.vector.tensor_reduce(col[:, 0:1], sel_[:, :], AX_X, ALU.add), "swap0")
                add = lambda o, x, y: link(nc.vector.tensor_tensor(col[:, o:o + 1], col[:, x:x + 1], col[:, y:y + 1], ALU.add))
                dve.wait_ge(s_swap, 32)
                add(2, 0, 1)
                link(nc.vector.tensor_scalar(one[:, 0, :], gidx[:, :], col[:, 2:3], None, ALU.is_equal))
                link(nc.vector.tensor_tensor(one[:, 1, :], one[:, 0, :], ends[:, :], ALU.mult))
                link(nc.vector.tensor_reduce(col[:, 3:4], one[:, 1, :], AX_X, ALU.add), "swap1")
                dve.wait_ge(s_swap, 64)
                add(5, 3, 4)
                link(nc.vector.tensor_scalar(col[:, 13:14], col[:, 2:3], 0.0, BIG, ALU.is_equal, ALU.mult))
                add(5, 5, 13)
                link(nc.vector.tensor_scalar(gt[:, :], sc[:, :], col[:, 5:6], 0.0, ALU.is_gt, ALU.add, accum_out=col[:, 6:7]))
                link(nc.vector.tensor_scalar(eq[:, :], sc[:, :], col[:, 5:6], 0.0, ALU.is_equal, ALU.add,
                                             accum_out=col[:, 10:11]), "swap2")
                link(nc.vector.tensor_tensor_scan(pre[:, :], ones[:, :], eq[:, :], 0.0, ALU.mult, ALU.add))
                dve.wait_ge(s_swap, 128)
                add(8, 6, 7)
                link(nc.vector.tensor_scalar(col[:, 14:15], col[:, 2:3], float(GROUP), None, ALU.mult))
                link(nc.vector.tensor_tensor(col[:, 9:10], col[:, 14:15], col[:, 8:9], ALU.subtract))
                link(nc.vector.tensor_tensor(col[64:P, 9:10], col[64:P, 9:10], col[64:P, 11:12], ALU.subtract))
                link(nc.vector.scalar_tensor_tensor(den[:, :], pre[:, :], col[:, 9:10], eq[:, :], ALU.is_le, ALU.mult))
                link(nc.vector.tensor_tensor(gt[:, :], gt[:, :], den[:, :], ALU.add))
                link(nc.vector.tensor_tensor(fs[:, :], sc[:, :], gt[:, :], ALU.mult), "fs")
                dve.wait_ge(s_sum, 1)
                link(nc.vector.tensor_scalar(den[:, :], dn_ps[:, :], 1e-6, None, ALU.add))
                link(nc.vector.reciprocal(eq[:, :], den[:, :]))
                for a in range(2):
                    link(nc.vector.tensor_tensor(fsn[:, a * HALF:(a + 1) * HALF], fs[64 * a:64 * a + 64, :],
                                                 eq[64 * a:64 * a + 64, :], ALU.mult))

            @block.sync
            def _(sp):
                for dst, src in ((ident, const["ident"]), (w_r, w["Wr"]),
                                 (b_r, w["br"].rearrange("(o e) -> o e", o=1).broadcast_to([P, EXPERTS])),
                                 (pairs, const["pairs"]), (gidx, const["gidx"])):
                    sp.dma_start(dst[:, :], src).then_inc(s_in, 16)
                sp.dma_start(tril[:, :, :], const["tril"]).then_inc(s_in, 16)
                for dst, src in ((w_up, "Wup"), (w_gate, "Wgate")):
                    sp.dma_start(dst[:, :, :].rearrange("d t (e h) -> d (t e) h", h=HID), w[src].rearrange("e d h -> d e h")
                                 ).then_inc(s_w, 16)
                sp.dma_start(w_down[:, :, :], w["Wdown"].rearrange("(t e) h d -> (e h) t d", e=EPT)).then_inc(s_w, 16)
                for dst, src in ((b_up, "bup"), (b_gate, "bgate")):
                    sp.dma_start(dst[:, :], w[src].rearrange("(t e) h -> (e h) t", e=EPT),
                                 allow_slow_non_contiguous=True).then_inc(s_w, 16)
                sp.dma_start(b_down[:, :], w["bdown"]).then_inc(s_w, 16)
                sp.dma_start(spread[:, :, :], const["spread"]).then_inc(s_w, 16)
                sp.wait_ge(s_dve, marks["halves"])
                sp.dma_start(low[:, :], marks["halves_in"][64:P, :]).then_inc(s_flip, 16)
                sp.wait_ge(s_dve, marks["gsT"])
                for a in range(2):
                    sp.dma_start(g_dram[GPH * a:GPH * (a + 1), :], gsT[:, 64 * a:64 * a + 64]).then_inc(s_gw, 16)
                sp.wait_ge(s_gw, 32)
                flat = g_dram.rearrange("g e -> (g e)")
                sp.dma_start(grow[:, :], flat.rearrange("(c p) -> c p", p=P)).then_inc(s_gr, 16)
                sp.dma_start(gall[:, :], flat.rearrange("(o n) -> o n", o=1).broadcast_to([P, SEQ])).then_inc(s_gr, 16)
                for mark, moves in (("swap0", ((1, 0),)), ("swap1", ((4, 3),)), ("swap2", ((7, 6), (11, 10)))):
                    sp.wait_ge(s_dve, marks[mark])
                    for o, x in moves:
                        for a in range(2):
                            sp.dma_start(col[64 * a:64 * a + 64, o:o + 1], col[64 - 64 * a:P - 64 * a, x:x + 1]).then_inc(s_swap, 16)
                sp.wait_ge(s_swap, 128)
                sp.wait_ge(s_w, 16 * 7)

            @block.scalar
            def _(act):
                act.wait_ge(s_dve, marks["shifted"])
                nc.scalar.activation(lg[:, :, :, :], lg[:, :, :, :], ACT.Exp).then_inc(s_exp, 1)
                act.sem_inc(h_silu, ETILES)
                act.sem_inc(h_gated, ETILES)
                with act.Fori(0, AHEAD) as c:
                    for t in range(ETILES):
                        b = t % 2
                        h_wait(act, h_up, c, t + 1)
                        h_wait(act, h_mul, c, t - 1)
                        nc.scalar.activation(silu[:, b, :], up_ps[:, b, :], ACT.Silu, bias=b_up[:, t:t + 1]).then_inc(h_silu, 1)
                        h_wait(act, h_gate, c, t + 1)
                        nc.scalar.activation(gate[:, b, :], gate_ps[:, b, :], ACT.Identity, bias=b_gate[:, t:t + 1]
                                             ).then_inc(h_gated, 1)

            @block.gpsimd
            def _(pool):
                pool.sem_inc(h_mul, ETILES)
                with pool.Fori(0, AHEAD) as c:
                    for t in range(ETILES):
                        b = t % 2
                        h_wait(pool, h_silu, c, t + 1)
                        h_wait(pool, h_gated, c, t + 1)
                        nc.gpsimd.tensor_tensor(ahead[:, t, ds(c * CH, CH)], silu[:, b, :], gate[:, b, :], ALU.mult
                                                ).then_inc(h_mul, 1)

            @block.tensor
            def _(pe):
                pe.wait_ge(s_in, 16 * 6)
                for t in range(TILES):
                    last = nc.tensor.matmul(lg_ps[:, t // 8, t % 8, :], xT[:, 1 + t * P:1 + (t + 1) * P], w_r[:, :],
                                            start=True, stop=True)
                last.then_inc(s_lg, 1)
                pe.wait_ge(s_dve, marks["scores"])
                for t in range(8):
                    last = nc.tensor.transpose(sc_ps[:, t * P:(t + 1) * P], lg[:, t, :, :].rearrange("p a e -> p (a e)"), ident[:, :])
                last.then_inc(s_scT, 1)
                for semaphore in (h_up, h_gate):
                    pe.sem_inc(semaphore, ETILES)
                pe.wait_ge(s_w, 16 * 7)
                pe.sem_inc(h_checkpoint, 1)
                with pe.Fori(0, AHEAD) as c:
                    x_c = xT[:, ds(c * CH + 1, CH)]
                    for t in range(ETILES):
                        b = t % 2
                        h_wait(pe, h_silu, c, t - 1)
                        nc.tensor.matmul(up_ps[:, b, :], w_up[:, t, :], x_c, start=True, stop=True).then_inc(h_up, 1)
                        h_wait(pe, h_gated, c, t - 1)
                        nc.tensor.matmul(gate_ps[:, b, :], w_gate[:, t, :], x_c, start=True, stop=True).then_inc(h_gate, 1)
                pe.wait_ge(s_dve, marks["gsum"])
                nc.tensor.transpose(t_ps[0:GPH, 0:P], gsum[:, :], ident[:, :]).then_inc(s_gT, 1)
                pe.wait_ge(s_gr, 32)
                nc.tensor.transpose(n_ps[:, 0:TILES], grow[:, :], ident[0:TILES, 0:TILES]).then_inc(s_rowT, 1)
                pe.wait_ge(s_dve, marks["fs"])
                for k in range(2):
                    last = nc.tensor.matmul(dn_ps[:, k * CH:(k + 1) * CH], pairs[:, :], fs[:, k * CH:(k + 1) * CH],
                                            start=True, stop=True)
                last.then_inc(s_sum, 1)

        ctx = ExitStack()
        with ctx:
            def sb(name, shape, dt=F32):
                return ctx.enter_context(nc.sbuf_tensor("d1_" + name, shape, dt))
            silu = sb("silu", [P, 2, CH])
            ug = sb("ug", [P, 2, CH])
            hid = sb("hid", [P, 2, CH])
            up_ps = [ctx.enter_context(nc.psum_tensor(f"d1_up{i}", [P, CH], F32)) for i in range(2)]
            gt_ps = [ctx.enter_context(nc.psum_tensor(f"d1_gate{i}", [P, CH], F32)) for i in range(2)]
            fs_ps = [ctx.enter_context(nc.psum_tensor(f"d1_fs{i}", [P, CH], F32)) for i in range(2)]
            o_ps = [ctx.enter_context(nc.psum_tensor(f"d1_o{i}", [P, CH], F32)) for i in range(1)]

            class Count:
                def __init__(self, name, per):
                    self.sem, self.per = ctx.enter_context(nc.semaphore("d1_" + name)), per

            s_gate = ctx.enter_context(nc.semaphore("d1_checkpoint"))
            C = {n: Count(n, per) for n, per in dict(up=ETILES, gate=ETILES, fs=ETILES, silu=ETILES, ug=ETILES, hid=ETILES,
                                                     out=1, cp=1, dn=ETILES).items()}
            block = ctx.enter_context(nc.Block())

            def wait(eng, name, c, k):
                eng.wait_ge(C[name].sem, c * C[name].per + (C[name].per + k))

            def chunks(eng, body):
                with eng.Fori(0, AHEAD) as c:
                    body(c, True)
                body(AHEAD, False)

            @block.scalar
            def _(act):
                act.sem_inc(C["silu"].sem, ETILES)
                for t in range(ETILES):
                    wait(act, "up", 0, t + 1)
                    wait(act, "ug", 0, t - 1)
                    nc.scalar.activation(silu[:, t % 2, :], up_ps[t % 2][:, :], ACT.Silu, bias=b_up[:, t:t + 1]
                                         ).then_inc(C["silu"].sem, 1)

            @block.vector
            def _(dve):
                for n in ("ug", "hid", "cp"):
                    dve.sem_inc(C[n].sem, C[n].per)

                def body(c, made):
                    for t in range(ETILES):
                        if not made:
                            wait(dve, "gate", 0, t + 1)
                            wait(dve, "silu", 0, t + 1)
                            nc.vector.scalar_tensor_tensor(ug[:, t % 2, :], gt_ps[t % 2][:, :], b_gate[:, t:t + 1],
                                                           silu[:, t % 2, :], ALU.add, ALU.mult).then_inc(C["ug"].sem, 1)
                            wait(dve, "ug", 0, t + 1)
                        wait(dve, "fs", c, t + 1)
                        wait(dve, "dn", c, t - 1)
                        nc.vector.tensor_tensor(hid[:, t % 2, :], ahead[:, t, ds(c * CH, CH)] if made else ug[:, t % 2, :],
                                                fs_ps[t % 2][:, :], ALU.mult).then_inc(C["hid"].sem, 1)
                    wait(dve, "out", c, 1)
                    nc.vector.tensor_copy(moe[:, ds(c * CH, CH)], o_ps[0][:, :]).then_inc(C["cp"].sem, 1)
                chunks(dve, body)

            @block.tensor
            def _(pe):
                for n in ("up", "gate", "fs", "out", "dn"):
                    pe.sem_inc(C[n].sem, C[n].per)

                def down(c, t):
                    wait(pe, "hid", c, t + 1)
                    nc.tensor.matmul(o_ps[0][:, :], w_down[:, t, :], hid[:, t % 2, :], start=False, stop=t == ETILES - 1
                                     ).then_inc(C["dn"].sem, 1)

                def body(c, made):
                    x_c = xT[:, ds(c * CH + 1, CH)]
                    f_c = fsn[:, ds(c * CH, CH)]
                    wait(pe, "cp", c, 0)
                    pe.sem_inc(s_gate, 1)
                    nc.tensor.matmul(o_ps[0][:, :], b_down[:, :], f_c, start=True, stop=False)
                    for t in range(ETILES):
                        if not made:
                            wait(pe, "silu", 0, t - 1)
                            nc.tensor.matmul(up_ps[t % 2][:, :], w_up[:, t, :], x_c, start=True, stop=True
                                             ).then_inc(C["up"].sem, 1)
                            wait(pe, "ug", 0, t - 1)
                            nc.tensor.matmul(gt_ps[t % 2][:, :], w_gate[:, t, :], x_c, start=True, stop=True
                                             ).then_inc(C["gate"].sem, 1)
                        wait(pe, "hid", c, t - 1)
                        pe.sem_inc(s_gate, 1)
                        nc.tensor.matmul(fs_ps[t % 2][:, :], spread[:, t, :], f_c, start=True, stop=True
                                         ).then_inc(C["fs"].sem, 1)
                        if t:
                            down(c, t - 1)
                    down(c, ETILES - 1)
                    pe.sem_inc(s_gate, 1)
                    wait(pe, "dn", c, ETILES)
                    pe.sem_inc(C["out"].sem, 1)
                chunks(pe, body)


def store(nc, xT, out, const):
    with ExitStack() as ctx:
        ident = ctx.enter_context(nc.sbuf_tensor("e_ident", [P, P], F32))
        tok = ctx.enter_context(nc.sbuf_tensor("e_tok", [P, TILES, DIM], F32))
        ps = [ctx.enter_context(nc.psum_tensor(f"e_ps{c}", [P, 4, DIM], F32)) for c in range(CHUNKS)]
        s_id, s_tr, s_tok, s_out = (ctx.enter_context(nc.semaphore("e_" + n)) for n in ("ident", "turned", "tok", "out"))
        block = ctx.enter_context(nc.Block())

        @block.sync
        def _(sp):
            sp.dma_start(ident[:, :], const["ident"]).then_inc(s_id, 16)
            for c in range(CHUNKS):
                sp.wait_ge(s_tok, c + 1)
                sp.dma_start(out[c * CH:(c + 1) * CH, :].rearrange("(t p) d -> p t d", p=P), tok[:, 4 * c:4 * c + 4, :]
                             ).then_inc(s_out, 16)
            sp.wait_ge(s_out, 16 * CHUNKS)

        @block.tensor
        def _(pe):
            pe.wait_ge(s_id, 16)
            for c in range(CHUNKS):
                for k in range(4):
                    t = 4 * c + k
                    last = nc.tensor.transpose(ps[c][:, k, :], xT[:, 1 + t * P:1 + (t + 1) * P], ident[:, :])
                last.then_inc(s_tr, 1)

        @block.vector
        def _(dve):
            for c in range(CHUNKS):
                dve.wait_ge(s_tr, c + 1)
                nc.vector.tensor_copy(tok[:, 4 * c:4 * c + 4, :], ps[c][:, :, :]).then_inc(s_tok, 1)


def program(nc, aps, const, out):
    part = lambda prefix: {n[len(prefix):]: ap for n, ap in aps.items() if n.startswith(prefix)}
    with nc.sbuf_tensor("xT", [DIM, 1 + SEQ], F32) as xT:
        with nc.sbuf_tensor("attended", [DIM, SEQ], F32) as attended:
            nc.disable_value_cache = True
            causal_attention(nc, xT, attended, part("L0_attn_"), const)
            nc.disable_value_cache = False
            residual_layernorm(nc, "ln0", xT, attended, xT)
        with nc.sbuf_tensor("x_layers", [DIM, 1 + SEQ], F32) as x_layers:
            local_layers(nc, xT, x_layers, part("L0_ffn_"), const)
            residual_layernorm(nc, "ln1", xT, x_layers, xT, first=1)
        with nc.sbuf_tensor("scanned", [DIM, SEQ], F32) as scanned:
            selective_scan(nc, xT, scanned, part("L1_attn_"))
            residual_layernorm(nc, "ln2", xT, scanned, xT)
        with nc.sbuf_tensor("expert_sum", [DIM, SEQ], F32) as expert_sum:
            routed_experts(nc, xT, expert_sum, part("L1_ffn_"), const)
            residual_layernorm(nc, "ln3", xT, expert_sum, xT)
        store(nc, xT, out, const)


def shape_constants():
    f = np.float32
    p = np.arange(P)
    c = {"ident": np.eye(P, dtype=f)}
    sel, denb = np.zeros((P, 4, P), f), np.zeros((P, P), f)
    for g in range(4):
        for j in range(4):
            for d in range(8):
                sel[8 * (4 * g + j) + d, g, 32 * j + d] = 1
            denb[32 * j + 8, 32 * j:32 * j + 32] = 1
    c["sel"], c["denb"] = sel, denb
    later = np.where(p[None, :] > p[:, None], -BIG, 0.0).astype(f)
    c["tri"] = np.stack([later, later.T], 1)
    key, query = np.arange(64), p % 32
    seen = (key[None, :] >= query[:, None]) & (key[None, :] <= query[:, None] + 32)
    masks = np.repeat(np.where(seen, 0.0, -BIG).astype(f)[:, None, :], TILES, 1)
    masks[0:32, 0, 0:32] = -BIG
    c["masks"] = masks
    half = np.arange(0, 64, 2, dtype=f)
    inv_freq = (f(1.0) / f(10000.0) ** (half / f(64))).astype(f)
    t = np.arange(SEQ, dtype=f)
    freqs = np.concatenate([t[:, None] * inv_freq[None, :]] * 2, -1).astype(f)
    base = ((half + f(0.4 * 64)) / f(1.4 * 64)).astype(f)
    power = ((t - SEQ // 2) / 16).astype(f)
    scale = np.concatenate([base[None, :] ** power[:, None]] * 2, -1).astype(f)
    sign = np.concatenate([-np.ones(32, f), np.ones(32, f)])
    cos, sin = np.cos(freqs), np.sin(freqs) * sign
    rot = np.stack([cos * scale, sin * scale, cos * (f(1) / scale), sin * (f(1) / scale)]).astype(f)
    c["rot"] = rot.reshape(4, TILES, P, 64).transpose(2, 0, 1, 3)
    c["pairs"] = (p[:, None] // 64 == p[None, :] // 64).astype(f)
    c["tril"] = np.stack([p[None, :] < p[:, None], p[None, :] >= p[:, None]], 1).astype(f)
    c["gidx"] = (1 + 16 * (p // 64)[:, None] + np.arange(16)[None, :]).astype(f)
    spread = np.zeros((64, 16, P), f)
    for e in range(64):
        spread[e, e // 4, 32 * (e % 4):32 * (e % 4) + 32] = 1
    c["spread"] = spread
    return {n: np.ascontiguousarray(a) for n, a in c.items()}


def kernel(**inputs):
    import concourse.bacc as bacc
    from concourse.bass_utils import run_bass_kernel_spmd

    nc = bacc.Bacc("TRN2", target_bir_lowering=False, num_devices=1)
    arrays, aps, const = {}, {}, {}
    for name, value in inputs.items():
        a = np.ascontiguousarray(value)
        arrays["in_" + name] = a
        aps[name] = nc.dram_tensor("in_" + name, a.shape, mybir.dt.from_np(a.dtype), kind="ExternalInput").ap()
    for name, a in shape_constants().items():
        arrays["const_" + name] = a
        const[name] = nc.dram_tensor("const_" + name, a.shape, mybir.dt.from_np(a.dtype), kind="ExternalInput").ap()
    out = nc.dram_tensor("out", [SEQ, DIM], F32, kind="ExternalOutput").ap()
    program(nc, aps, const, out)
    r = run_bass_kernel_spmd(nc, [arrays], core_ids=[0])
    return r.results[0]["out"].reshape(1, SEQ, DIM)
```
